# Optimizing a Trainium2 kernel written in Bass

```python
import numpy as np
import jax
import jax.numpy as jnp

def _softmax(x, axis=-1):
    return jax.nn.softmax(x, axis=axis)

def _gelu(x):
    return jax.nn.gelu(x, approximate=True)

def _silu(x):
    return jax.nn.silu(x)

def _sigmoid(x):
    return jax.nn.sigmoid(x)

def _layernorm(x, axis=-1, eps=1e-05):
    m = jnp.mean(x, axis=axis, keepdims=True)
    v = jnp.var(x, axis=axis, keepdims=True)
    return (x - m) / jnp.sqrt(v + eps)

def _scatter_add(tgt, idx, src, axis=0):
    return tgt.at[idx].add(src)

def _segment_sum(src, seg, n):
    return jax.ops.segment_sum(src, seg, n)
kernel_name = 'mk_gnn_resnorm_d4_gnn_r32_e0f9ce'

def setup_inputs(seed: int=0):
    np.random.seed(seed)
    _w = jnp.asarray

    def _rec_inputs():
        import jax
        import jax.numpy as jnp
        _gk = jax.random.key(seed)
        x = -0.0003713 + 1 * jax.random.normal(jax.random.fold_in(_gk, 1), (3125, 128), jnp.float32)
        _s = jax.random.randint(jax.random.fold_in(_gk, 2), (25000,), 0, 3125, jnp.int32)
        _d = jax.random.randint(jax.random.fold_in(_gk, 3), (25000,), 0, 3125, jnp.int32)
        _loop = jnp.arange(3125, dtype=jnp.int32)
        src = jnp.concatenate([_s, _d, _loop])
        dst = jnp.concatenate([_d, _s, _loop])
        _o = jnp.argsort(dst, stable=True)
        src = src[_o]
        dst = dst[_o]
        edge_weight = jax.random.uniform(jax.random.fold_in(_gk, 13), (53125,), jnp.float32, 0.0, 1)
        return (x, src, dst, edge_weight)
    x, src, dst, edge_weight = _rec_inputs()

    def _L0_gnn_setup():
        import jax, jax.numpy as jnp
        import numpy as np
        N = 3125
        E = 50000
        D_IN = 128
        D_OUT = 128
        key = jax.random.key(seed)
        k1, k2, k3, k4, k5, k6 = jax.random.split(key, 6)
        x = jax.random.normal(k1, (N, D_IN), dtype=jnp.float32)
        W = jax.random.normal(k2, (D_IN, D_OUT), dtype=jnp.float32) * (1.0 / np.sqrt(D_IN))
        b = jax.random.normal(k3, (D_OUT,), dtype=jnp.float32) * 0.01
        row = jax.random.randint(k4, (E,), 0, N, dtype=jnp.int32)
        col = jax.random.randint(k5, (E,), 0, N, dtype=jnp.int32)
        vals = jax.random.uniform(k6, (E,), dtype=jnp.float32)
        return {'x': x, 'W': W, 'b': b, 'row': row, 'col': col, 'vals': vals}
    _L0_gnn_all = _L0_gnn_setup()
    _L0_gnn_in = {k: v for k, v in _L0_gnn_all.items() if k in ('W', 'b')}
    del _L0_gnn_all

    def _L1_gnn_setup():
        import jax, jax.numpy as jnp
        import numpy as np
        N = 3125
        E = 50000
        D = 128
        H = 8
        DH = D // H
        EPS = 1e-05

        def layer_norm(x, g, b):
            mu = jnp.mean(x, axis=-1, keepdims=True)
            var = jnp.var(x, axis=-1, keepdims=True)
            return (x - mu) * jax.lax.rsqrt(var + EPS) * g + b
        key = jax.random.key(seed)
        ks = jax.random.split(key, 16)
        s = 1.0 / np.sqrt(D)
        inp = {'h': jax.random.normal(ks[0], (N, D), jnp.float32), 'src': jax.random.randint(ks[1], (E,), 0, N, jnp.int32), 'dst': jax.random.randint(ks[2], (E,), 0, N, jnp.int32), 'Wq': jax.random.uniform(ks[3], (D, D), jnp.float32, -s, s), 'Wk': jax.random.uniform(ks[4], (D, D), jnp.float32, -s, s), 'Wv': jax.random.uniform(ks[5], (D, D), jnp.float32, -s, s), 'Wo': jax.random.uniform(ks[6], (D, D), jnp.float32, -s, s), 'bo': jnp.zeros((D,), jnp.float32), 'g1': jnp.ones((D,), jnp.float32), 'b1': jnp.zeros((D,), jnp.float32), 'g2': jnp.ones((D,), jnp.float32), 'b2': jnp.zeros((D,), jnp.float32), 'W1': jax.random.uniform(ks[7], (D, 2 * D), jnp.float32, -s, s), 'c1': jnp.zeros((2 * D,), jnp.float32), 'W2': jax.random.uniform(ks[8], (2 * D, D), jnp.float32, -1.0 / np.sqrt(2 * D), 1.0 / np.sqrt(2 * D)), 'c2': jnp.zeros((D,), jnp.float32)}
        return inp
    _L1_gnn_all = _L1_gnn_setup()
    _L1_gnn_in = {k: v for k, v in _L1_gnn_all.items() if k in ('Wq', 'Wk', 'Wv', 'Wo', 'bo', 'g1', 'b1', 'g2', 'b2', 'W1', 'c1', 'W2', 'c2')}
    del _L1_gnn_all

    def _L2_gnn_setup():
        import jax, jax.numpy as jnp
        import numpy as np
        N = 50000
        E = 25000
        HEADS = 2
        HID = 64
        L = 2
        NEG_SLOPE = 0.2
        PAIRNORM_EPS = 1e-05
        SOFTMAX_EPS = 1e-16

        def _gatv2_layer(x, src, dst, Wl, Wr, att, bias):
            n = x.shape[0]
            xs = (x @ Wl).reshape(n, HEADS, HID)
            xd = (x @ Wr).reshape(n, HEADS, HID)
            e = jax.nn.leaky_relu(xs[src] + xd[dst], NEG_SLOPE)
            logits = jnp.einsum('ehc,hc->eh', e, att)
            m = jax.ops.segment_max(logits, dst, num_segments=n)
            alpha = jnp.exp(logits - m[dst])
            denom = jax.ops.segment_sum(alpha, dst, num_segments=n)
            alpha = alpha / (denom[dst] + SOFTMAX_EPS)
            msg = alpha[:, :, None] * xs[src]
            out = jax.ops.segment_sum(msg, dst, num_segments=n)
            return out.reshape(n, HEADS * HID) + bias

        def _pairnorm(x):
            x = x - jnp.mean(x, axis=0, keepdims=True)
            scale = jnp.sqrt(PAIRNORM_EPS + jnp.mean(jnp.sum(x * x, axis=-1)))
            return x / scale
        key = jax.random.key(seed)
        ks = jax.random.split(key, 6)
        x = jax.random.normal(ks[0], (N, 128), dtype=jnp.float32)
        edge_index = jax.random.randint(ks[1], (2, E), 0, N, dtype=jnp.int64)
        Wl = jax.random.normal(ks[2], (L, 128, HEADS * HID), dtype=jnp.float32) * 0.08
        Wr = jax.random.normal(ks[3], (L, 128, HEADS * HID), dtype=jnp.float32) * 0.08
        att = jax.random.normal(ks[4], (L, HEADS, HID), dtype=jnp.float32) * 0.08
        bias = jax.random.normal(ks[5], (L, HEADS * HID), dtype=jnp.float32) * 0.02
        return {'x': x, 'edge_index': edge_index, 'Wl': Wl, 'Wr': Wr, 'att': att, 'bias': bias}
    _L2_gnn_all = _L2_gnn_setup()
    _L2_gnn_in = {k: v for k, v in _L2_gnn_all.items() if k in ('Wl', 'Wr', 'att', 'bias')}
    del _L2_gnn_all

    def _L3_gnn_setup():
        import math
        import jax, jax.numpy as jnp
        import numpy as np
        N = 50000
        E = 25000
        HID = 128
        H = 8
        D = HID // H
        key = jax.random.key(seed)
        ks = jax.random.split(key, 12)
        s = 1.0 / math.sqrt(HID)
        inp = {'h': jax.random.normal(ks[0], (N, HID), dtype=jnp.float32), 'src': jax.random.randint(ks[1], (E,), 0, N, dtype=jnp.int32), 'dst': jax.random.randint(ks[2], (E,), 0, N, dtype=jnp.int32), 'Wq': jax.random.normal(ks[3], (HID, HID), dtype=jnp.float32) * s, 'bq': jax.random.normal(ks[4], (HID,), dtype=jnp.float32) * s, 'Wk': jax.random.normal(ks[5], (HID, HID), dtype=jnp.float32) * s, 'bk': jax.random.normal(ks[6], (HID,), dtype=jnp.float32) * s, 'Wv': jax.random.normal(ks[7], (HID, HID), dtype=jnp.float32) * s, 'bv': jax.random.normal(ks[8], (HID,), dtype=jnp.float32) * s, 'Wo': jax.random.normal(ks[9], (HID, HID), dtype=jnp.float32) * s, 'bo': jax.random.normal(ks[10], (HID,), dtype=jnp.float32) * s}
        return inp
    _L3_gnn_all = _L3_gnn_setup()
    _L3_gnn_in = {k: v for k, v in _L3_gnn_all.items() if k in ('Wq', 'bq', 'Wk', 'bk', 'Wv', 'bv', 'Wo', 'bo')}
    del _L3_gnn_all
    return {'x': x, 'src': src, 'dst': dst, 'edge_weight': edge_weight, 'L0_gnn_W': _L0_gnn_in['W'], 'L0_gnn_b': _L0_gnn_in['b'], 'L1_gnn_Wq': _L1_gnn_in['Wq'], 'L1_gnn_Wk': _L1_gnn_in['Wk'], 'L1_gnn_Wv': _L1_gnn_in['Wv'], 'L1_gnn_Wo': _L1_gnn_in['Wo'], 'L1_gnn_bo': _L1_gnn_in['bo'], 'L1_gnn_g1': _L1_gnn_in['g1'], 'L1_gnn_b1': _L1_gnn_in['b1'], 'L1_gnn_g2': _L1_gnn_in['g2'], 'L1_gnn_b2': _L1_gnn_in['b2'], 'L1_gnn_W1': _L1_gnn_in['W1'], 'L1_gnn_c1': _L1_gnn_in['c1'], 'L1_gnn_W2': _L1_gnn_in['W2'], 'L1_gnn_c2': _L1_gnn_in['c2'], 'L2_gnn_Wl': _L2_gnn_in['Wl'], 'L2_gnn_Wr': _L2_gnn_in['Wr'], 'L2_gnn_att': _L2_gnn_in['att'], 'L2_gnn_bias': _L2_gnn_in['bias'], 'L3_gnn_Wq': _L3_gnn_in['Wq'], 'L3_gnn_bq': _L3_gnn_in['bq'], 'L3_gnn_Wk': _L3_gnn_in['Wk'], 'L3_gnn_bk': _L3_gnn_in['bk'], 'L3_gnn_Wv': _L3_gnn_in['Wv'], 'L3_gnn_bv': _L3_gnn_in['bv'], 'L3_gnn_Wo': _L3_gnn_in['Wo'], 'L3_gnn_bo': _L3_gnn_in['bo']}

def reference(x, src, dst, edge_weight, L0_gnn_W, L0_gnn_b, L1_gnn_Wq, L1_gnn_Wk, L1_gnn_Wv, L1_gnn_Wo, L1_gnn_bo, L1_gnn_g1, L1_gnn_b1, L1_gnn_g2, L1_gnn_b2, L1_gnn_W1, L1_gnn_c1, L1_gnn_W2, L1_gnn_c2, L2_gnn_Wl, L2_gnn_Wr, L2_gnn_att, L2_gnn_bias, L3_gnn_Wq, L3_gnn_bq, L3_gnn_Wk, L3_gnn_bk, L3_gnn_Wv, L3_gnn_bv, L3_gnn_Wo, L3_gnn_bo):
    import jax
    import jax.numpy as jnp

    def _L0_gnn_ref(x, W, b, row, col, vals):
        import jax, jax.numpy as jnp
        import numpy as np
        N = 3125
        E = 50000
        D_IN = 128
        D_OUT = 128
        support = x @ W
        msgs = support[col] * vals[:, None]
        out = jax.ops.segment_sum(msgs, row, num_segments=N)
        return out + b

    def _L1_gnn_ref(h, src, dst, Wq, Wk, Wv, Wo, bo, g1, b1, g2, b2, W1, c1, W2, c2):
        import jax, jax.numpy as jnp
        import numpy as np
        N = 3125
        E = 50000
        D = 128
        H = 8
        DH = D // H
        EPS = 1e-05

        def layer_norm(x, g, b):
            mu = jnp.mean(x, axis=-1, keepdims=True)
            var = jnp.var(x, axis=-1, keepdims=True)
            return (x - mu) * jax.lax.rsqrt(var + EPS) * g + b
        n = h.shape[0]
        Q = (h @ Wq).reshape(n, H, DH)
        K = (h @ Wk).reshape(n, H, DH)
        V = (h @ Wv).reshape(n, H, DH)
        score = jnp.einsum('ehd,ehd->eh', K[src], Q[dst])
        score = jnp.exp(jnp.clip(score / np.sqrt(DH), -5.0, 5.0))
        wV = jax.ops.segment_sum(V[src] * score[:, :, None], dst, num_segments=n)
        z = jax.ops.segment_sum(score, dst, num_segments=n)
        zb = z[:, :, None]
        head_out = jnp.where(zb > 0, wV / jnp.where(zb > 0, zb, 1.0), wV)
        a = head_out.reshape(n, D) @ Wo + bo
        hh = layer_norm(h + a, g1, b1)
        ff = jax.nn.relu(hh @ W1 + c1) @ W2 + c2
        return layer_norm(hh + ff, g2, b2)

    def _L2_gnn_ref(x, edge_index, Wl, Wr, att, bias):
        import jax, jax.numpy as jnp
        import numpy as np
        N = 50000
        E = 25000
        HEADS = 2
        HID = 64
        L = 2
        NEG_SLOPE = 0.2
        PAIRNORM_EPS = 1e-05
        SOFTMAX_EPS = 1e-16

        def _gatv2_layer(x, src, dst, Wl, Wr, att, bias):
            n = x.shape[0]
            xs = (x @ Wl).reshape(n, HEADS, HID)
            xd = (x @ Wr).reshape(n, HEADS, HID)
            e = jax.nn.leaky_relu(xs[src] + xd[dst], NEG_SLOPE)
            logits = jnp.einsum('ehc,hc->eh', e, att)
            m = jax.ops.segment_max(logits, dst, num_segments=n)
            alpha = jnp.exp(logits - m[dst])
            denom = jax.ops.segment_sum(alpha, dst, num_segments=n)
            alpha = alpha / (denom[dst] + SOFTMAX_EPS)
            msg = alpha[:, :, None] * xs[src]
            out = jax.ops.segment_sum(msg, dst, num_segments=n)
            return out.reshape(n, HEADS * HID) + bias

        def _pairnorm(x):
            x = x - jnp.mean(x, axis=0, keepdims=True)
            scale = jnp.sqrt(PAIRNORM_EPS + jnp.mean(jnp.sum(x * x, axis=-1)))
            return x / scale
        n = x.shape[0]
        loop = jnp.arange(n, dtype=edge_index.dtype)
        src = jnp.concatenate([edge_index[0], loop])
        dst = jnp.concatenate([edge_index[1], loop])
        for i in range(L):
            x = _gatv2_layer(x, src, dst, Wl[i], Wr[i], att[i], bias[i])
            x = _pairnorm(x)
            x = jax.nn.relu(x)
        return x

    def _L3_gnn_ref(h, src, dst, Wq, bq, Wk, bk, Wv, bv, Wo, bo):
        import math
        import jax, jax.numpy as jnp
        import numpy as np
        N = 50000
        E = 25000
        HID = 128
        H = 8
        D = HID // H
        n = h.shape[0]
        q = (h @ Wq.T + bq).reshape(n, H, D)
        k = (h @ Wk.T + bk).reshape(n, H, D)
        v = (h @ Wv.T + bv).reshape(n, H, D)
        eq = q[dst]
        ek = k[src]
        ev = v[src]
        scores = jnp.einsum('ehd,ehd->eh', eq, ek) / jnp.sqrt(jnp.asarray(D, h.dtype))
        scores = jnp.clip(scores, -5.0, 5.0)
        m = jax.ops.segment_max(scores, dst, num_segments=n)
        ex = jnp.exp(scores - m[dst])
        z = jax.ops.segment_sum(ex, dst, num_segments=n)
        attn = ex / z[dst]
        out = jax.ops.segment_sum(attn[..., None] * ev, dst, num_segments=n)
        out = out.reshape(n, H * D)
        return out @ Wo.T + bo
    edge_index = jnp.stack([src, dst])
    x = _layernorm(x + _L0_gnn_ref(x, L0_gnn_W, L0_gnn_b, src, dst, edge_weight), axis=-1)
    x = _layernorm(x + _L1_gnn_ref(x, src, dst, L1_gnn_Wq, L1_gnn_Wk, L1_gnn_Wv, L1_gnn_Wo, L1_gnn_bo, L1_gnn_g1, L1_gnn_b1, L1_gnn_g2, L1_gnn_b2, L1_gnn_W1, L1_gnn_c1, L1_gnn_W2, L1_gnn_c2), axis=-1)
    x = _layernorm(x + _L2_gnn_ref(x, edge_index, L2_gnn_Wl, L2_gnn_Wr, L2_gnn_att, L2_gnn_bias), axis=-1)
    x = _layernorm(x + _L3_gnn_ref(x, src, dst, L3_gnn_Wq, L3_gnn_bq, L3_gnn_Wk, L3_gnn_bk, L3_gnn_Wv, L3_gnn_bv, L3_gnn_Wo, L3_gnn_bo), axis=-1)
    return x

_drawn_inputs = setup_inputs


def setup_inputs(seed=0):
    import zlib

    import numpy as np

    out = dict(_drawn_inputs(seed))
    spreads = {'L1_gnn_bo': (0.0, 0.1),
     'L1_gnn_g1': (1.0, 0.2),
     'L1_gnn_b1': (0.0, 0.1),
     'L1_gnn_g2': (1.0, 0.2),
     'L1_gnn_b2': (0.0, 0.1),
     'L1_gnn_c1': (0.0, 0.359),
     'L1_gnn_c2': (0.0, 0.1)}
    factors = {'L0_gnn_b': 8.0,
     'L1_gnn_Wq': 3.795,
     'L1_gnn_Wk': 3.714,
     'L2_gnn_Wr': 8.0,
     'L2_gnn_att': 3.706,
     'L2_gnn_bias': 64.0,
     'L3_gnn_bk': 64.0}
    for name, (base, spread) in spreads.items():
        noise = np.random.default_rng([zlib.crc32(name.encode()), seed]).standard_normal(out[name].shape)
        drawn = base * np.exp(spread * noise) if base else spread * noise
        out[name] = jnp.asarray(drawn.astype(out[name].dtype))
    for name, factor in factors.items():
        out[name] = (out[name] * factor).astype(out[name].dtype)
    return out
```

```python
import concourse.bass as bass
from concourse import mybir
from contextlib import ExitStack
from collections import namedtuple

F32 = mybir.dt.float32
I32 = mybir.dt.int32
ALU = mybir.AluOpType
ACT = mybir.ActivationFunctionType
AX = mybir.AxisListType

P = 128
N = 3125
E = 53125
D = 128
TILES = -(-E // P)
G = 4
NG = TILES // G
SLOTS = 4
TURNS = NG // SLOTS
EPAD = TILES * P
ROWS = 104
QUARTERS = TILES // ROWS
NB = -(-N // P) + 1
NPAD = NB * P
FULLB = N // P
TAILR = N - FULLB * P
CHUNKS = [(b, min(4, NB - b)) for b in range(0, NB, 4)]
HEADS = 8
DH = D // HEADS
GHEADS = 2
GC = D // GHEADS
BIG = 1e30
LN_EPS = 1e-5
FAR = 1 << 20
HI = -(-N // P)
SENT = D + 4


def gnn_program(nc, a, out):
    ctx = ExitStack()
    with ctx:
        def sb(name, shape, dt=F32):
            return ctx.enter_context(nc.sbuf_tensor(name, shape, dt))

        def ps(name, shape):
            return ctx.enter_context(nc.psum_tensor(name, shape, F32))

        def sem(name):
            return ctx.enter_context(nc.semaphore(name))

        def sems(prefix, names):
            return SimpleNamespace(**{n: sem(f"{prefix}_{n}") for n in names.split()})

        def slot_sems(name):
            return [sem(f"{name}{s}") for s in range(SLOTS)]

        def dram(name, shape):
            return nc.dram_tensor(name, shape, F32, kind="Internal").ap()

        kv_table = [dram(f"kv_table{i}", (NPAD, 2 * D)) for i in range(2)]
        q_table = [dram(f"q_table{i}", (NPAD, D)) for i in range(2)]
        xs_table = [dram(f"xs_table{i}", (NPAD, D)) for i in range(2)]
        xd_table = [dram(f"xd_table{i}", (NPAD, D)) for i in range(2)]
        x_table = dram("x_table", (NPAD, D))
        sorted_msgs = dram("sorted_msgs", (EPAD, SENT))
        edge_rows = [dram(f"edge_rows{i}", (NG, P, G * D)) for i in range(2)]

        rowspace = sb("rowspace", [P, 3 * GHEADS * QUARTERS * P])
        rows_f = rowspace[0:ROWS, 0:5 * QUARTERS * P].rearrange("r (n q p) -> r n q p", n=5, q=QUARTERS)
        src_idx = sb("src_idx", [P, TILES], I32)
        dst_rel = sb("dst_rel", [P, TILES])
        weight = sb("weight", [P, TILES])
        src_f = sb("src_f", [P, TILES])
        softbuf = sb("softbuf", [P, 2 * TILES * GHEADS])
        src_low = softbuf[:, 0:TILES]
        src_high = softbuf[:, TILES:2 * TILES]
        first_src_bc = softbuf[:, 2 * TILES:3 * TILES]
        part_i = softbuf[:, 3 * TILES:4 * TILES].bitcast(I32)
        first_src = sb("first_src", [1, TILES], I32)
        first_src_f = sb("first_src_f", [1, TILES])
        copies = sb("copies", [P, TILES])
        first_i = sb("first_i", [1, TILES], I32)
        first_dst = sb("first_dst", [1, TILES], I32)
        first_f = sb("first_f", [1, TILES])
        endbuf = sb("endbuf", [2, 4 * TILES])
        ends_i = endbuf[:, :].bitcast(I32).rearrange("h (n t) -> h n t", n=4)
        ends_f = sb("ends_f", [2, 4, TILES])
        scan_fwd = sb("scan_fwd", [ROWS, QUARTERS, GHEADS, P])
        scan_bwd = sb("scan_bwd", [ROWS, QUARTERS, GHEADS, P])
        open_fwd = sb("open_fwd", [ROWS, QUARTERS, P])
        open_bwd = sb("open_bwd", [ROWS, QUARTERS, P])
        pass_fwd = sb("pass_fwd", [2, TILES])
        pass_bwd = sb("pass_bwd", [2, TILES])

        ident = sb("ident", [P, P])
        iota = sb("iota", [P, P])
        iota_i = sb("iota_i", [P, P], I32)
        ones = sb("ones", [P, P])
        sel8 = sb("sel8", [P, HEADS])
        sel2 = sb("sel2", [P, GHEADS])
        eps = sb("eps", [P, 1])
        earlier = sb("earlier", [P, P])
        later = sb("later", [P, P])

        W0 = sb("W0", [P, D])
        Wkvq = [sb(f"Wkvq{i}", [P, 3 * D]) for i in range(2)]
        Wo = [sb(f"Wo{i}", [P, D]) for i in range(2)]
        W1 = sb("W1", [P, 2 * D])
        W2 = sb("W2", [P, 2, D])
        Wsd = [sb(f"Wsd{i}", [P, 2 * D]) for i in range(2)]
        att = [sb(f"att{i}", [P, D]) for i in range(2)]
        row_b0 = sb("row_b0", [1, D])
        row_bo = [sb(f"row_bo{i}", [1, D]) for i in range(2)]
        row_c2 = sb("row_c2", [1, D])
        row_kvq = sb("row_kvq", [1, 3 * D])
        col_g1 = sb("col_g1", [P, 1])
        col_b1 = sb("col_b1", [P, 1])
        col_c1 = sb("col_c1", [P, 2])
        col_gat = sb("col_gat", [P, 2])
        bc_g2 = sb("bc_g2", [P, D])
        bc_b2 = sb("bc_b2", [P, D])

        xN = sb("xN", [P, NB, D])
        nodebuf = sb("nodebuf", [P, 4 * NPAD])
        acc = nodebuf[:, 0:2 * NPAD].rearrange("p (w n) -> p w n", w=2)
        xT = nodebuf[:, 2 * NPAD:3 * NPAD]
        nA = nodebuf[:, 3 * NPAD:4 * NPAD].rearrange("p (b f) -> p b f", f=D)
        rows_i = nA[0:ROWS, 4:4 + 4 * QUARTERS, :].bitcast(I32).rearrange("r (n q) p -> r n q p", n=4)
        sources = [nodebuf[:, 11264 + k * G * P:11264 + (k + 1) * G * P].bitcast(I32) for k in range(SLOTS)]
        before = nodebuf[:, 0:HI * (TILES + 1)].rearrange("p (h t) -> p h t", h=HI)
        stats = [sb(f"stats{i}", [P, 4, 6]) for i in range(2)]
        mv = [sb(f"mv{i}", [P, 4, 2]) for i in range(2)]
        std = [sb(f"std{i}", [P, 4]) for i in range(2)]
        rstd = [sb(f"rstd{i}", [P, 4]) for i in range(2)]
        shift = [sb(f"shift{i}", [P, 4]) for i in range(2)]
        den = sb("den", [P, NB * HEADS])
        rden = sb("rden", [P, NB * HEADS])
        pair = sb("pair", [P, 8])

        idx = [sb(f"idx{s}", [P, G], I32) for s in range(SLOTS)]
        rowbuf = sb("rowbuf", [P, SLOTS * G * 2 * D])
        rows = [rowbuf[:, s * G * 2 * D:(s + 1) * G * 2 * D] for s in range(SLOTS)]
        winbuf = sb("winbuf", [P, SLOTS, G * D])
        window = [winbuf[:, s, :].rearrange("p (k f) -> p k f", k=G) for s in range(SLOTS)]
        stage = [rowbuf[:, i * 12 * D:(i + 1) * 12 * D].rearrange("p (b w) -> p b w", b=4) for i in range(2)]
        ffT = [winbuf[:, 2 * i:2 * i + 2, :] for i in range(2)]
        hot = [sb(f"hot{s}", [P, G, P]) for s in range(SLOTS)]
        hotT = [sb(f"hotT{i}", [P, G, P]) for i in range(2)]
        prod = [sb(f"prod{i}", [P, G, D]) for i in range(2)]
        leaky = [sb(f"leaky{i}", [P, G, D]) for i in range(2)]
        raw = [sb(f"raw{i}", [P, G, HEADS]) for i in range(2)]
        clipped = [sb(f"clipped{i}", [P, G, HEADS]) for i in range(2)]
        score = [sb(f"score{i}", [P, G, D]) for i in range(2)]
        msg = [sb(f"msg{i}", [P, G, D]) for i in range(2)]
        low_hot, low_hotT, low_hot_b = prod, leaky, msg
        high_hot = [sb(f"high_hot{i}", [P, G, HI]) for i in range(4)]
        prior_h = [sb(f"prior_h{i}", [P, G, HI]) for i in range(2)]
        prior = [sb(f"prior{i}", [P, G]) for i in range(2)]
        within = [sb(f"within{i}", [P, G]) for i in range(2)]
        place = [sb(f"place{s}", [P, G], I32) for s in range(SLOTS)]
        base = sb("base", [P, HI])
        high_sum = sb("high_sum", [P, HI + 1])
        matched = score
        msg_rel = [sb(f"msg_rel{i}", [P, G]) for i in range(SLOTS)]
        alpha_g = score

        logits = softbuf[:, 0:GHEADS * TILES].rearrange("p (t h) -> p t h", h=GHEADS)
        alpha = softbuf[:, GHEADS * TILES:].rearrange("p (t h) -> p t h", h=GHEADS)
        best_f, best_b, held = [
            rowspace[0:ROWS, i * 1024:(i + 1) * 1024].rearrange("r (q h p) -> r q h p", q=QUARTERS, h=GHEADS)
            for i in range(3)]
        carry_f = endbuf[:, 0:TILES + 1]
        carry_b = endbuf[:, 2 * TILES:3 * TILES + 1]

        psT = [ps(f"psT{i}", [P, 512]) for i in range(2)]
        psQ = [ps(f"psQ{i}", [P, 512]) for i in range(2)]
        psA = [ps(f"psA{i}", [P, 1024]) for i in range(2)]
        psS = [psA[i][:, :].rearrange("p (k w n) -> p k w n", k=G, w=2) for i in range(2)]

        s_meta = sem("meta_landed")
        s_x = sem("x_landed")
        s_wts = sem("weights_landed")
        s_pool = sem("pool_made")
        s_seeded = sem("seeded")
        s_tofloat = sem("tofloat")
        s_cols = sem("cols_in_psum")
        s_colsv = sem("cols_copied")
        s_mask = sem("masks_made")
        s_out = sem("out_stored")

        class Count:

            def __init__(self, sem, base):
                self.sem, self.base = sem, base

        def counted(name, totals):
            handle = sem(name)
            return [Count(handle, sum(totals[:u])) for u in range(len(totals))]

        def shared(prefix, uses):
            spaces = [{} for _ in uses]
            for name in dict.fromkeys(n for use in uses for n in use):
                totals = [use.get(name, 0) for use in uses]
                width = max(len(t) if isinstance(t, list) else 0 for t in totals)
                if width:
                    per_slot = [counted(f"{prefix}_{name}{k}", [t[k] if t else 0 for t in totals]) for k in range(width)]
                for u, space in enumerate(spaces):
                    if width:
                        space[name] = [slot[u] for slot in per_slot]
                if not width:
                    for space, count in zip(spaces, counted(f"{prefix}_{name}", totals)):
                        space[name] = count
            return [namedtuple("Use", space)(**space) for space in spaces]

        def turns(eng, step):
            for s in range(SLOTS):
                step(0, s)
            with eng.Fori(1, TURNS - 1) as i:
                for s in range(SLOTS):
                    step(i, s)
            for s in range(SLOTS):
                step(TURNS - 1, s)

        def ahead(i, s, n):
            j, t = divmod(s + n, SLOTS)
            if isinstance(i, int) and i + j >= TURNS:
                return None
            return i + j, t

        def behind(i, s):
            if s > 0:
                return i, s - 1
            if isinstance(i, int) and i == 0:
                return None
            return i - 1, SLOTS - 1

        def reached(eng, count, n):
            if isinstance(n, int) and n <= 0:
                return
            eng.wait_ge(count.sem, count.base + n)

        s_chain = sem("dve_chain")
        s_xtable = sem("x_table_stored")
        s_first = sem("first_src_landed")
        s_total = sem("totals_in_psum")
        s_base = sem("base_ready")

        SP, DVE = mybir.EngineType.SP, mybir.EngineType.DVE

        def load_firsts(engine, g, first=None):
            _, values = nc.values_load_multi_w_load_instructions(
                (first_dst if first is None else first)[0:1, bass.ds(G * g, G)], engines=[engine], min_val=0, max_val=NPAD - P,
                skip_runtime_bounds_check_because="the program caps them at NPAD - P, and node numbers are not negative")
            return values

        def whole(name):
            return a[name]

        def row(name):
            return a[name].rearrange("(o f) -> o f", o=1)

        def col(name):
            return a[name].rearrange("(f o) -> f o", o=1)

        weight_loads = [
            (W0[:, :], a["L0_gnn_W"]),
            (Wkvq[0][:, 0:D], a["L1_gnn_Wk"]), (Wkvq[0][:, D:2 * D], a["L1_gnn_Wv"]), (Wkvq[0][:, 2 * D:], a["L1_gnn_Wq"]),
            (Wkvq[1][:, 0:D], a["L3_gnn_Wk"]), (Wkvq[1][:, D:2 * D], a["L3_gnn_Wv"]), (Wkvq[1][:, 2 * D:], a["L3_gnn_Wq"]),
            (Wo[0][:, :], a["L1_gnn_Wo"]), (Wo[1][:, :], a["L3_gnn_Wo"]),
            (W1[:, :], a["L1_gnn_W1"]), (W2[:, :, :], a["L1_gnn_W2"].rearrange("(k p) f -> p k f", p=P)),
            (row_b0[:, :], row("L0_gnn_b")), (row_bo[0][:, :], row("L1_gnn_bo")), (row_bo[1][:, :], row("L3_gnn_bo")),
            (row_c2[:, :], row("L1_gnn_c2")),
            (row_kvq[:, 0:D], row("L3_gnn_bk")), (row_kvq[:, D:2 * D], row("L3_gnn_bv")), (row_kvq[:, 2 * D:], row("L3_gnn_bq")),
            (col_g1[:, :], col("L1_gnn_g1")), (col_b1[:, :], col("L1_gnn_b1")),
            (col_c1[:, :], a["L1_gnn_c1"].rearrange("(k p) -> p k", p=P)),
            (col_gat[:, :], a["L2_gnn_bias"].rearrange("l f -> f l")),
            (bc_g2[:, :], row("L1_gnn_g2").to_broadcast([P, D])), (bc_b2[:, :], row("L1_gnn_b2").to_broadcast([P, D])),
        ]
        for l in range(2):
            weight_loads += [
                (Wsd[l][:, 0:D], a["L2_gnn_Wl"][l]), (Wsd[l][:, D:], a["L2_gnn_Wr"][l]),
                (att[l][:, :], a["L2_gnn_att"][l:l + 1].rearrange("o h c -> o (h c)").to_broadcast([P, D])),
            ]


        def per_group(names):
            return {n: NG for n in names.split()}

        GATHERED = dict(slot_open=NG, idx_open=NG, idx_landed=[16 * TURNS] * SLOTS, rows_landed=[16 * G * TURNS] * SLOTS)
        SPREAD = dict(window_landed=[16 * G * TURNS] * SLOTS, **per_group("hotT_psum hotT_ready spread_ready"))
        SUMMED = dict(acc_written=TILES, **per_group("hot_ready sums_ready"))
        ATT = {**GATHERED, **SPREAD, **SUMMED, **per_group("spread_used raw_ready clip_ready score_ready msg_ready")}
        GAT = {**GATHERED, **SPREAD, **per_group("spread_used hot_ready leaky_ready weighted logit_ready"), "spilled": [16 * TURNS] * SLOTS}
        MIX = {**SUMMED, **per_group("alpha_copied msg_ready"), "rows_loaded": [16 * TURNS] * SLOTS}
        COUNT = per_group("hot_ready counted before_ready")
        SEND = {**SPREAD, **per_group("hot_ready low_ready low_used low_psum lowT_ready prior_psum slot_open "
                                      "prior_ready within_ready prior_used place_ready scaled"),
                "rows_sent": [16 * G * TURNS] * SLOTS, "sources_landed": [16 * TURNS] * SLOTS}
        SUM = {**SUMMED, **per_group("rel_ready"), "rows_loaded": [16 * TURNS] * SLOTS}
        a_count, a_send, a_sum, att0, gat0, mix0, gat1, mix1, att1 = shared("edge", [COUNT, SEND, SUM, ATT, GAT, MIX, GAT, MIX, ATT])
        a_att, a_gat, a_mix = [att0, att1], [gat0, gat1], [mix0, mix1]
        NCH = len(CHUNKS)

        def per_chunk(names):
            return {n: NCH for n in names.split()}

        LN = per_chunk("z_ready stats_ready var_ready std_ready rstd_ready coef_ready norm_ready")
        n_ln = shared("ln", [LN] * 4)
        n_tr = shared("tr", [per_chunk("in_psum copied")] * 4)
        n_ff, = shared("ff", [{**LN, **per_chunk("up_ready up_copied scaled xb_ready v_ready stats3_ready var3_ready "
                                                 "std3_ready rstd3_ready coef3_ready")}])
        STORED = [32 * len(CHUNKS[c::2]) for c in range(2)]
        n_tb = shared("tb", [dict(product_ready=NB, copied=NB, stored=STORED)] * 4)
        n_nm = shared("nm", [dict(den_ready=1, den_copied=1, rden_ready=1, **per_chunk("along spread_ready scaled"))] * 4)
        n_sm = shared("sm", [dict.fromkeys("rowwise scanned ends_up carried carries_down best best_up alpha_ready_in "
                                           "exp_ready alpha_ready".split(), 1)] * 2)
        n_pr = shared("pr", [dict.fromkeys("summed mean squared total std ready x_ready".split(), 1)] * 2)
        s_zeroed = sem("acc_zeroed")

        ctx.enter_context(nc.allow_non_contiguous_dma(reason="small loads at the start: tile ends, per-feature columns"))
        block = ctx.enter_context(nc.Block())

        TABLES = [
            (Wkvq[0], [(kv_table[0], 0, 2 * D), (q_table[0], 2 * D, 3 * D)], None),
            (Wsd[0], [(xs_table[0], 0, D), (xd_table[0], D, 2 * D)], None),
            (Wsd[1], [(xs_table[1], 0, D), (xd_table[1], D, 2 * D)], None),
            (Wkvq[1], [(kv_table[1], 0, 2 * D), (q_table[1], 2 * D, 3 * D)], row_kvq),
        ]
        def tables_in_dram(eng, t):
            for c in range(2):
                reached(eng, n_tb[t].stored[c], STORED[c])

        @block.sync
        def _(sp):
            for n, at in ((0, 1), (1, 0), (2, 2)):
                sp.dma_start(rows_i[:, n], a["dst"][at:at + EPAD].rearrange("(q r p) -> r q p", q=QUARTERS, r=ROWS)).then_inc(s_meta, 16)
            sp.dma_start(rows_i[:, 3], a["src"].rearrange("(q r p) -> r q p", q=QUARTERS, r=ROWS)).then_inc(s_meta, 16)
            sp.dma_start(rows_f[:, 4], a["edge_weight"].rearrange("(q r p) -> r q p", q=QUARTERS, r=ROWS)).then_inc(s_meta, 16)
            sp.dma_start(first_i[0:1, :], a["dst"][1:1 + P * (TILES - 1) + 1:P].rearrange("(o t) -> o t", o=1)).then_inc(s_meta, 16)
            for h in range(GHEADS):
                for j, at in enumerate((0, 1, P, P + 1)):
                    sp.dma_start(ends_i[h:h + 1, j, :],
                                 a["dst"][at:at + P * (TILES - 1) + 1:P].rearrange("(o t) -> o t", o=1)).then_inc(s_meta, 16)
            sp.dma_start(xN[:, 0:FULLB, :], a["x"][0:FULLB * P, :].rearrange("(b p) f -> p b f", p=P)).then_inc(s_x, 16)
            sp.wait_ge(s_pool, 1)
            sp.dma_start(xN[0:TAILR, FULLB, :], a["x"][FULLB * P:N, :]).then_inc(s_x, 16)
            for dst, src in weight_loads:
                sp.dma_start(dst, src).then_inc(s_wts, 16)

            def fetch_idx(ns, i, s):
                g = SLOTS * i + s
                reached(sp, ns.rows_landed[s], 16 * G * i)
                sp.sem_inc(ns.idx_open.sem, 1)
                sp.dma_start(idx[s][:, :], src_idx[:, bass.ds(G * g, G)]).then_inc(ns.idx_landed[s].sem, 16)

            def fetch_window(ns, table, i, s):
                g = SLOTS * i + s
                firsts = load_firsts(SP, g)
                reached(sp, ns.spread_ready, g - SLOTS + 1)
                for k in range(G):
                    sp.dma_start(window[s][:, k, :], table[bass.ds(firsts[k], P), :]).then_inc(ns.window_landed[s].sem, 16)

            def store_tables(t):
                for c, (b0, nb) in enumerate(CHUNKS):
                    reached(sp, n_tb[t].copied, b0 + nb)
                    for table, lo, hi in TABLES[t][1]:
                        sp.dma_start(table[b0 * P:(b0 + nb) * P, :].rearrange("(b p) f -> p b f", p=P),
                                     stage[c % 2][:, 0:nb, lo:hi]).then_inc(n_tb[t].stored[c % 2].sem, 16)

            sp.wait_ge(s_x, 32)
            sp.dma_start(x_table.rearrange("(b p) f -> p b f", p=P), xN[:, :, :]).then_inc(s_xtable, 16)
            sp.wait_ge(s_xtable, 16)
            sp.wait_ge(s_colsv, 1)

            def fetch_sources(i, s):
                g = SLOTS * i + s
                reached(sp, a_send.prior_used, g - SLOTS + 1)
                sp.dma_start(sources[s], a["src"][bass.ds(g * (G * P), G * P)].rearrange("(o e) -> o e", o=1)
                             .to_broadcast([P, G * P])).then_inc(a_send.sources_landed[s].sem, 16)
                fetch_window(a_send, x_table, i, s)
            turns(sp, fetch_sources)
            for s in range(SLOTS):
                reached(sp, a_send.rows_sent[s], 16 * G * TURNS)
            sp.dma_start(first_src_f[0:1, :], sorted_msgs.rearrange("(t p) w -> t p w", p=P)[:, 0, D]
                         .rearrange("(o t) -> o t", o=1)).then_inc(s_first, 16)

            def fetch_messages(i, s):
                g = SLOTS * i + s
                reached(sp, a_sum.sums_ready, g - SLOTS + 1)
                sp.dma_start(rows[s][:, 0:G * SENT].rearrange("p (k w) -> p k w", k=G),
                             sorted_msgs[bass.ds(g * (G * P), G * P), :].rearrange("(k p) w -> p k w", p=P)
                             ).then_inc(a_sum.rows_loaded[s].sem, 16)
            turns(sp, fetch_messages)

            def attention(n, t):
                ns = a_att[n]
                store_tables(t)
                tables_in_dram(sp, t)

                def step(i, s):
                    fetch_idx(ns, i, s)
                    fetch_window(ns, q_table[n], i, s)
                turns(sp, step)

            def gat(n, t):
                ns, mix = a_gat[n], a_mix[n]
                store_tables(t)
                tables_in_dram(sp, t)

                def step(i, s):
                    fetch_idx(ns, i, s)
                    fetch_window(ns, xd_table[n], i, s)
                    if s >= 2:
                        spill_rows(i, s - 2)
                    elif not (isinstance(i, int) and i == 0):
                        spill_rows(i - 1, s + 2)

                def spill_rows(i, s):
                    g = SLOTS * i + s
                    reached(sp, ns.rows_landed[s], 16 * G * (i + 1))
                    sp.dma_start(edge_rows[n][bass.ds(g, 1)].rearrange("o p f -> (o p) f"),
                                 rows[s][:, 0:G * D]).then_inc(ns.spilled[s].sem, 16)
                turns(sp, step)
                spill_rows(TURNS - 1, 2)
                spill_rows(TURNS - 1, 3)
                for s in range(SLOTS):
                    reached(sp, ns.spilled[s], 16 * TURNS)
                reached(sp, ns.spread_used, NG)

                def refetch(i, s):
                    g = SLOTS * i + s
                    reached(sp, mix.msg_ready, g - SLOTS + 1)
                    sp.dma_start(rows[s][:, 0:G * D],
                                 edge_rows[n][bass.ds(g, 1)].rearrange("o p f -> (o p) f")).then_inc(mix.rows_loaded[s].sem, 16)
                turns(sp, refetch)

            attention(0, 0)
            gat(0, 1)
            gat(1, 2)
            attention(1, 3)
            for c, (b0, nb) in enumerate(CHUNKS):
                reached(sp, n_ln[3].norm_ready, c + 1)
                full = min(b0 + nb, FULLB) - b0
                if full > 0:
                    sp.dma_start(out[b0 * P:(b0 + full) * P, :].rearrange("(b p) f -> p b f", p=P),
                                 xN[:, b0:b0 + full, :]).then_inc(s_out, 16)
                if b0 <= FULLB < b0 + nb:
                    sp.dma_start(out[FULLB * P:N, :], xN[0:TAILR, FULLB, :]).then_inc(s_out, 16)
            sp.wait_ge(s_out, 16 * 7)

        @block.gpsimd
        def _(pool):
            nc.gpsimd.memset(xN[:, FULLB:NB, :], 0.0).then_inc(s_pool, 1)
            nc.gpsimd.memset(ident[:, :], 0.0)
            nc.gpsimd.memset(ones[:, :], 1.0)
            nc.gpsimd.memset(sel8[:, :], 0.0)
            nc.gpsimd.memset(sel2[:, :], 0.0)
            nc.gpsimd.memset(earlier[:, :], 1.0)
            nc.gpsimd.memset(later[:, :], 1.0)
            nc.gpsimd.memset(rowbuf[:, :], 0.0)
            nc.gpsimd.memset(before[:, :, 0:1], 0.0)
            nc.gpsimd.iota(iota_i[:, :], pattern=[[1, P]], base=0, channel_multiplier=0)
            nc.gpsimd.memset(eps[:, :], LN_EPS).then_inc(s_pool, 1)
            pool.wait_ge(s_pool, 2)
            nc.gpsimd.tensor_copy(iota[:, :], iota_i[:, :])
            nc.gpsimd.affine_select(out=ident[:, :], in_=ident[:, :], compare_op=ALU.not_equal, fill=1.0,
                                    base=0, pattern=[[-1, P]], channel_multiplier=1)
            nc.gpsimd.affine_select(out=earlier[:, :], in_=earlier[:, :], compare_op=ALU.is_gt, fill=0.0,
                                    base=0, pattern=[[-1, P]], channel_multiplier=1)
            nc.gpsimd.affine_select(out=later[:, :], in_=later[:, :], compare_op=ALU.is_gt, fill=0.0,
                                    base=0, pattern=[[1, P]], channel_multiplier=-1)
            nc.gpsimd.affine_select(out=sel8[:, :], in_=sel8[:, :], compare_op=ALU.not_equal, fill=1.0,
                                    base=0, pattern=[[-DH, HEADS]], channel_multiplier=1)
            nc.gpsimd.affine_select(out=sel2[:, :], in_=sel2[:, :], compare_op=ALU.not_equal, fill=1.0,
                                    base=0, pattern=[[-GC, GHEADS]], channel_multiplier=1).then_inc(s_pool, 1)

            def gather(ns, table, width, i, s, free):
                g = SLOTS * i + s
                reached(pool, ns.idx_landed[s], 16 * (i + 1))
                for fs, n in free(i, s, g):
                    reached(pool, fs, n)
                pool.sem_inc(ns.slot_open.sem, 1)
                for k in range(G):
                    pool.indirect_dma_start(
                        out=rows[s][:, k * width:(k + 1) * width], out_offset=None, in_=table,
                        in_offset=bass.IndirectOffsetOnAxis(ap=idx[s][:, k:k + 1], axis=0)).then_inc(ns.rows_landed[s].sem, 16)

            def send(i, s):
                ns, g = a_send, SLOTS * i + s
                reached(pool, ns.place_ready, g + 1)
                reached(pool, ns.scaled, g + 1)
                pool.sem_inc(ns.slot_open.sem, 1)
                for k in range(G):
                    pool.indirect_dma_start(
                        out=sorted_msgs, out_offset=bass.IndirectOffsetOnAxis(ap=place[s][:, k:k + 1], axis=0),
                        in_=rows[s][:, k * SENT:(k + 1) * SENT], in_offset=None).then_inc(ns.rows_sent[s].sem, 16)
            turns(pool, send)
            for s in range(SLOTS):
                reached(pool, a_send.rows_sent[s], 16 * G * TURNS)
            pool.wait_ge(s_xtable, 16)
            reached(pool, a_send.place_ready, NG)
            nc.gpsimd.memset(nodebuf[:, 0:3 * NPAD], 0.0).then_inc(s_zeroed, 1)

            def attention(n, t):
                ns = a_att[n]
                tables_in_dram(pool, t)
                turns(pool, lambda i, s: gather(ns, kv_table[n][:, :], 2 * D, i, s,
                                                lambda i, s, g: [(ns.msg_ready, g - SLOTS + 1)]))

            def gat(n, t):
                ns, mix = a_gat[n], a_mix[n]
                tables_in_dram(pool, t)
                turns(pool, lambda i, s: gather(ns, xs_table[n][:, :], D, i, s,
                                                lambda i, s, g: [(ns.spread_used, g - SLOTS + 1), (ns.spilled[s], 16 * i)]))
                reached(pool, n_sm[n].alpha_ready, 1)

                def weigh(i, s):
                    g, par = SLOTS * i + s, s % 2
                    reached(pool, mix.sums_ready, g - 1)
                    reached(pool, mix.rows_loaded[s], 16 * (i + 1))
                    reached(pool, mix.alpha_copied, g + 1)
                    nc.gpsimd.tensor_tensor(msg[par][:, :, :].rearrange("p k f -> p (k f)"), rows[s][:, 0:G * D],
                                            alpha_g[par][:, :, :].rearrange("p k f -> p (k f)"),
                                            ALU.mult).then_inc(mix.msg_ready.sem, 1)
                turns(pool, weigh)

            def zero_acc(s, n):
                reached(pool, s, n)
                nc.gpsimd.memset(acc[:, :, :], 0.0).then_inc(s_zeroed, 1)

            zero_acc(n_ln[0].z_ready, len(CHUNKS))
            attention(0, 0)
            pool.wait_ge(s_wts, 16 * len(weight_loads))
            for c, (b0, nb) in enumerate(CHUNKS):
                if c == 0:
                    reached(pool, n_ln[1].z_ready, len(CHUNKS))
                nc.gpsimd.tensor_tensor(xN[:, b0:b0 + nb, :], xN[:, b0:b0 + nb, :],
                                        bc_b2[:, :].unsqueeze(1).to_broadcast([P, nb, D]), ALU.add).then_inc(n_ff.xb_ready.sem, 1)
            zero_acc(n_ln[1].z_ready, len(CHUNKS))
            gat(0, 1)
            zero_acc(n_pr[0].x_ready, 1)
            gat(1, 2)
            zero_acc(n_pr[1].x_ready, 1)
            attention(1, 3)

        @block.scalar
        def _(act):
            def copy_hotT(ns, i, s):
                g, par = SLOTS * i + s, s % 2
                reached(act, ns.hotT_psum, g + 1)
                reached(act, ns.spread_ready, g - 1)
                nc.scalar.copy(hotT[par][:, :, :].rearrange("p k n -> p (k n)"), psT[par][:, :]).then_inc(ns.hotT_ready.sem, 1)

            def next_hotT(ns, i, s):
                if s < SLOTS - 1:
                    copy_hotT(ns, i, s + 1)
                elif not (isinstance(i, int) and i == TURNS - 1):
                    copy_hotT(ns, i + 1, 0)

            def attention(n):
                ns = a_att[n]

                def step(i, s):
                    g, par = SLOTS * i + s, s % 2
                    next_hotT(ns, i, s)
                    reached(act, ns.clip_ready, g + 1)
                    reached(act, ns.sums_ready, g - 1)
                    nc.scalar.activation(score[par][:, :, :].rearrange("p k (h c) -> p (k h) c", c=DH),
                                         clipped[par][:, :, :].rearrange("p k h -> p (k h)").unsqueeze(2)
                                         .to_broadcast([P, G * HEADS, DH]), ACT.Exp,
                                         scale=float(DH) ** -0.5).then_inc(ns.score_ready.sem, 1)
                copy_hotT(ns, 0, 0)
                turns(act, step)

            def gat(n):
                ns = a_gat[n]

                def step(i, s):
                    next_hotT(ns, i, s)
                copy_hotT(ns, 0, 0)
                turns(act, step)
                sm = n_sm[n]
                reached(act, sm.alpha_ready_in, 1)
                nc.scalar.activation(alpha[:, :, :], alpha[:, :, :], ACT.Exp).then_inc(sm.exp_ready.sem, 1)
                reached(act, sm.alpha_ready, 1)

                def spread_alpha(i, s):
                    mix, g, par = a_mix[n], SLOTS * i + s, s % 2
                    reached(act, mix.sums_ready, g - 1)
                    nc.scalar.copy(alpha_g[par][:, :, :].rearrange("p k (h c) -> p (k h) c", c=GC),
                                   alpha[:, bass.ds(G * g, G), :].rearrange("p k h -> p (k h)").unsqueeze(2)
                                   .to_broadcast([P, G * GHEADS, GC])).then_inc(mix.alpha_copied.sem, 1)
                turns(act, spread_alpha)

            def root(dst, var, ready, done, n):
                reached(act, ready, n)
                nc.scalar.activation(dst, var, ACT.Sqrt, bias=eps[:, :]).then_inc(done.sem, 1)

            def normalise(ns, dest, source=lambda c: psA[c % 2][:, 0:512].rearrange("p (b f) -> p b f", f=D)):
                for c, (b0, nb) in enumerate(CHUNKS):
                    root(std[c % 2][:, 0:nb], mv[c % 2][:, 0:nb, 1], ns.var_ready, ns.std_ready, c + 1)
                    reached(act, ns.coef_ready, c + 1)
                    for j in range(nb):
                        last = nc.scalar.activation(dest[:, b0 + j, :], source(c)[:, j, :], ACT.Identity,
                                                    bias=shift[c % 2][:, j:j + 1], scale=rstd[c % 2][:, j:j + 1])
                    last.then_inc(ns.norm_ready.sem, 1)

            def spread_rden(n, heads):
                ns = n_nm[n]
                reached(act, ns.rden_ready, 1)
                for c, (b0, nb) in enumerate(CHUNKS):
                    nc.scalar.copy(nA[:, b0:b0 + nb, :].rearrange("p b (h c) -> p (b h) c", h=heads),
                                   rden[:, b0 * heads:(b0 + nb) * heads].unsqueeze(2)
                                   .to_broadcast([P, nb * heads, D // heads])).then_inc(ns.along.sem, 1)

            def tables(t):
                ns, width = n_tb[t], 3 * D if TABLES[t][0] in Wkvq else 2 * D
                for c, (b0, nb) in enumerate(CHUNKS):
                    for j in range(nb):
                        b = b0 + j
                        reached(act, ns.product_ready, b + 1)
                        if c >= 2 and j == 0:
                            reached(act, ns.stored[c % 2], 32 * (c // 2))
                        nc.scalar.copy(stage[c % 2][:, j, 0:width], psQ[b % 2][:, 0:width]).then_inc(ns.copied.sem, 1)

            def count(i, s):
                g = SLOTS * i + s
                reached(act, a_count.counted, g + 1)
                nc.scalar.copy(before[:, :, bass.ds(G * g + 1, G)].rearrange("p h k -> p k h"),
                               psQ[s % 2][:, 0:G * HI].rearrange("p (k h) -> p k h", k=G)).then_inc(a_count.before_ready.sem, 1)

            def send(i, s):
                ns, g, par = a_send, SLOTS * i + s, s % 2
                nxt = ahead(i, s, 1)
                if nxt:
                    transposed_hots(*nxt)
                reached(act, ns.spread_ready, g + 1)
                reached(act, ns.rows_sent[s], 16 * G * i)
                row = rows[s][:, 0:G * SENT].rearrange("p (k w) -> p k w", k=G)
                for k in range(G):
                    nc.scalar.activation(row[:, k, 0:D], psQ[par][:, k * D:(k + 1) * D], ACT.Copy,
                                         scale=weight[:, bass.ds(G * g + k, 1)])
                nc.scalar.copy(row[:, :, D], src_f[:, bass.ds(G * g, G)]).then_inc(ns.scaled.sem, 1)

            def transposed_hots(i, s):
                ns, g, par = a_send, SLOTS * i + s, s % 2
                reached(act, ns.hotT_psum, g + 1)
                reached(act, ns.spread_ready, g - 1)
                nc.scalar.copy(hotT[par][:, :, :].rearrange("p k n -> p (k n)"), psT[0][:, :]).then_inc(ns.hotT_ready.sem, 1)
                reached(act, ns.low_psum, g + 1)
                reached(act, ns.prior_psum, g - 1)
                nc.scalar.copy(low_hotT[par][:, :, :].rearrange("p k n -> p (k n)"), psT[1][:, :]).then_inc(ns.lowT_ready.sem, 1)

            act.wait_ge(s_pool, 3)
            turns(act, count)
            act.wait_ge(s_colsv, 2)
            transposed_hots(0, 0)
            turns(act, send)
            normalise(n_ln[0], xN)
            tables(0)
            attention(0)
            spread_rden(0, HEADS)
            normalise(n_ln[1], nA)
            act.wait_ge(s_wts, 16 * len(weight_loads))
            for c, (b0, nb) in enumerate(CHUNKS):
                reached(act, n_tr[1].in_psum, c + 1)
                nc.scalar.activation(xT[:, b0 * P:(b0 + nb) * P], psT[c % 2][:, 0:nb * P], ACT.Identity,
                                     bias=col_b1[:, :], scale=col_g1[:, :]).then_inc(n_tr[1].copied.sem, 1)
            for c, (b0, nb) in enumerate(CHUNKS):
                reached(act, n_ff.up_ready, c + 1)
                for k in range(2):
                    last = nc.scalar.activation(ffT[c % 2][:, k, 0:nb * P], psQ[k][:, 0:nb * P], ACT.Relu,
                                                bias=col_c1[:, k:k + 1])
                last.then_inc(n_ff.up_copied.sem, 1)
                root(std[c % 2][:, 0:nb], mv[c % 2][:, 0:nb, 1], n_ff.var_ready, n_ff.std_ready, c + 1)
                root(std[c % 2][:, 0:nb], mv[c % 2][:, 0:nb, 1], n_ff.var3_ready, n_ff.std3_ready, c + 1)
                reached(act, n_ff.coef3_ready, c + 1)
                for j in range(nb):
                    last = nc.scalar.activation(xN[:, b0 + j, :], nA[:, b0 + j, :], ACT.Identity,
                                                bias=shift[c % 2][:, j:j + 1], scale=rstd[c % 2][:, j:j + 1])
                last.then_inc(n_ff.norm_ready.sem, 1)

            def pairnorm(n):
                pr = n_pr[n]
                spread_rden(1 + n, GHEADS)
                reached(act, n_nm[1 + n].scaled, len(CHUNKS))
                nc.scalar.activation(acc[:, 0, 0:N], acc[:, 0, 0:N], ACT.Identity, bias=col_gat[:, n:n + 1],
                                     accum_out=pair[:, 0:1]).then_inc(pr.summed.sem, 1)
                reached(act, pr.mean, 1)
                nc.scalar.activation(acc[:, 1, 0:N], acc[:, 0, 0:N], ACT.Square, bias=pair[:, 1:2],
                                     accum_out=pair[:, 2:3]).then_inc(pr.squared.sem, 1)
                reached(act, pr.total, 1)
                nc.scalar.activation(pair[:, 3:4], psT[1][:, 0:1], ACT.Sqrt, bias=eps[:, :], scale=1.0 / N).then_inc(pr.std.sem, 1)
                reached(act, pr.ready, 1)
                nc.scalar.activation(xT[:, 0:N], acc[:, 0, 0:N], ACT.Relu, bias=pair[:, 5:6],
                                     scale=pair[:, 4:5]).then_inc(pr.x_ready.sem, 1)

            tables(1)
            gat(0)
            pairnorm(0)
            tables(2)
            gat(1)
            pairnorm(1)
            normalise(n_ln[2], xN)
            tables(3)
            attention(1)
            spread_rden(3, HEADS)
            normalise(n_ln[3], xN)

        @block.vector
        def _(dve):
            chain = [0]

            def link(ins):
                chain[0] += 1
                ins.then_inc(s_chain, 1)
                dve.wait_ge(s_chain, chain[0])

            V = nc.vector
            dve.wait_ge(s_meta, 16 * 14)
            V.tensor_copy(rows_f[:, 0:4], rows_i[:, 0:4])
            V.tensor_scalar(first_dst[:, :], first_i[:, :], float(NPAD - P), None, ALU.min)
            link(V.tensor_copy(ends_f[:, :, :], ends_i[:, :, :]))
            link(V.tensor_copy(first_f[:, :], first_dst[:, :]))
            link(V.tensor_tensor(open_bwd[:, :, :], rows_f[:, 0], rows_f[:, 2], ALU.not_equal))
            V.tensor_scalar(open_bwd[:, :, :], open_bwd[:, :, :], 1.0, None, ALU.add).then_inc(s_tofloat, 1)
            dve.wait_ge(s_cols, 1)
            V.tensor_copy(src_f[:, :], psT[0][:, 0:TILES])
            link(V.tensor_copy(src_idx[:, :], psT[0][:, 0:TILES]))
            for part, op, by in ((src_high, ALU.arith_shift_right, 7), (src_low, ALU.bitwise_and, P - 1)):
                link(V.tensor_scalar(part_i, src_idx[:, :], by, None, op))
                link(V.tensor_copy(part, part_i))
            V.tensor_copy(first_f[:, :], first_dst[:, :]).then_inc(s_colsv, 1)
            V.tensor_copy(weight[:, :], psQ[0][:, 0:TILES])
            V.tensor_copy(copies[:, :], psQ[1][:, 0:TILES])
            link(V.tensor_copy(dst_rel[:, :], psT[1][:, 0:TILES]))
            V.tensor_tensor(dst_rel[:, :], dst_rel[:, :], psA[0][:, 0:TILES], ALU.subtract).then_inc(s_colsv, 1)
            dve.wait_ge(s_colsv, 2)

            def masks():
                for q_scan, q_open, nb, edge, first in ((scan_fwd, open_fwd, 1, 0, 0), (scan_bwd, open_bwd, 2, P - 1, P - 1)):
                    link(V.tensor_tensor(q_open[:, :, :], rows_f[:, 0], rows_f[:, nb], ALU.not_equal))
                    for h in range(GHEADS):
                        link(V.tensor_scalar(q_scan[:, :, h, :], q_open[:, :, :], -BIG, None, ALU.mult))
                    link(V.memset(q_scan[:, :, :, edge:edge + 1], -BIG))
                    link(V.tensor_tensor(q_open[:, :, :], rows_f[:, 0],
                                         rows_f[:, nb, :, edge:edge + 1].to_broadcast([ROWS, QUARTERS, P]), ALU.not_equal))
                    link(V.tensor_scalar(q_open[:, :, :], q_open[:, :, :], -BIG, None, ALU.mult))
                link(V.tensor_tensor(pass_fwd[:, :], ends_f[:, 2, :], ends_f[:, 0, :], ALU.not_equal))
                link(V.tensor_scalar(pass_fwd[:, :], pass_fwd[:, :], -BIG, None, ALU.mult))
                link(V.tensor_tensor(pass_bwd[:, :], ends_f[:, 1, :], ends_f[:, 3, :], ALU.not_equal))
                link(V.tensor_scalar(pass_bwd[:, :], pass_bwd[:, :], -BIG, None, ALU.mult))

            def make_hot(ns, i, s):
                g = SLOTS * i + s
                V.tensor_tensor(hot[s][:, :, :], iota[:, :].unsqueeze(1).to_broadcast([P, G, P]),
                                dst_rel[:, bass.ds(G * g, G)].unsqueeze(2).to_broadcast([P, G, P]),
                                ALU.is_equal).then_inc(ns.hot_ready.sem, 1)

            def add_sums(ns, i, s, both):
                g, par = SLOTS * i + s, s % 2
                firsts = load_firsts(DVE, g, first_src if ns is a_sum else first_dst)
                reached(dve, ns.sums_ready, g + 1)
                for k in range(G):
                    reached(dve, ns.acc_written, G * g + k)
                    if both:
                        d, v = acc[:, :, bass.ds(firsts[k], P)], psS[par][:, k]
                    else:
                        d, v = acc[:, 0, bass.ds(firsts[k], P)], psS[par][:, k, 0]
                    V.tensor_tensor(d, d, v, ALU.add).then_inc(ns.acc_written.sem, 1)

            def hot_high(dst, g):
                return V.tensor_tensor(dst[:, :, :], iota[:, 0:HI].unsqueeze(1).to_broadcast([P, G, HI]),
                                       src_high[:, bass.ds(G * g, G)].unsqueeze(2).to_broadcast([P, G, HI]), ALU.is_equal)

            def hot_low(dst, g):
                return V.tensor_tensor(dst[:, :, :], iota[:, :].unsqueeze(1).to_broadcast([P, G, P]),
                                       src_low[:, bass.ds(G * g, G)].unsqueeze(2).to_broadcast([P, G, P]), ALU.is_equal)

            def count(i, s):
                g = SLOTS * i + s
                reached(dve, a_count.counted, g - SLOTS + 1)
                hot_high(high_hot[s], g)
                hot_low(hot[s], g).then_inc(a_count.hot_ready.sem, 1)

            def run_up():
                reached(dve, a_count.before_ready, NG)
                link(V.memset(high_sum[:, 0:1], 0.0))
                for h in range(HI):
                    c = before[:, h, 1:TILES + 1]
                    last = V.tensor_tensor_scan(c, ones[:, 0:1].to_broadcast([P, TILES]), c, 0.0, ALU.mult, ALU.add)
                last.then_inc(s_total, 1)
                dve.wait_ge(s_base, 1)
                link(V.tensor_tensor_scan(high_sum[:, 1:HI + 1], ones[:, 0:HI], psQ[1][:, 0:HI], 0.0, ALU.mult, ALU.add))
                V.tensor_tensor(base[:, :], psQ[0][:, 0:HI], high_sum[:, 0:HI], ALU.add).then_inc(s_base, 1)

            def send_hots(i, s):
                ns, g, par = a_send, SLOTS * i + s, s % 2
                reached(dve, ns.spread_ready, g - SLOTS + 1)
                make_hot(ns, i, s)
                reached(dve, ns.low_psum, g - 1)
                hot_low(low_hot[par], g)
                hot_high(high_hot[s], g).then_inc(ns.low_ready.sem, 1)

            def send(i, s):
                ns, g, par = a_send, SLOTS * i + s, s % 2
                reached(dve, ns.sources_landed[s], 16 * (i + 1))
                for k in range(G):
                    V.scalar_tensor_tensor(matched[par][:, k, :], sources[s][:, k * P:(k + 1) * P], src_f[:, bass.ds(G * g + k, 1)],
                                           earlier[:, :], ALU.is_equal, ALU.mult, accum_out=within[par][:, k:k + 1])
                reached(dve, ns.prior_psum, g + 1)
                V.tensor_tensor(prior_h[par][:, :, :], psA[par][:, 512:512 + G * HI].rearrange("p (k h) -> p k h", k=G),
                                high_hot[s][:, :, :], ALU.mult).then_inc(ns.prior_used.sem, 1)
                reached(dve, ns.prior_used, g + 1)
                V.tensor_reduce(prior[par][:, :], prior_h[par][:, :, :], AX.X, ALU.add).then_inc(ns.prior_ready.sem, 1)
                if ahead(i, s, 2):
                    send_hots(*ahead(i, s, 2))
                reached(dve, ns.prior_ready, g + 1)
                reached(dve, ns.rows_sent[s], 16 * G * i)
                V.tensor_tensor(place[s][:, :], prior[par][:, :], within[par][:, :], ALU.add).then_inc(ns.place_ready.sem, 1)

            def sum_pass():
                ns = a_sum

                def relative(i, s):
                    g = SLOTS * i + s
                    reached(dve, ns.rows_loaded[s], 16 * (i + 1))
                    V.tensor_tensor(msg_rel[s][:, :], rows[s][:, 0:G * SENT].rearrange("p (k w) -> p k w", k=G)[:, :, D],
                                    first_src_bc[:, bass.ds(G * g, G)], ALU.subtract).then_inc(ns.rel_ready.sem, 1)

                def step(i, s):
                    g = SLOTS * i + s
                    if g is not None and ahead(i, s, 1):
                        relative(*ahead(i, s, 1))
                    reached(dve, ns.rel_ready, g + 1)
                    reached(dve, ns.sums_ready, g - SLOTS + 1)
                    V.tensor_tensor(hot[s][:, :, :], iota[:, :].unsqueeze(1).to_broadcast([P, G, P]),
                                    msg_rel[s][:, :].unsqueeze(2).to_broadcast([P, G, P]),
                                    ALU.is_equal).then_inc(ns.hot_ready.sem, 1)
                    if behind(i, s):
                        add_sums(ns, *behind(i, s), False)
                dve.wait_ge(s_first, 16)
                link(V.tensor_scalar(first_src_f[:, :], first_src_f[:, :], float(NPAD - P), None, ALU.min))
                V.tensor_copy(first_src[:, :], first_src_f[:, :]).then_inc(s_first, 1)
                dve.wait_ge(s_first, 18)
                V.tensor_copy(first_src_bc, psT[0][:, 0:TILES]).then_inc(s_first, 1)
                dve.wait_ge(s_first, 19)
                relative(0, 0)
                turns(dve, step)
                add_sums(ns, TURNS - 1, SLOTS - 1, False)

            def attention(n):
                ns = a_att[n]

                def step(i, s):
                    g, par = SLOTS * i + s, s % 2
                    kv = rows[s][:, :].rearrange("p (k w) -> p k w", k=G)
                    reached(dve, ns.spread_ready, g + 1)
                    reached(dve, ns.rows_landed[s], 16 * G * (i + 1))
                    V.tensor_tensor(prod[par][:, :, :], kv[:, :, 0:D],
                                    psQ[par][:, :].rearrange("p (k f) -> p k f", k=G), ALU.mult).then_inc(ns.spread_used.sem, 1)
                    reached(dve, ns.spread_used, g + 1)
                    V.tensor_reduce(raw[par][:, :, :].rearrange("p k h -> p (k h)"),
                                    prod[par][:, :, :].rearrange("p k (h c) -> p (k h) c", c=DH),
                                    AX.X, ALU.add).then_inc(ns.raw_ready.sem, 1)
                    reached(dve, ns.raw_ready, g + 1)
                    lim = 5.0 * float(DH) ** 0.5
                    V.tensor_scalar(clipped[par][:, :, :], raw[par][:, :, :], lim, -lim, ALU.min, ALU.max).then_inc(ns.clip_ready.sem, 1)
                    if ahead(i, s, 2):
                        reached(dve, ns.sums_ready, g - 1)
                        make_hot(ns, *ahead(i, s, 2))
                    if behind(i, s):
                        add_sums(ns, *behind(i, s), True)
                    reached(dve, ns.score_ready, g + 1)
                    V.tensor_tensor(msg[par][:, :, :], kv[:, :, D:2 * D], score[par][:, :, :], ALU.mult).then_inc(ns.msg_ready.sem, 1)
                make_hot(ns, 0, 0)
                make_hot(ns, 0, 1)
                turns(dve, step)
                add_sums(ns, TURNS - 1, SLOTS - 1, True)

            def gat(n):
                ns, mix, sm = a_gat[n], a_mix[n], n_sm[n]

                def weigh(i, s):
                    g, par = SLOTS * i + s, s % 2
                    reached(dve, ns.spread_used, g + 1)
                    V.scalar_tensor_tensor(leaky[par][:, :, :], prod[par][:, :, :], 0.2, prod[par][:, :, :],
                                           ALU.mult, ALU.max).then_inc(ns.leaky_ready.sem, 1)
                    reached(dve, ns.leaky_ready, g + 1)
                    V.tensor_tensor(msg[par][:, :, :], leaky[par][:, :, :],
                                    att[n][:, :].unsqueeze(1).to_broadcast([P, G, D]), ALU.mult).then_inc(ns.weighted.sem, 1)
                    reached(dve, ns.weighted, g + 1)
                    V.tensor_reduce(logits[:, bass.ds(G * g, G), :].rearrange("p k h -> p (k h)"),
                                    msg[par][:, :, :].rearrange("p k (h c) -> p (k h) c", c=GC),
                                    AX.X, ALU.add).then_inc(ns.logit_ready.sem, 1)

                def step(i, s):
                    g, par = SLOTS * i + s, s % 2
                    reached(dve, ns.spread_ready, g + 1)
                    reached(dve, ns.rows_landed[s], 16 * G * (i + 1))
                    V.tensor_tensor(prod[par][:, :, :].rearrange("p k f -> p (k f)"), rows[s][:, 0:G * D],
                                    psQ[par][:, :], ALU.add).then_inc(ns.spread_used.sem, 1)
                    if ahead(i, s, 2):
                        reached(dve, ns.hotT_psum, g - 1)
                        make_hot(ns, *ahead(i, s, 2))
                    if behind(i, s):
                        weigh(*behind(i, s))
                make_hot(ns, 0, 0)
                make_hot(ns, 0, 1)
                turns(dve, step)
                weigh(TURNS - 1, SLOTS - 1)

                flat = "r q h p -> r (q h p)"
                reached(dve, sm.rowwise, 1)
                rowlog = psA[0][0:ROWS, :]
                V.tensor_tensor_scan(best_f[:, :, :, :].rearrange(flat), scan_fwd[:, :, :, :].rearrange(flat), rowlog,
                                     -BIG, ALU.add, ALU.max)
                V.tensor_tensor_scan(best_b[:, :, :, :].rearrange(flat)[:, ::-1], scan_bwd[:, :, :, :].rearrange(flat)[:, ::-1],
                                     rowlog[:, ::-1], -BIG, ALU.add, ALU.max).then_inc(sm.scanned.sem, 1)
                V.memset(carry_f[:, 0:1], -BIG)
                V.memset(carry_b[:, TILES:TILES + 1], -BIG)
                reached(dve, sm.ends_up, 1)
                V.tensor_tensor_scan(carry_f[:, 1:TILES + 1], pass_fwd[:, :], psT[0][0:2, 0:TILES], -BIG, ALU.add, ALU.max)
                V.tensor_tensor_scan(carry_b[:, 0:TILES][:, ::-1], pass_bwd[:, ::-1], psT[1][0:2, 0:TILES][:, ::-1],
                                     -BIG, ALU.add, ALU.max).then_inc(sm.carried.sem, 1)
                reached(dve, sm.carries_down, 1)
                for best, opened, psc in ((best_f, open_fwd, psQ[0]), (best_b, open_bwd, psQ[1])):
                    link(V.tensor_tensor(
                        held[:, :, :, :],
                        opened[:, :, :].unsqueeze(2).to_broadcast([ROWS, QUARTERS, GHEADS, P]),
                        psc[0:ROWS, 0:QUARTERS * GHEADS].rearrange("r (q h) -> r q h", q=QUARTERS).unsqueeze(3)
                        .to_broadcast([ROWS, QUARTERS, GHEADS, P]), ALU.add))
                    link(V.tensor_tensor(best[:, :, :, :], best[:, :, :, :], held[:, :, :, :], ALU.max))
                V.tensor_tensor(best_f[:, :, :, :], best_f[:, :, :, :], best_b[:, :, :, :], ALU.max).then_inc(sm.best.sem, 1)
                reached(dve, sm.best_up, 1)
                V.tensor_tensor(alpha[:, :, :].rearrange("p t h -> p h t"), logits[:, :, :].rearrange("p t h -> p h t"),
                                psA[1][:, :].rearrange("p (h t) -> p h t", h=2)[:, :, 0:TILES],
                                ALU.subtract).then_inc(sm.alpha_ready_in.sem, 1)
                reached(dve, sm.exp_ready, 1)
                V.tensor_tensor(alpha[:, :, :], alpha[:, :, :], copies[:, :].unsqueeze(2).to_broadcast([P, TILES, GHEADS]),
                                ALU.mult).then_inc(sm.alpha_ready.sem, 1)

                def mix_step(i, s):
                    nxt = ahead(i, s, 1)
                    if nxt:
                        reached(dve, mix.sums_ready, SLOTS * i + s + 1 - SLOTS + 1)
                        make_hot(mix, *nxt)
                    if behind(i, s):
                        add_sums(mix, *behind(i, s), True)
                make_hot(mix, 0, 0)
                turns(dve, mix_step)
                add_sums(mix, TURNS - 1, SLOTS - 1, True)

            def block_stats(ready, n, z, st, m, nb, s1, s2):
                reached(dve, ready, n)
                for j in range(nb):
                    last = V.bn_stats(st[:, j, :], z[:, j, :])
                last.then_inc(s1.sem, 1)
                reached(dve, s1, n)
                for j in range(nb):
                    last = V.bn_aggr(m[:, j, :], st[:, j, :])
                last.then_inc(s2.sem, 1)

            def coefficients(std_ready, s1, s2, n, c, nb):
                reached(dve, std_ready, n)
                V.reciprocal(rstd[c % 2][:, 0:nb], std[c % 2][:, 0:nb]).then_inc(s1.sem, 1)
                reached(dve, s1, n)
                V.scalar_tensor_tensor(shift[c % 2][:, 0:nb], mv[c % 2][:, 0:nb, 0], -1.0, rstd[c % 2][:, 0:nb],
                                       ALU.mult, ALU.mult).then_inc(s2.sem, 1)

            def zchunk(c):
                return psA[c % 2][:, 0:512].rearrange("p (b f) -> p b f", f=D)

            def layernorm(ns):
                nc_ = len(CHUNKS)

                def first_half(c):
                    if c >= 2:
                        reached(dve, ns.norm_ready, c - 1)
                    block_stats(ns.z_ready, c + 1, zchunk(c), stats[c % 2], mv[c % 2], CHUNKS[c][1], ns.stats_ready, ns.var_ready)
                first_half(0)
                for c in range(nc_):
                    if c + 1 < nc_:
                        first_half(c + 1)
                    coefficients(ns.std_ready, ns.rstd_ready, ns.coef_ready, c + 1, c, CHUNKS[c][1])

            def copy_transposed(ns):
                for c, (b0, nb) in enumerate(CHUNKS):
                    reached(dve, ns.in_psum, c + 1)
                    V.tensor_copy(xT[:, b0 * P:(b0 + nb) * P], psT[c % 2][:, 0:nb * P]).then_inc(ns.copied.sem, 1)

            def divide_by_sums(n, heads, op, guard):
                ns = n_nm[n]
                reached(dve, ns.den_ready, 1)
                V.tensor_scalar(den[:, 0:NB * heads], psT[0][:, 0:NB * heads], guard, None, op).then_inc(ns.den_copied.sem, 1)
                reached(dve, ns.den_copied, 1)
                V.reciprocal(rden[:, 0:NB * heads], den[:, 0:NB * heads]).then_inc(ns.rden_ready.sem, 1)
                for c, (b0, nb) in enumerate(CHUNKS):
                    reached(dve, ns.spread_ready, c + 1)
                    d = acc[:, 0, b0 * P:(b0 + nb) * P]
                    V.tensor_tensor(d, d, psQ[c % 2][:, 0:nb * P], ALU.mult).then_inc(ns.scaled.sem, 1)

            def pairnorm(n):
                pr = n_pr[n]
                reached(dve, pr.summed, 1)
                V.tensor_scalar(pair[:, 1:2], pair[:, 0:1], -1.0 / N, None, ALU.mult).then_inc(pr.mean.sem, 1)
                reached(dve, pr.std, 1)
                link(V.reciprocal(pair[:, 4:5], pair[:, 3:4]))
                V.tensor_tensor(pair[:, 5:6], pair[:, 1:2], pair[:, 4:5], ALU.mult).then_inc(pr.ready.sem, 1)

            dve.wait_ge(s_pool, 3)
            turns(dve, count)
            run_up()
            send_hots(0, 0)
            send_hots(0, 1)
            turns(dve, send)
            dve.wait_ge(s_zeroed, 1)
            sum_pass()
            layernorm(n_ln[0])
            copy_transposed(n_tr[0])
            dve.wait_ge(s_zeroed, 2)
            attention(0)
            divide_by_sums(0, HEADS, ALU.max, 1e-30)
            layernorm(n_ln[1])
            masks()
            dve.wait_ge(s_wts, 16 * len(weight_loads))
            reached(dve, n_ln[1].norm_ready, len(CHUNKS))
            for c, (b0, nb) in enumerate(CHUNKS):
                m, st, z = mv[c % 2], stats[c % 2], zchunk(c)
                if c >= 2:
                    reached(dve, n_ff.norm_ready, c - 1)
                block_stats(n_ff.z_ready, c + 1, z, st, m, nb, n_ff.stats_ready, n_ff.var_ready)
                reached(dve, n_ff.std_ready, c + 1)
                V.reciprocal(rstd[c % 2][:, 0:nb], std[c % 2][:, 0:nb]).then_inc(n_ff.rstd_ready.sem, 1)
                for j in range(nb):
                    last = V.scalar_tensor_tensor(nA[:, b0 + j, :], z[:, j, :], m[:, j, 0:1], bc_g2[:, :],
                                                  ALU.subtract, ALU.mult)
                last.then_inc(n_ff.scaled.sem, 1)
                reached(dve, n_ff.rstd_ready, c + 1)
                reached(dve, n_ff.scaled, c + 1)
                reached(dve, n_ff.xb_ready, c + 1)
                for j in range(nb):
                    last = V.scalar_tensor_tensor(nA[:, b0 + j, :], nA[:, b0 + j, :], rstd[c % 2][:, j:j + 1],
                                                  xN[:, b0 + j, :], ALU.mult, ALU.add)
                last.then_inc(n_ff.v_ready.sem, 1)
                block_stats(n_ff.v_ready, c + 1, nA[:, b0:b0 + nb, :], st, m, nb, n_ff.stats3_ready, n_ff.var3_ready)
                coefficients(n_ff.std3_ready, n_ff.rstd3_ready, n_ff.coef3_ready, c + 1, c, nb)
            copy_transposed(n_tr[2])
            dve.wait_ge(s_zeroed, 3)
            gat(0)
            divide_by_sums(1, GHEADS, ALU.add, 1e-16)
            pairnorm(0)
            dve.wait_ge(s_zeroed, 4)
            gat(1)
            divide_by_sums(2, GHEADS, ALU.add, 1e-16)
            pairnorm(1)
            layernorm(n_ln[2])
            copy_transposed(n_tr[3])
            dve.wait_ge(s_zeroed, 5)
            attention(1)
            divide_by_sums(3, HEADS, ALU.max, 1e-30)
            layernorm(n_ln[3])

        @block.tensor
        def _(pe):
            mm, tr = nc.tensor.matmul, nc.tensor.transpose
            pe.wait_ge(s_pool, 3)
            pe.wait_ge(s_tofloat, 1)
            for ps_, src in ((psT[0], rows_f[:, 3]), (psT[1], rows_f[:, 0]), (psQ[0], rows_f[:, 4]), (psQ[1], open_bwd[:, :, :])):
                for q in range(QUARTERS):
                    tr(ps_[:, q * ROWS:(q + 1) * ROWS], src[:, q, :], ident[0:ROWS, 0:ROWS])
            mm(psA[0][:, 0:TILES], ones[0:1, :], first_f[0:1, :], start=True, stop=True).then_inc(s_cols, 1)

            def transpose_hot(ns, i, s):
                g, par = SLOTS * i + s, s % 2
                reached(pe, ns.hot_ready, g + 1)
                reached(pe, ns.hotT_ready, g - 1)
                for k in range(G):
                    last = tr(psT[par][:, k * P:(k + 1) * P], hot[s][:, k, :], ident[:, :])
                last.then_inc(ns.hotT_psum.sem, 1)

            def spread(ns, i, s):
                g, par = SLOTS * i + s, s % 2
                reached(pe, ns.window_landed[s], 16 * G * (i + 1))
                reached(pe, ns.spread_used, g - 1)
                reached(pe, ns.hotT_ready, g + 1)
                for k in range(G):
                    last = mm(psQ[par][:, k * D:(k + 1) * D], hotT[par][:, k, :], window[s][:, k, :], start=True, stop=True)
                last.then_inc(ns.spread_ready.sem, 1)

            def next_spread(ns, i, s):
                if s < SLOTS - 1:
                    nxt = (i, s + 1)
                elif isinstance(i, int) and i == TURNS - 1:
                    return
                else:
                    nxt = (i + 1, 0)
                transpose_hot(ns, *nxt)
                spread(ns, *nxt)

            def scatter(ns, i, s, messages, weights):
                g, par = SLOTS * i + s, s % 2
                reached(pe, ns.acc_written, G * (g - 1))
                for k in range(G):
                    last = mm(psS[par][:, k, 0, :], messages(s, k), hot[s][:, k, :], start=True, stop=True)
                    if weights:
                        last = mm(psS[par][:, k, 1, :], weights(par, k), hot[s][:, k, :], start=True, stop=True)
                last.then_inc(ns.sums_ready.sem, 1)

            def count(i, s):
                g = SLOTS * i + s
                reached(pe, a_count.hot_ready, g + 1)
                reached(pe, a_count.before_ready, g - 1)
                for k in range(G):
                    last = mm(psQ[s % 2][:, k * HI:(k + 1) * HI], hot[s][:, k, :], high_hot[s][:, k, :], start=True, stop=True)
                last.then_inc(a_count.counted.sem, 1)

            def send_transposes(i, s):
                ns, g, par = a_send, SLOTS * i + s, s % 2
                reached(pe, ns.hot_ready, g + 1)
                reached(pe, ns.hotT_ready, g)
                for k in range(G):
                    last = tr(psT[0][:, k * P:(k + 1) * P], hot[s][:, k, :], ident[:, :])
                last.then_inc(ns.hotT_psum.sem, 1)
                reached(pe, ns.low_ready, g + 1)
                reached(pe, ns.lowT_ready, g)
                for k in range(G):
                    last = tr(psT[1][:, k * P:(k + 1) * P], low_hot[par][:, k, :], ident[:, :])
                last.then_inc(ns.low_psum.sem, 1)
                reached(pe, ns.window_landed[s], 16 * G * (i + 1))
                reached(pe, ns.scaled, g - 1)
                reached(pe, ns.hotT_ready, g + 1)
                for k in range(G):
                    last = mm(psQ[par][:, k * D:(k + 1) * D], hotT[par][:, k, :], window[s][:, k, :], start=True, stop=True)
                last.then_inc(ns.spread_ready.sem, 1)
                reached(pe, ns.lowT_ready, g + 1)
                reached(pe, ns.prior_used, g - 1)
                for k in range(G):
                    at = psA[par][:, 512 + k * HI:512 + (k + 1) * HI]
                    mm(at, low_hotT[par][:, k, :], base[:, :], start=True, stop=False)
                    last = mm(at, low_hotT[par][:, k, :], before[:, :, bass.ds(G * g + k, 1)].rearrange("p h o -> p (h o)"),
                              start=False, stop=True)
                last.then_inc(ns.prior_psum.sem, 1)

            def sum_pass():
                ns = a_sum
                pe.wait_ge(s_first, 17)
                mm(psT[0][:, 0:TILES], ones[0:1, :], first_src_f[0:1, :], start=True, stop=True).then_inc(s_first, 1)

                def step(i, s):
                    reached(pe, ns.hot_ready, SLOTS * i + s + 1)
                    reached(pe, ns.rows_loaded[s], 16 * (i + 1))
                    scatter(ns, i, s, lambda s, k: rows[s][:, k * SENT:k * SENT + D], None)
                turns(pe, step)

            def attention(n):
                ns = a_att[n]

                def step(i, s):
                    next_spread(ns, i, s)
                    reached(pe, ns.msg_ready, SLOTS * i + s + 1)
                    scatter(ns, i, s, lambda s, k: msg[s % 2][:, k, :],
                            lambda par, k: score[par][:, k, :])
                transpose_hot(ns, 0, 0)
                spread(ns, 0, 0)
                turns(pe, step)

            def gat(n):
                ns, mix, sm = a_gat[n], a_mix[n], n_sm[n]
                transpose_hot(ns, 0, 0)
                spread(ns, 0, 0)
                turns(pe, lambda i, s: next_spread(ns, i, s))

                reached(pe, ns.logit_ready, NG)
                for q in range(QUARTERS):
                    for h in range(GHEADS):
                        at = (q * GHEADS + h) * P
                        last = tr(psA[0][0:ROWS, at:at + P], logits[:, q * ROWS:(q + 1) * ROWS, h], ident[:, :])
                last.then_inc(sm.rowwise.sem, 1)
                reached(pe, sm.scanned, 1)
                for q in range(QUARTERS):
                    tr(psT[0][0:GHEADS, q * ROWS:(q + 1) * ROWS], best_f[:, q, :, P - 1], ident[0:ROWS, 0:ROWS])
                    last = tr(psT[1][0:GHEADS, q * ROWS:(q + 1) * ROWS], best_b[:, q, :, 0], ident[0:ROWS, 0:ROWS])
                last.then_inc(sm.ends_up.sem, 1)
                reached(pe, sm.carried, 1)
                for q in range(QUARTERS):
                    at = q * ROWS
                    tr(psQ[0][0:ROWS, q * GHEADS:(q + 1) * GHEADS], carry_f[:, at:at + ROWS], ident[0:2, 0:2])
                    last = tr(psQ[1][0:ROWS, q * GHEADS:(q + 1) * GHEADS], carry_b[:, at + 1:at + 1 + ROWS], ident[0:2, 0:2])
                last.then_inc(sm.carries_down.sem, 1)
                reached(pe, sm.best, 1)
                for q in range(QUARTERS):
                    for h in range(GHEADS):
                        last = tr(psA[1][:, h * 512 + q * ROWS:h * 512 + (q + 1) * ROWS], best_f[:, q, h, :], ident[0:ROWS, 0:ROWS])
                last.then_inc(sm.best_up.sem, 1)
                reached(pe, sm.alpha_ready, 1)

                def mix_step(i, s):
                    g = SLOTS * i + s
                    reached(pe, mix.hot_ready, g + 1)
                    reached(pe, mix.msg_ready, g + 1)
                    scatter(mix, i, s, lambda s, k: msg[s % 2][:, k, :],
                            lambda par, k: alpha_g[par][:, k, :])
                turns(pe, mix_step)

            def add_row(dst, row):
                return mm(dst, ones[0:1, :], row, start=False, stop=True)

            def zchunk(c):
                return psA[c % 2][:, 0:512].rearrange("p (b f) -> p b f", f=D)

            def residual(ns, product):
                for c, (b0, nb) in enumerate(CHUNKS):
                    if c >= 2:
                        reached(pe, ns.norm_ready, c - 1)
                    for j in range(nb):
                        z = zchunk(c)[:, j, :]
                        mm(z, ident[:, :], xN[:, b0 + j, :], start=True, stop=False)
                        last = product(z, b0 + j)
                    last.then_inc(ns.z_ready.sem, 1)

            def transposed(ns, ready, src):
                for c, (b0, nb) in enumerate(CHUNKS):
                    reached(pe, ready, c + 1)
                    if c >= 2:
                        reached(pe, ns.copied, c - 1)
                    for j in range(nb):
                        last = tr(psT[c % 2][:, j * P:(j + 1) * P], src[:, b0 + j, :], ident[:, :])
                    last.then_inc(ns.in_psum.sem, 1)

            def tables(t, ready):
                ns, (w, outs, bias) = n_tb[t], TABLES[t]
                width = 3 * D if w in Wkvq else 2 * D
                for c, (b0, nb) in enumerate(CHUNKS):
                    ready(c)
                    for b in range(b0, b0 + nb):
                        if b >= 2:
                            reached(pe, ns.copied, b - 1)
                        last = mm(psQ[b % 2][:, 0:width], xT[:, b * P:(b + 1) * P], w[:, 0:width], start=True, stop=bias is None)
                        if bias is not None:
                            last = add_row(psQ[b % 2][:, 0:width], bias[0:1, 0:width])
                        last.then_inc(ns.product_ready.sem, 1)

            def divide_by_sums(n, heads, sel, added, acc_count):
                ns = n_nm[n]
                reached(pe, added, acc_count)
                for b in range(NB):
                    last = mm(psT[0][:, b * heads:(b + 1) * heads], acc[:, 1, b * P:(b + 1) * P], sel[:, :], start=True, stop=True)
                last.then_inc(ns.den_ready.sem, 1)
                for c, (b0, nb) in enumerate(CHUNKS):
                    reached(pe, ns.along, c + 1)
                    if c >= 2:
                        reached(pe, ns.scaled, c - 1)
                    for j in range(nb):
                        b = b0 + j
                        last = mm(psQ[c % 2][:, j * P:(j + 1) * P], nA[:, b, :], ident[:, :], start=True, stop=True)
                    last.then_inc(ns.spread_ready.sem, 1)

            def project(w, bias):
                def product(z, b):
                    mm(z, acc[:, 0, b * P:(b + 1) * P], w[:, :], start=False, stop=False)
                    return add_row(z, bias[0:1, :])
                return product

            def pair_total(n):
                reached(pe, n_pr[n].squared, 1)
                mm(psT[1][:, 0:1], ones[:, :], pair[:, 2:3], start=True, stop=True).then_inc(n_pr[n].total.sem, 1)

            def by_copied(ns):
                return lambda c: reached(pe, ns.copied, c + 1)

            pe.wait_ge(s_colsv, 2)
            turns(pe, count)
            pe.wait_ge(s_total, 1)
            total = before[:, :, TILES]
            mm(psQ[0][:, 0:HI], later[:, :], total, start=True, stop=True)
            mm(psQ[1][:, 0:HI], ones[:, :], total, start=True, stop=True).then_inc(s_base, 1)
            pe.wait_ge(s_base, 2)
            turns(pe, send_transposes)
            sum_pass()
            pe.wait_ge(s_wts, 16 * len(weight_loads))
            pe.wait_ge(s_x, 32)
            reached(pe, a_sum.acc_written, TILES)
            residual(n_ln[0], project(W0, row_b0))
            transposed(n_tr[0], n_ln[0].norm_ready, xN)
            tables(0, by_copied(n_tr[0]))
            attention(0)
            divide_by_sums(0, HEADS, sel8, a_att[0].acc_written, TILES)
            reached(pe, n_nm[0].scaled, len(CHUNKS))
            residual(n_ln[1], project(Wo[0], row_bo[0]))
            transposed(n_tr[1], n_ln[1].norm_ready, nA)
            for c, (b0, nb) in enumerate(CHUNKS):
                cols = slice(b0 * P, (b0 + nb) * P)
                reached(pe, n_tr[1].copied, c + 1)
                if c >= 1:
                    reached(pe, n_ff.up_copied, c)
                for k in range(2):
                    last = mm(psQ[k][:, 0:nb * P], W1[:, k * D:(k + 1) * D], xT[:, cols], start=True, stop=True)
                last.then_inc(n_ff.up_ready.sem, 1)
                reached(pe, n_ff.up_copied, c + 1)
                if c >= 2:
                    reached(pe, n_ff.scaled, c - 1)
                for j in range(nb):
                    z = zchunk(c)[:, j, :]
                    mm(z, xT[:, (b0 + j) * P:(b0 + j + 1) * P], ident[:, :], start=True, stop=False)
                    for k in range(2):
                        mm(z, ffT[c % 2][:, k, j * P:(j + 1) * P], W2[:, k, :], start=False, stop=False)
                    last = add_row(z, row_c2[0:1, :])
                last.then_inc(n_ff.z_ready.sem, 1)
            transposed(n_tr[2], n_ff.norm_ready, xN)
            tables(1, by_copied(n_tr[2]))
            gat(0)
            divide_by_sums(1, GHEADS, sel2, a_mix[0].acc_written, TILES)
            pair_total(0)
            tables(2, lambda c: reached(pe, n_pr[0].x_ready, 1))
            gat(1)
            divide_by_sums(2, GHEADS, sel2, a_mix[1].acc_written, TILES)
            pair_total(1)
            reached(pe, n_pr[1].x_ready, 1)
            residual(n_ln[2], lambda z, b: mm(z, xT[:, b * P:(b + 1) * P], ident[:, :], start=False, stop=True))
            transposed(n_tr[3], n_ln[2].norm_ready, xN)
            tables(3, by_copied(n_tr[3]))
            attention(1)
            divide_by_sums(3, HEADS, sel8, a_att[1].acc_written, TILES)
            reached(pe, n_nm[3].scaled, len(CHUNKS))
            residual(n_ln[3], project(Wo[1], row_bo[1]))


ARGS = ["x", "src", "dst", "edge_weight", "L0_gnn_W", "L0_gnn_b", "L1_gnn_Wq", "L1_gnn_Wk", "L1_gnn_Wv", "L1_gnn_Wo",
        "L1_gnn_bo", "L1_gnn_g1", "L1_gnn_b1", "L1_gnn_g2", "L1_gnn_b2", "L1_gnn_W1", "L1_gnn_c1", "L1_gnn_W2",
        "L1_gnn_c2", "L2_gnn_Wl", "L2_gnn_Wr", "L2_gnn_att", "L2_gnn_bias", "L3_gnn_Wq", "L3_gnn_bq", "L3_gnn_Wk",
        "L3_gnn_bk", "L3_gnn_Wv", "L3_gnn_bv", "L3_gnn_Wo", "L3_gnn_bo"]
TRANSPOSED = ["L3_gnn_Wq", "L3_gnn_Wk", "L3_gnn_Wv", "L3_gnn_Wo"]


def kernel(**inputs):
    import numpy as _np
    import concourse.bacc as _bacc
    from concourse import mybir as _mybir
    from concourse.bass_utils import run_bass_kernel_spmd as _run

    nc = _bacc.Bacc("TRN2", target_bir_lowering=False, num_devices=1)
    arrays, args = {}, {}
    for name in ARGS:
        v = _np.asarray(inputs[name])
        if name in TRANSPOSED:
            v = v.T
        if name == "src":
            v = _np.concatenate([v, _np.full(EPAD - E, HI * P - 1, v.dtype)])
        if name == "edge_weight":
            v = _np.concatenate([v, _np.zeros(EPAD - E, v.dtype)])
        if name == "dst":
            v = _np.concatenate([_np.full(1, -1, v.dtype), v, _np.full(EPAD - E, FAR, v.dtype), _np.full(1, -2, v.dtype)])
        v = _np.ascontiguousarray(v)
        arrays[f"in_{name}"] = v
        args[name] = nc.dram_tensor(f"in_{name}", v.shape, _mybir.dt.from_np(v.dtype), kind="ExternalInput").ap()
    out = nc.dram_tensor("out_0", (N, D), _mybir.dt.float32, kind="ExternalOutput").ap()
    gnn_program(nc, args, out)
    r = _run(nc, [arrays], core_ids=[0])
    return r.results[0]["out_0"]
```

```python
import concourse.bass as bass
from concourse import mybir
from contextlib import ExitStack
from collections import namedtuple

F32 = mybir.dt.float32
I32 = mybir.dt.int32
BF16 = mybir.dt.bfloat16
ALU = mybir.AluOpType
ACT = mybir.ActivationFunctionType
AX = mybir.AxisListType

P = 128
N = 3125
E = 53125
D = 128
TILES = -(-E // P)
G = 4
NG = TILES // G
SLOTS = 4
TURNS = NG // SLOTS
LONG = 2 * SLOTS
EPAD = TILES * P
ROWS = 104
QUARTERS = TILES // ROWS
NB = -(-N // P) + 1
NPAD = NB * P
FULLB = N // P
TAILR = N - FULLB * P
CHUNKS = [(b, min(4, NB - b)) for b in range(0, NB, 4)]
HEADS = 8
DH = D // HEADS
GHEADS = 2
GC = D // GHEADS
BIG = 1e30
LN_EPS = 1e-5
FAR = 1 << 20
HI = -(-N // P)
SENT = D + 4


def gnn_program(nc, a, out):
    ctx = ExitStack()
    with ctx:
        def sb(name, shape, dt=F32):
            return ctx.enter_context(nc.sbuf_tensor(name, shape, dt))

        def ps(name, shape):
            return ctx.enter_context(nc.psum_tensor(name, shape, F32))

        def sem(name):
            return ctx.enter_context(nc.semaphore(name))

        def dram(name, shape):
            return nc.dram_tensor(name, shape, F32, kind="Internal").ap()

        kv_table = [dram(f"kv_table{i}", (NPAD, 2 * D)) for i in range(2)]
        q_table = [dram(f"q_table{i}", (NPAD, D)) for i in range(2)]
        xs_table = [dram(f"xs_table{i}", (NPAD, D)) for i in range(2)]
        xd_table = [dram(f"xd_table{i}", (NPAD, D)) for i in range(2)]
        x_table = dram("x_table", (NPAD, D))
        sorted_msgs = dram("sorted_msgs", (EPAD, SENT))
        edge_rows = [dram(f"edge_rows{i}", (NG, P, G * D)) for i in range(2)]

        rowspace = sb("rowspace", [P, 3 * GHEADS * QUARTERS * P])
        rows_f = rowspace[0:ROWS, 0:5 * QUARTERS * P].rearrange("r (n q p) -> r n q p", n=5, q=QUARTERS)
        src_idx = sb("src_idx", [P, TILES], I32)
        dst_rel = sb("dst_rel", [P, TILES])
        weight = sb("weight", [P, TILES])
        src_f = sb("src_f", [P, TILES])
        softbuf = sb("softbuf", [P, 2 * TILES * GHEADS])
        src_low = softbuf[:, 0:TILES]
        src_high = softbuf[:, TILES:2 * TILES]
        first_src_bc = softbuf[:, 2 * TILES:3 * TILES]
        part_i = softbuf[:, 3 * TILES:4 * TILES].bitcast(I32)
        first_src = sb("first_src", [1, TILES], I32)
        first_src_f = sb("first_src_f", [1, TILES])
        copies = sb("copies", [ROWS, QUARTERS, P])
        first_i = sb("first_i", [1, TILES], I32)
        first_dst = sb("first_dst", [1, TILES], I32)
        first_f = sb("first_f", [1, TILES])
        endbuf = sb("endbuf", [2, 4 * TILES])
        ends_i = endbuf[:, :].bitcast(I32).rearrange("h (n t) -> h n t", n=4)
        ends_f = sb("ends_f", [2, 4, TILES])
        scan_fwd = sb("scan_fwd", [ROWS, QUARTERS, GHEADS, P])
        scan_bwd = sb("scan_bwd", [ROWS, QUARTERS, GHEADS, P])
        open_fwd = sb("open_fwd", [ROWS, QUARTERS, P])
        open_bwd = sb("open_bwd", [ROWS, QUARTERS, P])
        pass_fwd = sb("pass_fwd", [2, TILES])
        pass_bwd = sb("pass_bwd", [2, TILES])
        whole_fwd, whole_bwd = ends_f[:, 0, :], ends_f[:, 3, :]

        ident = sb("ident", [P, P])
        iota = sb("iota", [P, P])
        iota_i = sb("iota_i", [P, P], I32)
        ones = sb("ones", [P, P])
        sel8 = sb("sel8", [P, HEADS])
        eps = sb("eps", [P, 1])
        earlier = sb("earlier", [P, P])
        later = sb("later", [P, P])

        W0 = sb("W0", [P, D])
        Wkvq = [sb(f"Wkvq{i}", [P, 3 * D]) for i in range(2)]
        Wo = [sb(f"Wo{i}", [P, D]) for i in range(2)]
        W1 = sb("W1", [P, 2 * D])
        W2 = sb("W2", [P, 2, D])
        Wsd = [sb(f"Wsd{i}", [P, 2 * D]) for i in range(2)]
        att = [sb(f"att{i}", [P, D]) for i in range(2)]
        row_b0 = sb("row_b0", [1, D])
        row_bo = [sb(f"row_bo{i}", [1, D]) for i in range(2)]
        row_c2 = sb("row_c2", [1, D])
        row_kvq = sb("row_kvq", [1, 3 * D])
        col_g1 = sb("col_g1", [P, 1])
        col_b1 = sb("col_b1", [P, 1])
        col_c1 = sb("col_c1", [P, 2])
        col_gat = sb("col_gat", [P, 2])
        bc_g2 = sb("bc_g2", [P, D])
        bc_b2 = sb("bc_b2", [P, D])

        xN = sb("xN", [P, NB, D])
        nodebuf = sb("nodebuf", [P, 4 * NPAD])
        acc = nodebuf[:, 0:2 * NPAD].rearrange("p (w n) -> p w n", w=2)
        parts = nodebuf[:, :].rearrange("p (w n) -> p w n", w=G)
        xT = nodebuf[:, 2 * NPAD:3 * NPAD]
        nA = nodebuf[:, 3 * NPAD:4 * NPAD].rearrange("p (b f) -> p b f", f=D)
        rows_i = nA[0:ROWS, 4:4 + 4 * QUARTERS, :].bitcast(I32).rearrange("r (n q) p -> r n q p", n=4)
        sources = [nodebuf[:, 11264 + k * G * P:11264 + (k + 1) * G * P].bitcast(I32) for k in range(SLOTS)]
        before = nodebuf[:, 0:HI * (TILES + 1)].rearrange("p (h t) -> p h t", h=HI)
        stats = [sb(f"stats{i}", [P, 4, 6]) for i in range(2)]
        mv = [sb(f"mv{i}", [P, 4, 2]) for i in range(2)]
        std = [sb(f"std{i}", [P, 4]) for i in range(2)]
        rstd = [sb(f"rstd{i}", [P, 4]) for i in range(2)]
        shift = [sb(f"shift{i}", [P, 4]) for i in range(2)]
        den = sb("den", [P, NB * HEADS])
        rden = sb("rden", [P, NB * HEADS])
        pair = sb("pair", [P, 8])

        idx = [sb(f"idx{s}", [P, G], I32) for s in range(SLOTS)]
        rowbuf = sb("rowbuf", [P, SLOTS * G * 2 * D])
        rows = [rowbuf[:, s * G * 2 * D:(s + 1) * G * 2 * D] for s in range(SLOTS)]
        winbuf = sb("winbuf", [P, SLOTS, G * D])
        window = [winbuf[:, s, :].rearrange("p (k f) -> p k f", k=G) for s in range(SLOTS)]
        message_rows = [winbuf[:, :, :].rearrange("p s f -> p (s f)")[:, 0:G * SENT]] + [
            rowbuf[:, j * G * SENT:(j + 1) * G * SENT] for j in range(7)]
        stage = [rowbuf[:, i * 12 * D:(i + 1) * 12 * D].rearrange("p (b w) -> p b w", b=4) for i in range(2)]
        ffT = [winbuf[:, 2 * i:2 * i + 2, :] for i in range(2)]
        hot = [sb(f"hot{s}", [P, G, P]) for s in range(SLOTS)]
        hotT = [sb(f"hotT{i}", [P, G, P]) for i in range(2)]
        prod = [sb(f"prod{i}", [P, G, D]) for i in range(2)]
        leaky = [sb(f"leaky{i}", [P, G, D]) for i in range(2)]
        raw = [sb(f"raw{i}", [P, G, HEADS]) for i in range(2)]
        clipped = [sb(f"clipped{i}", [P, G, HEADS]) for i in range(2)]
        score = [sb(f"score{i}", [P, G, D]) for i in range(2)]
        msg = [sb(f"msg{i}", [P, G, D]) for i in range(2)]
        low_hot, low_hotT, low_hot_b = prod, leaky, msg
        hot_b = [hot[s][:, 0:G // 2, :].rearrange("p k n -> p (k n)").bitcast(BF16).rearrange("p (k n) -> p k n", k=G)
                 for s in range(SLOTS)]
        high_hot = [sb(f"high_hot{i}", [P, G, HI]) for i in range(4)]
        high_b = [sb(f"high_b{i}", [P, G, HI], BF16) for i in range(SLOTS)]
        prior_h = [sb(f"prior_h{i}", [P, G, HI]) for i in range(2)]
        prior = [sb(f"prior{i}", [P, G]) for i in range(2)]
        within = [sb(f"within{i}", [P, G]) for i in range(2)]
        place = [sb(f"place{s}", [P, G], I32) for s in range(SLOTS)]
        base = sb("base", [P, HI])
        high_sum = sb("high_sum", [P, HI + 1])
        matched = score
        msg_rel = [sb(f"msg_rel{i}", [P, G]) for i in range(SLOTS)]

        logits = softbuf[:, 0:GHEADS * TILES].rearrange("p (t h) -> p t h", h=GHEADS)
        alpha = softbuf[:, GHEADS * TILES:].rearrange("p (t h) -> p t h", h=GHEADS)
        best_f, best_b, held = [
            rowspace[0:ROWS, i * 1024:(i + 1) * 1024].rearrange("r (q h p) -> r q h p", q=QUARTERS, h=GHEADS)
            for i in range(3)]
        carry_f = endbuf[:, 0:TILES + 1]
        carry_b = endbuf[:, 2 * TILES:3 * TILES + 1]

        psT = [ps(f"psT{i}", [P, 512]) for i in range(2)]
        psQ = [ps(f"psQ{i}", [P, 512]) for i in range(2)]
        psA = [ps(f"psA{i}", [P, 1024]) for i in range(2)]
        psS = [psA[i][:, :].rearrange("p (k w n) -> p k w n", k=G, w=2) for i in range(2)]

        s_meta = sem("meta_landed")
        s_x = sem("x_landed")
        s_wts = sem("weights_landed")
        s_pool = sem("pool_made")
        s_tofloat = sem("tofloat")
        s_cols = sem("cols_in_psum")
        s_colsv = sem("cols_copied")
        s_out = sem("out_stored")

        class Count:

            def __init__(self, sem, base):
                self.sem, self.base = sem, base

        def counted(name, totals):
            handle = sem(name)
            return [Count(handle, sum(totals[:u])) for u in range(len(totals))]

        def shared(prefix, uses):
            spaces = [{} for _ in uses]
            for name in dict.fromkeys(n for use in uses for n in use):
                totals = [use.get(name, 0) for use in uses]
                width = max(len(t) if isinstance(t, list) else 0 for t in totals)
                if width:
                    per_slot = [counted(f"{prefix}_{name}{k}", [t[k] if t and k < len(t) else 0 for t in totals]) for k in range(width)]
                for u, space in enumerate(spaces):
                    if width:
                        space[name] = [slot[u] for slot in per_slot]
                if not width:
                    for space, count in zip(spaces, counted(f"{prefix}_{name}", totals)):
                        space[name] = count
            return [namedtuple("Use", space)(**space) for space in spaces]

        def turns(eng, step):
            for s in range(SLOTS):
                step(0, s)
            with eng.Fori(1, TURNS - 1) as i:
                for s in range(SLOTS):
                    step(i, s)
            for s in range(SLOTS):
                step(TURNS - 1, s)

        def long_turns(eng, step):
            def turn(n):
                for j in range(LONG):
                    step(2 * n + j // SLOTS, j % SLOTS, n, j)
            turn(0)
            with eng.Fori(1, NG // LONG - 1) as n:
                turn(n)
            turn(NG // LONG - 1)

        def ahead(i, s, n):
            j, t = divmod(s + n, SLOTS)
            if isinstance(i, int) and i + j >= TURNS:
                return None
            return i + j, t

        def behind(i, s):
            if s > 0:
                return i, s - 1
            if isinstance(i, int) and i == 0:
                return None
            return i - 1, SLOTS - 1

        def reached(eng, count, n):
            if isinstance(n, int) and n <= 0:
                return
            eng.wait_ge(count.sem, count.base + n)

        s_chain = sem("dve_chain")
        s_xtable = sem("x_table_stored")
        s_first = sem("first_src_landed")
        s_total = sem("totals_in_psum")
        s_base = sem("base_ready")

        SP, DVE = mybir.EngineType.SP, mybir.EngineType.DVE

        def load_firsts(engine, g, first=None):
            _, values = nc.values_load_multi_w_load_instructions(
                (first_dst if first is None else first)[0:1, bass.ds(G * g, G)], engines=[engine], min_val=0, max_val=NPAD - P,
                skip_runtime_bounds_check_because="the program caps them at NPAD - P, and node numbers are not negative")
            return values

        def row(name):
            return a[name].rearrange("(o f) -> o f", o=1)

        def col(name):
            return a[name].rearrange("(f o) -> f o", o=1)

        weight_loads = [
            (W0[:, :], a["L0_gnn_W"]),
            (Wkvq[0][:, 0:D], a["L1_gnn_Wk"]), (Wkvq[0][:, D:2 * D], a["L1_gnn_Wv"]), (Wkvq[0][:, 2 * D:], a["L1_gnn_Wq"]),
            (Wkvq[1][:, 0:D], a["L3_gnn_Wk"]), (Wkvq[1][:, D:2 * D], a["L3_gnn_Wv"]), (Wkvq[1][:, 2 * D:], a["L3_gnn_Wq"]),
            (Wo[0][:, :], a["L1_gnn_Wo"]), (Wo[1][:, :], a["L3_gnn_Wo"]),
            (W1[:, :], a["L1_gnn_W1"]), (W2[:, :, :], a["L1_gnn_W2"].rearrange("(k p) f -> p k f", p=P)),
            (row_b0[:, :], row("L0_gnn_b")), (row_bo[0][:, :], row("L1_gnn_bo")), (row_bo[1][:, :], row("L3_gnn_bo")),
            (row_c2[:, :], row("L1_gnn_c2")),
            (row_kvq[:, 0:D], row("L3_gnn_bk")), (row_kvq[:, D:2 * D], row("L3_gnn_bv")), (row_kvq[:, 2 * D:], row("L3_gnn_bq")),
            (col_g1[:, :], col("L1_gnn_g1")), (col_b1[:, :], col("L1_gnn_b1")),
            (col_c1[:, :], a["L1_gnn_c1"].rearrange("(k p) -> p k", p=P)),
            (col_gat[:, :], a["L2_gnn_bias"].rearrange("l f -> f l")),
            (bc_g2[:, :], row("L1_gnn_g2").to_broadcast([P, D])), (bc_b2[:, :], row("L1_gnn_b2").to_broadcast([P, D])),
        ]
        for l in range(2):
            weight_loads += [
                (Wsd[l][:, 0:D], a["L2_gnn_Wl"][l]), (Wsd[l][:, D:], a["L2_gnn_Wr"][l]),
                (att[l][:, :], a["L2_gnn_att"][l:l + 1].rearrange("o h c -> o (h c)").to_broadcast([P, D])),
            ]


        def per_group(names):
            return {n: NG for n in names.split()}

        GATHERED = dict(slot_open=NG, idx_open=NG, idx_landed=[16 * TURNS] * SLOTS, rows_landed=[16 * G * TURNS] * SLOTS)
        SPREAD = dict(window_landed=[16 * G * TURNS] * SLOTS, **per_group("hotT_psum hotT_ready spread_ready"))
        SUMMED = dict(acc_written=TILES, **per_group("hot_ready sums_ready"))
        ATT = {**GATHERED, **SPREAD, **SUMMED, **per_group("squared spread_used raw_ready clip_ready score_ready msg_ready")}
        GAT = {**GATHERED, **SPREAD, **per_group("spread_used hot_ready leaky_ready weighted logit_ready"), "spilled": [16 * TURNS] * SLOTS}
        MIX = {**SUMMED, **per_group("squared last_hot_ready msg_ready"), "folded": 2, "rows_loaded": [16 * TURNS] * SLOTS}
        COUNT = per_group("hot_ready counted before_ready")
        SEND = {**SPREAD, **per_group("hot_ready low_ready low_used low_psum lowT_ready prior_psum slot_open "
                                      "prior_ready within_ready prior_used place_ready scaled"),
                "rows_sent": [16 * G * TURNS] * SLOTS, "sources_landed": [16 * TURNS] * SLOTS}
        SUM = {**SUMMED, **per_group("rel_ready squared last_hot_ready"), "folded": 2, "rows_loaded": [16 * NG // LONG] * LONG}
        a_count, a_send, a_sum, att0, gat0, mix0, gat1, mix1, att1 = shared("edge", [COUNT, SEND, SUM, ATT, GAT, MIX, GAT, MIX, ATT])
        a_att, a_gat, a_mix = [att0, att1], [gat0, gat1], [mix0, mix1]
        NCH = len(CHUNKS)

        def per_chunk(names):
            return {n: NCH for n in names.split()}

        LN = per_chunk("z_ready stats_ready var_ready std_ready rstd_ready coef_ready norm_ready")
        n_ln = shared("ln", [LN] * 4)
        n_tr = shared("tr", [per_chunk("in_psum copied")] * 4)
        n_ff, = shared("ff", [{**LN, **per_chunk("up_ready up_copied scaled xb_ready v_ready stats3_ready var3_ready "
                                                 "std3_ready rstd3_ready coef3_ready")}])
        STORED = [32 * len(CHUNKS[c::2]) for c in range(2)]
        n_tb = shared("tb", [dict(product_ready=NB, copied=NB, stored=STORED)] * 4)
        n_nm = shared("nm", [dict(den_ready=1, den_copied=1, rden_ready=1, **per_chunk("along spread_ready scaled"))] * 2)
        n_sm = shared("sm", [dict.fromkeys("rowwise scanned ends_up carried carries_down shifted exp_ready sums_scanned "
                                           "sum_ends_up sums_carried sums_down alpha_rows alpha_up alpha_ready".split(), 1)] * 2)
        n_pr = shared("pr", [dict.fromkeys("mean squared total std ready x_ready".split(), 1)] * 2)
        s_zeroed = sem("acc_zeroed")

        ctx.enter_context(nc.allow_non_contiguous_dma(reason="small loads at the start: tile ends, per-feature columns"))
        block = ctx.enter_context(nc.Block())

        TABLES = [
            (Wkvq[0], [(kv_table[0], 0, 2 * D), (q_table[0], 2 * D, 3 * D)], None),
            (Wsd[0], [(xs_table[0], 0, D), (xd_table[0], D, 2 * D)], None),
            (Wsd[1], [(xs_table[1], 0, D), (xd_table[1], D, 2 * D)], None),
            (Wkvq[1], [(kv_table[1], 0, 2 * D), (q_table[1], 2 * D, 3 * D)], row_kvq),
        ]
        def tables_in_dram(eng, t):
            for c in range(2):
                reached(eng, n_tb[t].stored[c], STORED[c])

        @block.sync
        def _(sp):
            for n, at in ((0, 1), (1, 0), (2, 2)):
                sp.dma_start(rows_i[:, n], a["dst"][at:at + EPAD].rearrange("(q r p) -> r q p", q=QUARTERS, r=ROWS)).then_inc(s_meta, 16)
            sp.dma_start(rows_i[:, 3], a["src"].rearrange("(q r p) -> r q p", q=QUARTERS, r=ROWS)).then_inc(s_meta, 16)
            sp.dma_start(rows_f[:, 4], a["edge_weight"].rearrange("(q r p) -> r q p", q=QUARTERS, r=ROWS)).then_inc(s_meta, 16)
            sp.dma_start(first_i[0:1, :], a["dst"][1:1 + P * (TILES - 1) + 1:P].rearrange("(o t) -> o t", o=1)).then_inc(s_meta, 16)
            for h in range(GHEADS):
                for j, at in enumerate((0, 1, P, P + 1)):
                    sp.dma_start(ends_i[h:h + 1, j, :],
                                 a["dst"][at:at + P * (TILES - 1) + 1:P].rearrange("(o t) -> o t", o=1)).then_inc(s_meta, 16)
            sp.dma_start(xN[:, 0:FULLB, :], a["x"][0:FULLB * P, :].rearrange("(b p) f -> p b f", p=P)).then_inc(s_x, 16)
            sp.wait_ge(s_pool, 1)
            sp.dma_start(xN[0:TAILR, FULLB, :], a["x"][FULLB * P:N, :]).then_inc(s_x, 16)
            for dst, src in weight_loads:
                sp.dma_start(dst, src).then_inc(s_wts, 16)

            def fetch_idx(ns, i, s):
                g = SLOTS * i + s
                reached(sp, ns.rows_landed[s], 16 * G * i)
                sp.sem_inc(ns.idx_open.sem, 1)
                sp.dma_start(idx[s][:, :], src_idx[:, bass.ds(G * g, G)]).then_inc(ns.idx_landed[s].sem, 16)

            def fetch_window(ns, table, i, s):
                g = SLOTS * i + s
                firsts = load_firsts(SP, g)
                reached(sp, ns.spread_ready, g - SLOTS + 1)
                for k in range(G):
                    sp.dma_start(window[s][:, k, :], table[bass.ds(firsts[k], P), :]).then_inc(ns.window_landed[s].sem, 16)

            def store_tables(t):
                for c, (b0, nb) in enumerate(CHUNKS):
                    reached(sp, n_tb[t].copied, b0 + nb)
                    for table, lo, hi in TABLES[t][1]:
                        sp.dma_start(table[b0 * P:(b0 + nb) * P, :].rearrange("(b p) f -> p b f", p=P),
                                     stage[c % 2][:, 0:nb, lo:hi]).then_inc(n_tb[t].stored[c % 2].sem, 16)

            sp.wait_ge(s_x, 32)
            sp.dma_start(x_table.rearrange("(b p) f -> p b f", p=P), xN[:, :, :]).then_inc(s_xtable, 16)
            sp.wait_ge(s_xtable, 16)
            sp.wait_ge(s_colsv, 1)

            def fetch_sources(i, s):
                g = SLOTS * i + s
                reached(sp, a_send.prior_used, g - SLOTS + 1)
                sp.dma_start(sources[s], a["src"][bass.ds(g * (G * P), G * P)].rearrange("(o e) -> o e", o=1)
                             .to_broadcast([P, G * P])).then_inc(a_send.sources_landed[s].sem, 16)
                fetch_window(a_send, x_table, i, s)
            turns(sp, fetch_sources)
            for s in range(SLOTS):
                reached(sp, a_send.rows_sent[s], 16 * G * TURNS)
            sp.dma_start(first_src_f[0:1, :], sorted_msgs.rearrange("(t p) w -> t p w", p=P)[:, 0, D]
                         .rearrange("(o t) -> o t", o=1)).then_inc(s_first, 16)

            def fetch_messages(i, s, n, j):
                g = SLOTS * i + s
                reached(sp, a_sum.sums_ready, g - LONG + 1)
                sp.dma_start(message_rows[j].rearrange("p (k w) -> p k w", k=G),
                             sorted_msgs[bass.ds(g * (G * P), G * P), :].rearrange("(k p) w -> p k w", p=P)
                             ).then_inc(a_sum.rows_loaded[j].sem, 16)
            long_turns(sp, fetch_messages)

            def attention(n, t):
                ns = a_att[n]
                store_tables(t)
                tables_in_dram(sp, t)

                def step(i, s):
                    fetch_idx(ns, i, s)
                    fetch_window(ns, q_table[n], i, s)
                turns(sp, step)

            def gat(n, t):
                ns, mix = a_gat[n], a_mix[n]
                store_tables(t)
                tables_in_dram(sp, t)

                def step(i, s):
                    fetch_idx(ns, i, s)
                    fetch_window(ns, xd_table[n], i, s)
                    if s >= 2:
                        spill_rows(i, s - 2)
                    elif not (isinstance(i, int) and i == 0):
                        spill_rows(i - 1, s + 2)

                def spill_rows(i, s):
                    g = SLOTS * i + s
                    reached(sp, ns.rows_landed[s], 16 * G * (i + 1))
                    sp.dma_start(edge_rows[n][bass.ds(g, 1)].rearrange("o p f -> (o p) f"),
                                 rows[s][:, 0:G * D]).then_inc(ns.spilled[s].sem, 16)
                turns(sp, step)
                spill_rows(TURNS - 1, 2)
                spill_rows(TURNS - 1, 3)
                for s in range(SLOTS):
                    reached(sp, ns.spilled[s], 16 * TURNS)
                reached(sp, ns.spread_used, NG)

                def refetch(i, s):
                    g = SLOTS * i + s
                    reached(sp, mix.msg_ready, g - SLOTS + 1)
                    sp.dma_start(rows[s][:, 0:G * D],
                                 edge_rows[n][bass.ds(g, 1)].rearrange("o p f -> (o p) f")).then_inc(mix.rows_loaded[s].sem, 16)
                turns(sp, refetch)

            attention(0, 0)
            gat(0, 1)
            gat(1, 2)
            attention(1, 3)
            for c, (b0, nb) in enumerate(CHUNKS):
                reached(sp, n_ln[3].norm_ready, c + 1)
                full = min(b0 + nb, FULLB) - b0
                if full > 0:
                    sp.dma_start(out[b0 * P:(b0 + full) * P, :].rearrange("(b p) f -> p b f", p=P),
                                 xN[:, b0:b0 + full, :]).then_inc(s_out, 16)
                if b0 <= FULLB < b0 + nb:
                    sp.dma_start(out[FULLB * P:N, :], xN[0:TAILR, FULLB, :]).then_inc(s_out, 16)
            sp.wait_ge(s_out, 16 * 7)

        @block.gpsimd
        def _(pool):
            nc.gpsimd.memset(xN[:, FULLB:NB, :], 0.0).then_inc(s_pool, 1)
            nc.gpsimd.memset(ident[:, :], 0.0)
            nc.gpsimd.memset(ones[:, :], 1.0)
            nc.gpsimd.memset(sel8[:, :], 0.0)
            nc.gpsimd.memset(earlier[:, :], 1.0)
            nc.gpsimd.memset(later[:, :], 1.0)
            nc.gpsimd.memset(rowbuf[:, :], 0.0)
            nc.gpsimd.memset(before[:, :, 0:1], 0.0)
            nc.gpsimd.iota(iota_i[:, :], pattern=[[1, P]], base=0, channel_multiplier=0)
            nc.gpsimd.memset(eps[:, :], LN_EPS).then_inc(s_pool, 1)
            pool.wait_ge(s_pool, 2)
            nc.gpsimd.tensor_copy(iota[:, :], iota_i[:, :])
            nc.gpsimd.affine_select(out=ident[:, :], in_=ident[:, :], compare_op=ALU.not_equal, fill=1.0,
                                    base=0, pattern=[[-1, P]], channel_multiplier=1)
            nc.gpsimd.affine_select(out=earlier[:, :], in_=earlier[:, :], compare_op=ALU.is_gt, fill=0.0,
                                    base=0, pattern=[[-1, P]], channel_multiplier=1)
            nc.gpsimd.affine_select(out=later[:, :], in_=later[:, :], compare_op=ALU.is_gt, fill=0.0,
                                    base=0, pattern=[[1, P]], channel_multiplier=-1)
            nc.gpsimd.affine_select(out=sel8[:, :], in_=sel8[:, :], compare_op=ALU.not_equal, fill=1.0,
                                    base=0, pattern=[[-DH, HEADS]], channel_multiplier=1).then_inc(s_pool, 1)

            def gather(ns, table, width, i, s, free):
                g = SLOTS * i + s
                reached(pool, ns.idx_landed[s], 16 * (i + 1))
                for fs, n in free(i, s, g):
                    reached(pool, fs, n)
                pool.sem_inc(ns.slot_open.sem, 1)
                for k in range(G):
                    pool.indirect_dma_start(
                        out=rows[s][:, k * width:(k + 1) * width], out_offset=None, in_=table,
                        in_offset=bass.IndirectOffsetOnAxis(ap=idx[s][:, k:k + 1], axis=0)).then_inc(ns.rows_landed[s].sem, 16)

            def send(i, s):
                ns, g = a_send, SLOTS * i + s
                reached(pool, ns.place_ready, g + 1)
                reached(pool, ns.scaled, g + 1)
                pool.sem_inc(ns.slot_open.sem, 1)
                for k in range(G):
                    pool.indirect_dma_start(
                        out=sorted_msgs, out_offset=bass.IndirectOffsetOnAxis(ap=place[s][:, k:k + 1], axis=0),
                        in_=rows[s][:, k * SENT:(k + 1) * SENT], in_offset=None).then_inc(ns.rows_sent[s].sem, 16)
            turns(pool, send)
            nc.gpsimd.memset(parts[:, 0:2, :], 0.0).then_inc(s_zeroed, 1)
            for s in range(SLOTS):
                reached(pool, a_send.rows_sent[s], 16 * G * TURNS)
            pool.wait_ge(s_first, 19)

            def relative(i, s, n, j):
                ns, g = a_sum, SLOTS * i + s
                reached(pool, ns.squared, g - SLOTS + 1)
                reached(pool, ns.last_hot_ready, g - SLOTS + 1)
                reached(pool, ns.rows_loaded[j], 16 * (n + 1))
                nc.gpsimd.tensor_tensor(msg_rel[s][:, :], message_rows[j].rearrange("p (k w) -> p k w", k=G)[:, :, D],
                                        first_src_bc[:, bass.ds(G * g, G)], ALU.subtract).then_inc(ns.rel_ready.sem, 1)
            long_turns(pool, relative)

            def fold(ns):
                reached(pool, ns.acc_written, TILES)
                nc.gpsimd.tensor_tensor(parts[:, 1, :], parts[:, 1, :], parts[:, 3, :], ALU.add).then_inc(ns.folded.sem, 1)
            fold(a_sum)

            def attention(n, t):
                ns = a_att[n]
                tables_in_dram(pool, t)
                turns(pool, lambda i, s: gather(ns, kv_table[n][:, :], 2 * D, i, s,
                                                lambda i, s, g: [(ns.msg_ready, g - SLOTS + 1)]))

            def gat(n, t):
                ns, mix = a_gat[n], a_mix[n]
                tables_in_dram(pool, t)
                turns(pool, lambda i, s: gather(ns, xs_table[n][:, :], D, i, s,
                                                lambda i, s, g: [(ns.spread_used, g - SLOTS + 1), (ns.spilled[s], 16 * i)]))
                reached(pool, n_sm[n].alpha_ready, 1)

                def weigh(i, s):
                    g, par = SLOTS * i + s, s % 2
                    reached(pool, mix.sums_ready, g - 1)
                    reached(pool, mix.rows_loaded[s], 16 * (i + 1))
                    nc.gpsimd.tensor_tensor(
                        msg[par][:, :, :].rearrange("p k (h c) -> p (k h) c", c=GC),
                        rows[s][:, 0:G * D].rearrange("p (x c) -> p x c", c=GC),
                        alpha[:, bass.ds(G * g, G), :].rearrange("p k h -> p (k h)").unsqueeze(2).to_broadcast([P, G * GHEADS, GC]),
                        ALU.mult).then_inc(mix.msg_ready.sem, 1)
                turns(pool, weigh)
                fold(mix)

            def zero_acc(s, n):
                reached(pool, s, n)
                nc.gpsimd.memset(acc[:, :, :], 0.0).then_inc(s_zeroed, 1)

            zero_acc(n_ln[0].z_ready, len(CHUNKS))
            attention(0, 0)
            pool.wait_ge(s_wts, 16 * len(weight_loads))
            for c, (b0, nb) in enumerate(CHUNKS):
                if c == 0:
                    reached(pool, n_ln[1].z_ready, len(CHUNKS))
                nc.gpsimd.tensor_tensor(xN[:, b0:b0 + nb, :], xN[:, b0:b0 + nb, :],
                                        bc_b2[:, :].unsqueeze(1).to_broadcast([P, nb, D]), ALU.add).then_inc(n_ff.xb_ready.sem, 1)
            gat(0, 1)
            gat(1, 2)
            zero_acc(n_pr[1].x_ready, 1)
            attention(1, 3)

        @block.scalar
        def _(act):
            def squares(ns, rel, tiles, i, s):
                reached(act, ns.sums_ready, SLOTS * i + s - SLOTS + 1)
                if ns is a_sum:
                    reached(act, ns.rel_ready, SLOTS * i + s + 1)
                for k in range(tiles):
                    last = nc.scalar.activation(hot[s][:, k, :], iota[:, :], ACT.Square, bias=rel(i, s, k), scale=-1.0)
                last.then_inc(ns.squared.sem, 1)

            def hot_from_squares(ns, tiles, i, s):
                reached(act, ns.squared, SLOTS * i + s + 1)
                flat = hot[s][:, 0:tiles, :].rearrange("p k n -> p (k n)")
                nc.scalar.activation(flat, flat, ACT.Relu, bias=ones[:, 0:1], scale=-1.0).then_inc(ns.hot_ready.sem, 1)

            def hots(ns, rel):
                def step(i, s):
                    if ahead(i, s, 1):
                        squares(ns, rel, G - 1, *ahead(i, s, 1))
                    hot_from_squares(ns, G - 1, i, s)
                squares(ns, rel, G - 1, 0, 0)
                turns(act, step)

            def zero_parts(first):
                nc.scalar.activation(nodebuf[:, first * NPAD:], ones[:, 0:1].to_broadcast([P, (G - first) * NPAD]), ACT.Copy,
                                     scale=0.0).then_inc(s_zeroed, 1)

            def src_rel(i, s, k):
                return msg_rel[s][:, k:k + 1]

            def dst_rel_of(i, s, k):
                return dst_rel[:, bass.ds(G * (SLOTS * i + s) + k, 1)]

            def copy_hotT(ns, i, s):
                g, par = SLOTS * i + s, s % 2
                reached(act, ns.hotT_psum, g + 1)
                reached(act, ns.spread_ready, g - 1)
                nc.scalar.copy(hotT[par][:, :, :].rearrange("p k n -> p (k n)"), psT[par][:, :]).then_inc(ns.hotT_ready.sem, 1)

            def next_hotT(ns, i, s):
                if s < SLOTS - 1:
                    copy_hotT(ns, i, s + 1)
                elif not (isinstance(i, int) and i == TURNS - 1):
                    copy_hotT(ns, i + 1, 0)

            def attention(n):
                ns = a_att[n]

                def step(i, s):
                    g, par = SLOTS * i + s, s % 2
                    next_hotT(ns, i, s)
                    reached(act, ns.clip_ready, g + 1)
                    reached(act, ns.sums_ready, g - 1)
                    nc.scalar.activation(score[par][:, :, :].rearrange("p k (h c) -> p (k h) c", c=DH),
                                         clipped[par][:, :, :].rearrange("p k h -> p (k h)").unsqueeze(2)
                                         .to_broadcast([P, G * HEADS, DH]), ACT.Exp,
                                         scale=float(DH) ** -0.5).then_inc(ns.score_ready.sem, 1)
                    if ahead(i, s, 2):
                        squares(ns, dst_rel_of, G, *ahead(i, s, 2))
                        hot_from_squares(ns, G, *ahead(i, s, 2))
                for s in (0, 1):
                    squares(ns, dst_rel_of, G, 0, s)
                    hot_from_squares(ns, G, 0, s)
                copy_hotT(ns, 0, 0)
                turns(act, step)

            def gat(n):
                ns = a_gat[n]

                def step(i, s):
                    next_hotT(ns, i, s)
                copy_hotT(ns, 0, 0)
                turns(act, step)
                mix, sm = a_mix[n], n_sm[n]
                reached(act, ns.logit_ready, NG)
                zero_parts(0)
                reached(act, sm.shifted, 1)
                nc.scalar.activation(best_f[:, :, :, :], best_f[:, :, :, :], ACT.Exp).then_inc(sm.exp_ready.sem, 1)
                hots(mix, dst_rel_of)

            def root(dst, var, ready, done, n):
                reached(act, ready, n)
                nc.scalar.activation(dst, var, ACT.Sqrt, bias=eps[:, :]).then_inc(done.sem, 1)

            def normalise(ns, dest, source=lambda c: psA[c % 2][:, 0:512].rearrange("p (b f) -> p b f", f=D)):
                for c, (b0, nb) in enumerate(CHUNKS):
                    root(std[c % 2][:, 0:nb], mv[c % 2][:, 0:nb, 1], ns.var_ready, ns.std_ready, c + 1)
                    reached(act, ns.coef_ready, c + 1)
                    for j in range(nb):
                        last = nc.scalar.activation(dest[:, b0 + j, :], source(c)[:, j, :], ACT.Identity,
                                                    bias=shift[c % 2][:, j:j + 1], scale=rstd[c % 2][:, j:j + 1])
                    last.then_inc(ns.norm_ready.sem, 1)

            def spread_rden(n):
                ns = n_nm[n]
                reached(act, ns.rden_ready, 1)
                for c, (b0, nb) in enumerate(CHUNKS):
                    nc.scalar.copy(nA[:, b0:b0 + nb, :].rearrange("p b (h c) -> p (b h) c", h=HEADS),
                                   rden[:, b0 * HEADS:(b0 + nb) * HEADS].unsqueeze(2)
                                   .to_broadcast([P, nb * HEADS, DH])).then_inc(ns.along.sem, 1)

            def tables(t):
                ns, width = n_tb[t], 3 * D if TABLES[t][0] in Wkvq else 2 * D
                for c, (b0, nb) in enumerate(CHUNKS):
                    for j in range(nb):
                        b = b0 + j
                        reached(act, ns.product_ready, b + 1)
                        if c >= 2 and j == 0:
                            reached(act, ns.stored[c % 2], 32 * (c // 2))
                        nc.scalar.copy(stage[c % 2][:, j, 0:width], psQ[b % 2][:, 0:width]).then_inc(ns.copied.sem, 1)

            def count(i, s):
                g = SLOTS * i + s
                reached(act, a_count.counted, g + 1)
                nc.scalar.copy(before[:, :, bass.ds(G * g + 1, G)].rearrange("p h k -> p k h"),
                               psQ[s % 2][:, 0:G * HI].rearrange("p (k h) -> p k h", k=G)).then_inc(a_count.before_ready.sem, 1)

            def send(i, s):
                ns, g, par = a_send, SLOTS * i + s, s % 2
                nxt = ahead(i, s, 1)
                if nxt:
                    transposed_hots(*nxt)
                reached(act, ns.spread_ready, g + 1)
                reached(act, ns.rows_sent[s], 16 * G * i)
                row = rows[s][:, 0:G * SENT].rearrange("p (k w) -> p k w", k=G)
                for k in range(G):
                    nc.scalar.activation(row[:, k, 0:D], psQ[par][:, k * D:(k + 1) * D], ACT.Copy,
                                         scale=weight[:, bass.ds(G * g + k, 1)])
                nc.scalar.copy(row[:, :, D], src_f[:, bass.ds(G * g, G)]).then_inc(ns.scaled.sem, 1)

            def transposed_hots(i, s):
                ns, g, par = a_send, SLOTS * i + s, s % 2
                reached(act, ns.hotT_psum, g + 1)
                reached(act, ns.spread_ready, g - 1)
                nc.scalar.copy(hotT[par][:, :, :].rearrange("p k n -> p (k n)"), psT[0][:, :]).then_inc(ns.hotT_ready.sem, 1)
                reached(act, ns.low_psum, g + 1)
                reached(act, ns.prior_psum, g - 1)
                nc.scalar.copy(low_hotT[par][:, :, :].rearrange("p k n -> p (k n)"), psT[1][:, :]).then_inc(ns.lowT_ready.sem, 1)

            act.wait_ge(s_pool, 3)
            turns(act, count)
            act.wait_ge(s_colsv, 2)
            transposed_hots(0, 0)
            turns(act, send)
            reached(act, a_send.place_ready, NG)
            zero_parts(2)
            hots(a_sum, src_rel)
            normalise(n_ln[0], xN)
            tables(0)
            attention(0)
            spread_rden(0)
            normalise(n_ln[1], nA)
            act.wait_ge(s_wts, 16 * len(weight_loads))
            for c, (b0, nb) in enumerate(CHUNKS):
                reached(act, n_tr[1].in_psum, c + 1)
                nc.scalar.activation(xT[:, b0 * P:(b0 + nb) * P], psT[c % 2][:, 0:nb * P], ACT.Identity,
                                     bias=col_b1[:, :], scale=col_g1[:, :]).then_inc(n_tr[1].copied.sem, 1)

            def relu_up(c):
                nb = CHUNKS[c][1]
                reached(act, n_ff.up_ready, c + 1)
                reached(act, n_ff.z_ready, c - 1)
                for k in range(2):
                    last = nc.scalar.activation(ffT[c % 2][:, k, 0:nb * P], psQ[k][:, 0:nb * P], ACT.Relu,
                                                bias=col_c1[:, k:k + 1])
                last.then_inc(n_ff.up_copied.sem, 1)
            relu_up(0)
            for c, (b0, nb) in enumerate(CHUNKS):
                if c + 1 < len(CHUNKS):
                    relu_up(c + 1)
                root(std[c % 2][:, 0:nb], mv[c % 2][:, 0:nb, 1], n_ff.var_ready, n_ff.std_ready, c + 1)
                root(std[c % 2][:, 0:nb], mv[c % 2][:, 0:nb, 1], n_ff.var3_ready, n_ff.std3_ready, c + 1)
                reached(act, n_ff.coef3_ready, c + 1)
                for j in range(nb):
                    last = nc.scalar.activation(xN[:, b0 + j, :], nA[:, b0 + j, :], ACT.Identity,
                                                bias=shift[c % 2][:, j:j + 1], scale=rstd[c % 2][:, j:j + 1])
                last.then_inc(n_ff.norm_ready.sem, 1)

            def pairnorm(n):
                pr = n_pr[n]
                reached(act, pr.mean, 1)
                nc.scalar.activation(acc[:, 1, 0:N], acc[:, 0, 0:N], ACT.Square, bias=pair[:, 1:2],
                                     accum_out=pair[:, 2:3]).then_inc(pr.squared.sem, 1)
                reached(act, pr.total, 1)
                nc.scalar.activation(pair[:, 3:4], psT[1][:, 0:1], ACT.Sqrt, bias=eps[:, :], scale=1.0 / N).then_inc(pr.std.sem, 1)
                reached(act, pr.ready, 1)
                nc.scalar.activation(xT[:, 0:N], acc[:, 0, 0:N], ACT.Relu, bias=pair[:, 5:6],
                                     scale=pair[:, 4:5]).then_inc(pr.x_ready.sem, 1)

            tables(1)
            gat(0)
            pairnorm(0)
            tables(2)
            gat(1)
            pairnorm(1)
            normalise(n_ln[2], xN)
            tables(3)
            attention(1)
            spread_rden(1)
            normalise(n_ln[3], xN)

        @block.vector
        def _(dve):
            chain = [0]

            def link(ins):
                chain[0] += 1
                ins.then_inc(s_chain, 1)
                dve.wait_ge(s_chain, chain[0])

            V = nc.vector
            dve.wait_ge(s_meta, 16 * 14)
            V.tensor_copy(rows_f[:, 0:4], rows_i[:, 0:4])
            V.tensor_scalar(first_dst[:, :], first_i[:, :], float(NPAD - P), None, ALU.min)
            link(V.tensor_copy(ends_f[:, :, :], ends_i[:, :, :]))
            link(V.tensor_copy(first_f[:, :], first_dst[:, :]))
            link(V.tensor_tensor(copies[:, :, :], rows_f[:, 0], rows_f[:, 2], ALU.not_equal))
            V.tensor_scalar(copies[:, :, :], copies[:, :, :], 1.0, None, ALU.add).then_inc(s_tofloat, 1)
            dve.wait_ge(s_cols, 1)
            V.tensor_copy(src_f[:, :], psT[0][:, 0:TILES])
            link(V.tensor_copy(src_idx[:, :], psT[0][:, 0:TILES]))
            for part, op, by in ((src_high, ALU.arith_shift_right, 7), (src_low, ALU.bitwise_and, P - 1)):
                link(V.tensor_scalar(part_i, src_idx[:, :], by, None, op))
                link(V.tensor_copy(part, part_i))
            V.tensor_copy(first_f[:, :], first_dst[:, :]).then_inc(s_colsv, 1)
            V.tensor_copy(weight[:, :], psQ[0][:, 0:TILES])
            link(V.tensor_copy(dst_rel[:, :], psT[1][:, 0:TILES]))
            V.tensor_tensor(dst_rel[:, :], dst_rel[:, :], psA[0][:, 0:TILES], ALU.subtract).then_inc(s_colsv, 1)
            dve.wait_ge(s_colsv, 2)

            def masks():
                for q_scan, q_open, nb, edge, first in ((scan_fwd, open_fwd, 1, 0, 0), (scan_bwd, open_bwd, 2, P - 1, P - 1)):
                    link(V.tensor_tensor(q_open[:, :, :], rows_f[:, 0], rows_f[:, nb], ALU.not_equal))
                    for h in range(GHEADS):
                        link(V.tensor_scalar(q_scan[:, :, h, :], q_open[:, :, :], -BIG, None, ALU.mult))
                    link(V.memset(q_scan[:, :, :, edge:edge + 1], -BIG))
                    link(V.tensor_tensor(q_open[:, :, :], rows_f[:, 0],
                                         rows_f[:, nb, :, edge:edge + 1].to_broadcast([ROWS, QUARTERS, P]), ALU.not_equal))
                    link(V.tensor_scalar(q_open[:, :, :], q_open[:, :, :], -BIG, None, ALU.mult))
                link(V.tensor_tensor(pass_fwd[:, :], ends_f[:, 2, :], ends_f[:, 0, :], ALU.not_equal))
                link(V.tensor_scalar(pass_fwd[:, :], pass_fwd[:, :], -BIG, None, ALU.mult))
                link(V.tensor_tensor(pass_bwd[:, :], ends_f[:, 1, :], ends_f[:, 3, :], ALU.not_equal))
                link(V.tensor_scalar(pass_bwd[:, :], pass_bwd[:, :], -BIG, None, ALU.mult))
                link(V.tensor_scalar(whole_fwd, pass_fwd[:, :], 0.0, None, ALU.is_ge))
                link(V.tensor_scalar(whole_bwd, pass_bwd[:, :], 0.0, None, ALU.is_ge))

            def make_hot(ns, i, s):
                g = SLOTS * i + s
                V.tensor_tensor(hot[s][:, :, :], iota[:, :].unsqueeze(1).to_broadcast([P, G, P]),
                                dst_rel[:, bass.ds(G * g, G)].unsqueeze(2).to_broadcast([P, G, P]),
                                ALU.is_equal).then_inc(ns.hot_ready.sem, 1)

            def add_sums(ns, i, s):
                g, par = SLOTS * i + s, s % 2
                firsts = load_firsts(DVE, g, first_src if ns is a_sum else first_dst)
                reached(dve, ns.sums_ready, g + 1)
                reached(dve, ns.acc_written, G * g)
                for k in range(G):
                    d = parts[:, k, bass.ds(firsts[k], P)]
                    V.tensor_tensor(d, d, psS[par][:, k, 0], ALU.add).then_inc(ns.acc_written.sem, 1)

            def add_tile(ns, i, s, k, firsts):
                reached(dve, ns.acc_written, G * (SLOTS * i + s) + k)
                d = acc[:, :, bass.ds(firsts[k], P)]
                V.tensor_tensor(d, d, psS[s % 2][:, k], ALU.add).then_inc(ns.acc_written.sem, 1)

            def last_hot(ns, rel, i, s):
                reached(dve, ns.sums_ready, SLOTS * i + s - SLOTS + 1)
                if ns is a_sum:
                    reached(dve, ns.rel_ready, SLOTS * i + s + 1)
                V.tensor_scalar(hot[s][:, G - 1, :], iota[:, :], rel(i, s), None, ALU.is_equal).then_inc(ns.last_hot_ready.sem, 1)

            def sum_tiles(ns, rel):
                def step(i, s):
                    if ahead(i, s, 1):
                        last_hot(ns, rel, *ahead(i, s, 1))
                    add_sums(ns, i, s)
                last_hot(ns, rel, 0, 0)
                turns(dve, step)
                fold(ns)

            def fold(ns):
                reached(dve, ns.acc_written, TILES)
                V.tensor_tensor(parts[:, 0, :], parts[:, 0, :], parts[:, 2, :], ALU.add).then_inc(ns.folded.sem, 1)
                reached(dve, ns.folded, 2)

            def hot_high(dst, g):
                return V.tensor_tensor(dst[:, :, :], iota[:, 0:HI].unsqueeze(1).to_broadcast([P, G, HI]),
                                       src_high[:, bass.ds(G * g, G)].unsqueeze(2).to_broadcast([P, G, HI]), ALU.is_equal)

            def hot_low(dst, g):
                return V.tensor_tensor(dst[:, :, :], iota[:, :].unsqueeze(1).to_broadcast([P, G, P]),
                                       src_low[:, bass.ds(G * g, G)].unsqueeze(2).to_broadcast([P, G, P]), ALU.is_equal)

            def count(i, s):
                g = SLOTS * i + s
                reached(dve, a_count.counted, g - SLOTS + 1)
                hot_high(high_b[s], g)
                hot_low(hot_b[s], g).then_inc(a_count.hot_ready.sem, 1)

            def run_up():
                reached(dve, a_count.before_ready, NG)
                link(V.memset(high_sum[:, 0:1], 0.0))
                for h in range(HI):
                    c = before[:, h, 1:TILES + 1]
                    last = V.tensor_tensor_scan(c, ones[:, 0:1].to_broadcast([P, TILES]), c, 0.0, ALU.mult, ALU.add)
                last.then_inc(s_total, 1)
                dve.wait_ge(s_base, 1)
                link(V.tensor_tensor_scan(high_sum[:, 1:HI + 1], ones[:, 0:HI], psQ[1][:, 0:HI], 0.0, ALU.mult, ALU.add))
                V.tensor_tensor(base[:, :], psQ[0][:, 0:HI], high_sum[:, 0:HI], ALU.add).then_inc(s_base, 1)

            def send_hots(i, s):
                ns, g, par = a_send, SLOTS * i + s, s % 2
                reached(dve, ns.spread_ready, g - SLOTS + 1)
                make_hot(ns, i, s)
                reached(dve, ns.low_psum, g - 1)
                hot_low(low_hot[par], g)
                hot_high(high_hot[s], g).then_inc(ns.low_ready.sem, 1)

            def send(i, s):
                ns, g, par = a_send, SLOTS * i + s, s % 2
                reached(dve, ns.sources_landed[s], 16 * (i + 1))
                for k in range(G):
                    V.scalar_tensor_tensor(matched[par][:, k, :], sources[s][:, k * P:(k + 1) * P], src_f[:, bass.ds(G * g + k, 1)],
                                           earlier[:, :], ALU.is_equal, ALU.mult, accum_out=within[par][:, k:k + 1])
                reached(dve, ns.prior_psum, g + 1)
                V.tensor_tensor(prior_h[par][:, :, :], psA[par][:, 512:512 + G * HI].rearrange("p (k h) -> p k h", k=G),
                                high_hot[s][:, :, :], ALU.mult).then_inc(ns.prior_used.sem, 1)
                reached(dve, ns.prior_used, g + 1)
                V.tensor_reduce(prior[par][:, :], prior_h[par][:, :, :], AX.X, ALU.add).then_inc(ns.prior_ready.sem, 1)
                if ahead(i, s, 2):
                    send_hots(*ahead(i, s, 2))
                reached(dve, ns.prior_ready, g + 1)
                reached(dve, ns.rows_sent[s], 16 * G * i)
                V.tensor_tensor(place[s][:, :], prior[par][:, :], within[par][:, :], ALU.add).then_inc(ns.place_ready.sem, 1)

            def sum_pass():
                ns = a_sum

                dve.wait_ge(s_first, 16)
                link(V.tensor_scalar(first_src_f[:, :], first_src_f[:, :], float(NPAD - P), None, ALU.min))
                V.tensor_copy(first_src[:, :], first_src_f[:, :]).then_inc(s_first, 1)
                dve.wait_ge(s_first, 18)
                V.tensor_copy(first_src_bc, psT[0][:, 0:TILES]).then_inc(s_first, 1)
                dve.wait_ge(s_first, 19)
                sum_tiles(ns, lambda i, s: msg_rel[s][:, G - 1:G])

            def attention(n):
                ns = a_att[n]

                def step(i, s):
                    g, par = SLOTS * i + s, s % 2
                    kv = rows[s][:, :].rearrange("p (k w) -> p k w", k=G)
                    reached(dve, ns.spread_ready, g + 1)
                    reached(dve, ns.rows_landed[s], 16 * G * (i + 1))
                    V.tensor_tensor(prod[par][:, :, :], kv[:, :, 0:D],
                                    psQ[par][:, :].rearrange("p (k f) -> p k f", k=G), ALU.mult).then_inc(ns.spread_used.sem, 1)
                    before_last = behind(*behind(i, s)) if behind(i, s) else None
                    firsts = before_last and load_firsts(DVE, g - 2)
                    if before_last:
                        reached(dve, ns.sums_ready, g - 1)

                    def add(k):
                        if before_last:
                            add_tile(ns, *before_last, k, firsts)
                    add(0)
                    reached(dve, ns.spread_used, g + 1)
                    V.tensor_reduce(raw[par][:, :, :].rearrange("p k h -> p (k h)"),
                                    prod[par][:, :, :].rearrange("p k (h c) -> p (k h) c", c=DH),
                                    AX.X, ALU.add).then_inc(ns.raw_ready.sem, 1)
                    add(1)
                    reached(dve, ns.raw_ready, g + 1)
                    lim = 5.0 * float(DH) ** 0.5
                    V.tensor_scalar(clipped[par][:, :, :], raw[par][:, :, :], lim, -lim, ALU.min, ALU.max).then_inc(ns.clip_ready.sem, 1)
                    add(2)
                    add(3)
                    reached(dve, ns.score_ready, g + 1)
                    V.tensor_tensor(msg[par][:, :, :], kv[:, :, D:2 * D], score[par][:, :, :], ALU.mult).then_inc(ns.msg_ready.sem, 1)
                turns(dve, step)
                for s in (SLOTS - 2, SLOTS - 1):
                    firsts = load_firsts(DVE, SLOTS * (TURNS - 1) + s)
                    reached(dve, ns.sums_ready, SLOTS * (TURNS - 1) + s + 1)
                    for k in range(G):
                        add_tile(ns, TURNS - 1, s, k, firsts)

            def gat(n, zeroed):
                ns, mix, sm = a_gat[n], a_mix[n], n_sm[n]

                def weigh(i, s):
                    g, par = SLOTS * i + s, s % 2
                    reached(dve, ns.spread_used, g + 1)
                    V.scalar_tensor_tensor(leaky[par][:, :, :], prod[par][:, :, :], 0.2, prod[par][:, :, :],
                                           ALU.mult, ALU.max).then_inc(ns.leaky_ready.sem, 1)
                    reached(dve, ns.leaky_ready, g + 1)
                    V.tensor_tensor(msg[par][:, :, :], leaky[par][:, :, :],
                                    att[n][:, :].unsqueeze(1).to_broadcast([P, G, D]), ALU.mult).then_inc(ns.weighted.sem, 1)
                    reached(dve, ns.weighted, g + 1)
                    V.tensor_reduce(logits[:, bass.ds(G * g, G), :].rearrange("p k h -> p (k h)"),
                                    msg[par][:, :, :].rearrange("p k (h c) -> p (k h) c", c=GC),
                                    AX.X, ALU.add).then_inc(ns.logit_ready.sem, 1)

                def step(i, s):
                    g, par = SLOTS * i + s, s % 2
                    reached(dve, ns.spread_ready, g + 1)
                    reached(dve, ns.rows_landed[s], 16 * G * (i + 1))
                    V.tensor_tensor(prod[par][:, :, :].rearrange("p k f -> p (k f)"), rows[s][:, 0:G * D],
                                    psQ[par][:, :], ALU.add).then_inc(ns.spread_used.sem, 1)
                    if ahead(i, s, 2):
                        reached(dve, ns.hotT_psum, g - 1)
                        make_hot(ns, *ahead(i, s, 2))
                    if behind(i, s):
                        weigh(*behind(i, s))
                make_hot(ns, 0, 0)
                make_hot(ns, 0, 1)
                turns(dve, step)
                weigh(TURNS - 1, SLOTS - 1)

                flat = "r q h p -> r (q h p)"
                reached(dve, sm.rowwise, 1)
                rowlog = psA[0][0:ROWS, :]
                V.tensor_tensor_scan(best_f[:, :, :, :].rearrange(flat), scan_fwd[:, :, :, :].rearrange(flat), rowlog,
                                     -BIG, ALU.add, ALU.max)
                V.tensor_tensor_scan(best_b[:, :, :, :].rearrange(flat)[:, ::-1], scan_bwd[:, :, :, :].rearrange(flat)[:, ::-1],
                                     rowlog[:, ::-1], -BIG, ALU.add, ALU.max).then_inc(sm.scanned.sem, 1)
                V.memset(carry_f[:, 0:1], -BIG)
                V.memset(carry_b[:, TILES:TILES + 1], -BIG)
                reached(dve, sm.ends_up, 1)
                V.tensor_tensor_scan(carry_f[:, 1:TILES + 1], pass_fwd[:, :], psT[0][0:2, 0:TILES], -BIG, ALU.add, ALU.max)
                V.tensor_tensor_scan(carry_b[:, 0:TILES][:, ::-1], pass_bwd[:, ::-1], psT[1][0:2, 0:TILES][:, ::-1],
                                     -BIG, ALU.add, ALU.max).then_inc(sm.carried.sem, 1)
                reached(dve, sm.carries_down, 1)
                entering = [psc[0:ROWS, 0:QUARTERS * GHEADS].rearrange("r (q h) -> r q h", q=QUARTERS).unsqueeze(3)
                            .to_broadcast([ROWS, QUARTERS, GHEADS, P]) for psc in (psQ[0], psQ[1])]
                per_head = [o[:, :, :].unsqueeze(2).to_broadcast([ROWS, QUARTERS, GHEADS, P]) for o in (open_fwd, open_bwd)]
                whole4 = (slice(None),) * 4
                for best, opened, entry in ((best_f, per_head[0], entering[0]), (best_b, per_head[1], entering[1])):
                    link(V.tensor_tensor(held[whole4], opened, entry, ALU.add))
                    link(V.tensor_tensor(best[whole4], best[whole4], held[whole4], ALU.max))
                link(V.tensor_tensor(best_f[whole4], best_f[whole4], best_b[whole4], ALU.max))
                V.tensor_tensor(best_f[:, :, :, :].rearrange(flat), rowlog, best_f[:, :, :, :].rearrange(flat),
                                ALU.subtract).then_inc(sm.shifted.sem, 1)

                V.tensor_scalar(held[whole4], scan_fwd[whole4], 0.0, None, ALU.is_ge)
                V.tensor_scalar(best_b[whole4], scan_bwd[whole4], 0.0, None, ALU.is_ge)
                V.memset(carry_f[:, 0:1], 0.0)
                V.memset(carry_b[:, TILES:TILES + 1], 0.0)
                reached(dve, sm.exp_ready, 1)
                rowexp = psA[1][0:ROWS, :]
                link(V.tensor_tensor(rowexp.rearrange("r (q h p) -> r q h p", q=QUARTERS, h=GHEADS), best_f[whole4],
                                     copies[:, :, :].unsqueeze(2).to_broadcast([ROWS, QUARTERS, GHEADS, P]), ALU.mult))
                V.tensor_tensor_scan(best_f[:, :, :, :].rearrange(flat), held[:, :, :, :].rearrange(flat), rowexp,
                                     0.0, ALU.mult, ALU.add)
                V.tensor_tensor_scan(best_b[:, :, :, :].rearrange(flat)[:, ::-1], best_b[:, :, :, :].rearrange(flat)[:, ::-1],
                                     rowexp[:, ::-1], 0.0, ALU.mult, ALU.add).then_inc(sm.sums_scanned.sem, 1)
                reached(dve, sm.sum_ends_up, 1)
                V.tensor_tensor_scan(carry_f[:, 1:TILES + 1], whole_fwd, psT[0][0:2, 0:TILES], 0.0, ALU.mult, ALU.add)
                V.tensor_tensor_scan(carry_b[:, 0:TILES][:, ::-1], whole_bwd[:, ::-1], psT[1][0:2, 0:TILES][:, ::-1],
                                     0.0, ALU.mult, ALU.add).then_inc(sm.sums_carried.sem, 1)
                link(V.tensor_tensor(best_f[whole4], best_f[whole4], best_b[whole4], ALU.add))
                link(V.tensor_tensor(best_f[:, :, :, :].rearrange(flat), best_f[:, :, :, :].rearrange(flat), rowexp, ALU.subtract))
                reached(dve, sm.sums_down, 1)
                for opened, entry in zip(per_head, entering):
                    for q in range(QUARTERS):
                        last = V.scalar_tensor_tensor(held[:, q], opened[:, q], 0.0, entry[:, q], ALU.is_ge, ALU.mult)
                    link(last)
                    link(V.tensor_tensor(best_f[whole4], best_f[whole4], held[whole4], ALU.add))
                link(V.tensor_scalar(best_f[whole4], best_f[whole4], 1e-16, None, ALU.add))
                link(V.reciprocal(best_f[whole4], best_f[whole4]))
                V.tensor_tensor(best_f[:, :, :, :].rearrange(flat), best_f[:, :, :, :].rearrange(flat), rowexp,
                                ALU.mult).then_inc(sm.alpha_rows.sem, 1)
                reached(dve, sm.alpha_up, 1)
                for h in range(GHEADS):
                    last = V.tensor_copy(alpha[:, :, h], psT[h][:, 0:TILES])
                last.then_inc(sm.alpha_ready.sem, 1)

                dve.wait_ge(s_zeroed, zeroed)
                sum_tiles(mix, lambda i, s: dst_rel[:, bass.ds(G * (SLOTS * i + s) + G - 1, 1)])

            def block_stats(ready, n, z, st, m, nb, s1, s2):
                reached(dve, ready, n)
                for j in range(nb):
                    last = V.bn_stats(st[:, j, :], z[:, j, :])
                last.then_inc(s1.sem, 1)
                reached(dve, s1, n)
                for j in range(nb):
                    last = V.bn_aggr(m[:, j, :], st[:, j, :])
                last.then_inc(s2.sem, 1)

            def coefficients(std_ready, s1, s2, n, c, nb):
                reached(dve, std_ready, n)
                V.reciprocal(rstd[c % 2][:, 0:nb], std[c % 2][:, 0:nb]).then_inc(s1.sem, 1)
                reached(dve, s1, n)
                V.scalar_tensor_tensor(shift[c % 2][:, 0:nb], mv[c % 2][:, 0:nb, 0], -1.0, rstd[c % 2][:, 0:nb],
                                       ALU.mult, ALU.mult).then_inc(s2.sem, 1)

            def zchunk(c):
                return psA[c % 2][:, 0:512].rearrange("p (b f) -> p b f", f=D)

            def layernorm(ns):
                for c, (b0, nb) in enumerate(CHUNKS):
                    if c >= 2:
                        reached(dve, ns.norm_ready, c - 1)
                    block_stats(ns.z_ready, c + 1, zchunk(c), stats[c % 2], mv[c % 2], nb, ns.stats_ready, ns.var_ready)
                    coefficients(ns.std_ready, ns.rstd_ready, ns.coef_ready, c + 1, c, nb)

            def copy_transposed(ns):
                for c, (b0, nb) in enumerate(CHUNKS):
                    reached(dve, ns.in_psum, c + 1)
                    V.tensor_copy(xT[:, b0 * P:(b0 + nb) * P], psT[c % 2][:, 0:nb * P]).then_inc(ns.copied.sem, 1)

            def divide_by_sums(n):
                ns = n_nm[n]
                reached(dve, ns.den_ready, 1)
                V.tensor_scalar(den[:, :], psT[0][:, 0:NB * HEADS], 1e-30, None, ALU.max).then_inc(ns.den_copied.sem, 1)
                reached(dve, ns.den_copied, 1)
                V.reciprocal(rden[:, :], den[:, :]).then_inc(ns.rden_ready.sem, 1)
                for c, (b0, nb) in enumerate(CHUNKS):
                    reached(dve, ns.spread_ready, c + 1)
                    d = acc[:, 0, b0 * P:(b0 + nb) * P]
                    V.tensor_tensor(d, d, psQ[c % 2][:, 0:nb * P], ALU.mult).then_inc(ns.scaled.sem, 1)

            def pairnorm(n):
                pr = n_pr[n]
                link(V.scalar_tensor_tensor(acc[:, 0, 0:N], acc[:, 0, 0:N], col_gat[:, n:n + 1], acc[:, 1, 0:N],
                                            ALU.add, ALU.add, accum_out=pair[:, 0:1]))
                V.tensor_scalar(pair[:, 1:2], pair[:, 0:1], -1.0 / N, None, ALU.mult).then_inc(pr.mean.sem, 1)
                reached(dve, pr.std, 1)
                link(V.reciprocal(pair[:, 4:5], pair[:, 3:4]))
                V.tensor_tensor(pair[:, 5:6], pair[:, 1:2], pair[:, 4:5], ALU.mult).then_inc(pr.ready.sem, 1)

            dve.wait_ge(s_pool, 3)
            turns(dve, count)
            run_up()
            send_hots(0, 0)
            send_hots(0, 1)
            turns(dve, send)
            masks()
            dve.wait_ge(s_zeroed, 2)
            sum_pass()
            layernorm(n_ln[0])
            copy_transposed(n_tr[0])
            dve.wait_ge(s_zeroed, 3)
            attention(0)
            divide_by_sums(0)
            layernorm(n_ln[1])
            dve.wait_ge(s_wts, 16 * len(weight_loads))
            reached(dve, n_ln[1].norm_ready, len(CHUNKS))
            for c, (b0, nb) in enumerate(CHUNKS):
                m, st, z = mv[c % 2], stats[c % 2], zchunk(c)
                if c >= 2:
                    reached(dve, n_ff.norm_ready, c - 1)
                block_stats(n_ff.z_ready, c + 1, z, st, m, nb, n_ff.stats_ready, n_ff.var_ready)
                reached(dve, n_ff.std_ready, c + 1)
                V.reciprocal(rstd[c % 2][:, 0:nb], std[c % 2][:, 0:nb]).then_inc(n_ff.rstd_ready.sem, 1)
                for j in range(nb):
                    last = V.scalar_tensor_tensor(nA[:, b0 + j, :], z[:, j, :], m[:, j, 0:1], bc_g2[:, :],
                                                  ALU.subtract, ALU.mult)
                last.then_inc(n_ff.scaled.sem, 1)
                reached(dve, n_ff.rstd_ready, c + 1)
                reached(dve, n_ff.scaled, c + 1)
                reached(dve, n_ff.xb_ready, c + 1)
                for j in range(nb):
                    last = V.scalar_tensor_tensor(nA[:, b0 + j, :], nA[:, b0 + j, :], rstd[c % 2][:, j:j + 1],
                                                  xN[:, b0 + j, :], ALU.mult, ALU.add)
                last.then_inc(n_ff.v_ready.sem, 1)
                block_stats(n_ff.v_ready, c + 1, nA[:, b0:b0 + nb, :], st, m, nb, n_ff.stats3_ready, n_ff.var3_ready)
                coefficients(n_ff.std3_ready, n_ff.rstd3_ready, n_ff.coef3_ready, c + 1, c, nb)
            copy_transposed(n_tr[2])
            gat(0, 4)
            pairnorm(0)
            gat(1, 5)
            pairnorm(1)
            layernorm(n_ln[2])
            copy_transposed(n_tr[3])
            dve.wait_ge(s_zeroed, 6)
            attention(1)
            divide_by_sums(1)
            layernorm(n_ln[3])

        @block.tensor
        def _(pe):
            mm, tr = nc.tensor.matmul, nc.tensor.transpose
            pe.wait_ge(s_pool, 3)
            pe.wait_ge(s_tofloat, 1)
            for ps_, src in ((psT[0], rows_f[:, 3]), (psT[1], rows_f[:, 0]), (psQ[0], rows_f[:, 4])):
                for q in range(QUARTERS):
                    tr(ps_[:, q * ROWS:(q + 1) * ROWS], src[:, q, :], ident[0:ROWS, 0:ROWS])
            mm(psA[0][:, 0:TILES], ones[0:1, :], first_f[0:1, :], start=True, stop=True).then_inc(s_cols, 1)

            def transpose_hot(ns, i, s):
                g, par = SLOTS * i + s, s % 2
                reached(pe, ns.hot_ready, g + 1)
                reached(pe, ns.hotT_ready, g - 1)
                for k in range(G):
                    last = tr(psT[par][:, k * P:(k + 1) * P], hot[s][:, k, :], ident[:, :])
                last.then_inc(ns.hotT_psum.sem, 1)

            def spread(ns, i, s):
                g, par = SLOTS * i + s, s % 2
                reached(pe, ns.window_landed[s], 16 * G * (i + 1))
                reached(pe, ns.spread_used, g - 1)
                reached(pe, ns.hotT_ready, g + 1)
                for k in range(G):
                    last = mm(psQ[par][:, k * D:(k + 1) * D], hotT[par][:, k, :], window[s][:, k, :], start=True, stop=True)
                last.then_inc(ns.spread_ready.sem, 1)

            def next_spread(ns, i, s):
                if s < SLOTS - 1:
                    nxt = (i, s + 1)
                elif isinstance(i, int) and i == TURNS - 1:
                    return
                else:
                    nxt = (i + 1, 0)
                transpose_hot(ns, *nxt)
                spread(ns, *nxt)

            def scatter(ns, i, s, messages, weights):
                g, par = SLOTS * i + s, s % 2
                reached(pe, ns.acc_written, G * (g - 1))
                for k in range(G):
                    last = mm(psS[par][:, k, 0, :], messages(s, k), hot[s][:, k, :], start=True, stop=True)
                    if weights:
                        last = mm(psS[par][:, k, 1, :], weights(par, k), hot[s][:, k, :], start=True, stop=True)
                last.then_inc(ns.sums_ready.sem, 1)

            def count(i, s):
                g = SLOTS * i + s
                reached(pe, a_count.hot_ready, g + 1)
                reached(pe, a_count.before_ready, g - 1)
                for k in range(G):
                    last = mm(psQ[s % 2][:, k * HI:(k + 1) * HI], hot_b[s][:, k, :], high_b[s][:, k, :], start=True, stop=True)
                last.then_inc(a_count.counted.sem, 1)

            def send_transposes(i, s):
                ns, g, par = a_send, SLOTS * i + s, s % 2
                reached(pe, ns.hot_ready, g + 1)
                reached(pe, ns.hotT_ready, g)
                for k in range(G):
                    last = tr(psT[0][:, k * P:(k + 1) * P], hot[s][:, k, :], ident[:, :])
                last.then_inc(ns.hotT_psum.sem, 1)
                reached(pe, ns.low_ready, g + 1)
                reached(pe, ns.lowT_ready, g)
                for k in range(G):
                    last = tr(psT[1][:, k * P:(k + 1) * P], low_hot[par][:, k, :], ident[:, :])
                last.then_inc(ns.low_psum.sem, 1)
                reached(pe, ns.window_landed[s], 16 * G * (i + 1))
                reached(pe, ns.scaled, g - 1)
                reached(pe, ns.hotT_ready, g + 1)
                for k in range(G):
                    last = mm(psQ[par][:, k * D:(k + 1) * D], hotT[par][:, k, :], window[s][:, k, :], start=True, stop=True)
                last.then_inc(ns.spread_ready.sem, 1)
                reached(pe, ns.lowT_ready, g + 1)
                reached(pe, ns.prior_used, g - 1)
                for k in range(G):
                    at = psA[par][:, 512 + k * HI:512 + (k + 1) * HI]
                    mm(at, low_hotT[par][:, k, :], base[:, :], start=True, stop=False)
                    last = mm(at, low_hotT[par][:, k, :], before[:, :, bass.ds(G * g + k, 1)].rearrange("p h o -> p (h o)"),
                              start=False, stop=True)
                last.then_inc(ns.prior_psum.sem, 1)

            def sum_pass():
                ns = a_sum
                pe.wait_ge(s_first, 17)
                mm(psT[0][:, 0:TILES], ones[0:1, :], first_src_f[0:1, :], start=True, stop=True).then_inc(s_first, 1)

                def step(i, s, n, j):
                    reached(pe, ns.hot_ready, SLOTS * i + s + 1)
                    reached(pe, ns.last_hot_ready, SLOTS * i + s + 1)
                    reached(pe, ns.rows_loaded[j], 16 * (n + 1))
                    scatter(ns, i, s, lambda s, k: message_rows[j][:, k * SENT:k * SENT + D], None)
                long_turns(pe, step)

            def attention(n):
                ns = a_att[n]

                def step(i, s):
                    next_spread(ns, i, s)
                    reached(pe, ns.msg_ready, SLOTS * i + s + 1)
                    scatter(ns, i, s, lambda s, k: msg[s % 2][:, k, :],
                            lambda par, k: score[par][:, k, :])
                transpose_hot(ns, 0, 0)
                spread(ns, 0, 0)
                turns(pe, step)

            def ends_up(done):
                for q in range(QUARTERS):
                    tr(psT[0][0:GHEADS, q * ROWS:(q + 1) * ROWS], best_f[:, q, :, P - 1], ident[0:ROWS, 0:ROWS])
                    last = tr(psT[1][0:GHEADS, q * ROWS:(q + 1) * ROWS], best_b[:, q, :, 0], ident[0:ROWS, 0:ROWS])
                last.then_inc(done.sem, 1)

            def carries_down(done):
                for q in range(QUARTERS):
                    at = q * ROWS
                    tr(psQ[0][0:ROWS, q * GHEADS:(q + 1) * GHEADS], carry_f[:, at:at + ROWS], ident[0:2, 0:2])
                    last = tr(psQ[1][0:ROWS, q * GHEADS:(q + 1) * GHEADS], carry_b[:, at + 1:at + 1 + ROWS], ident[0:2, 0:2])
                last.then_inc(done.sem, 1)

            def gat(n):
                ns, mix, sm = a_gat[n], a_mix[n], n_sm[n]
                transpose_hot(ns, 0, 0)
                spread(ns, 0, 0)
                turns(pe, lambda i, s: next_spread(ns, i, s))

                reached(pe, ns.logit_ready, NG)
                for q in range(QUARTERS):
                    for h in range(GHEADS):
                        at = (q * GHEADS + h) * P
                        last = tr(psA[0][0:ROWS, at:at + P], logits[:, q * ROWS:(q + 1) * ROWS, h], ident[:, :])
                last.then_inc(sm.rowwise.sem, 1)
                reached(pe, sm.scanned, 1)
                ends_up(sm.ends_up)
                reached(pe, sm.carried, 1)
                carries_down(sm.carries_down)
                reached(pe, sm.sums_scanned, 1)
                ends_up(sm.sum_ends_up)
                reached(pe, sm.sums_carried, 1)
                carries_down(sm.sums_down)
                reached(pe, sm.alpha_rows, 1)
                for q in range(QUARTERS):
                    for h in range(GHEADS):
                        last = tr(psT[h][:, q * ROWS:(q + 1) * ROWS], best_f[:, q, h, :], ident[0:ROWS, 0:ROWS])
                last.then_inc(sm.alpha_up.sem, 1)
                reached(pe, sm.alpha_ready, 1)

                def mix_step(i, s):
                    g = SLOTS * i + s
                    reached(pe, mix.hot_ready, g + 1)
                    reached(pe, mix.last_hot_ready, g + 1)
                    reached(pe, mix.msg_ready, g + 1)
                    scatter(mix, i, s, lambda s, k: msg[s % 2][:, k, :], None)
                turns(pe, mix_step)

            def add_row(dst, row):
                return mm(dst, ones[0:1, :], row, start=False, stop=True)

            def zchunk(c):
                return psA[c % 2][:, 0:512].rearrange("p (b f) -> p b f", f=D)

            def residual(ns, product):
                for c, (b0, nb) in enumerate(CHUNKS):
                    if c >= 2:
                        reached(pe, ns.norm_ready, c - 1)
                    for j in range(nb):
                        z = zchunk(c)[:, j, :]
                        mm(z, ident[:, :], xN[:, b0 + j, :], start=True, stop=False)
                        last = product(z, b0 + j)
                    last.then_inc(ns.z_ready.sem, 1)

            def transposed(ns, ready, src):
                for c, (b0, nb) in enumerate(CHUNKS):
                    reached(pe, ready, c + 1)
                    if c >= 2:
                        reached(pe, ns.copied, c - 1)
                    for j in range(nb):
                        last = tr(psT[c % 2][:, j * P:(j + 1) * P], src[:, b0 + j, :], ident[:, :])
                    last.then_inc(ns.in_psum.sem, 1)

            def tables(t, ready):
                ns, (w, outs, bias) = n_tb[t], TABLES[t]
                width = 3 * D if w in Wkvq else 2 * D
                for c, (b0, nb) in enumerate(CHUNKS):
                    ready(c)
                    for b in range(b0, b0 + nb):
                        if b >= 2:
                            reached(pe, ns.copied, b - 1)
                        last = mm(psQ[b % 2][:, 0:width], xT[:, b * P:(b + 1) * P], w[:, 0:width], start=True, stop=bias is None)
                        if bias is not None:
                            last = add_row(psQ[b % 2][:, 0:width], bias[0:1, 0:width])
                        last.then_inc(ns.product_ready.sem, 1)

            def divide_by_sums(n):
                ns = n_nm[n]
                reached(pe, a_att[n].acc_written, TILES)
                for b in range(NB):
                    last = mm(psT[0][:, b * HEADS:(b + 1) * HEADS], acc[:, 1, b * P:(b + 1) * P], sel8[:, :], start=True, stop=True)
                last.then_inc(ns.den_ready.sem, 1)
                for c, (b0, nb) in enumerate(CHUNKS):
                    reached(pe, ns.along, c + 1)
                    if c >= 2:
                        reached(pe, ns.scaled, c - 1)
                    for j in range(nb):
                        b = b0 + j
                        last = mm(psQ[c % 2][:, j * P:(j + 1) * P], nA[:, b, :], ident[:, :], start=True, stop=True)
                    last.then_inc(ns.spread_ready.sem, 1)

            def project(w, bias, halves=1):
                def product(z, b):
                    for h in range(halves):
                        mm(z, acc[:, h, b * P:(b + 1) * P], w[:, :], start=False, stop=False)
                    return add_row(z, bias[0:1, :])
                return product

            def pair_total(n):
                reached(pe, n_pr[n].squared, 1)
                mm(psT[1][:, 0:1], ones[:, :], pair[:, 2:3], start=True, stop=True).then_inc(n_pr[n].total.sem, 1)

            def by_copied(ns):
                return lambda c: reached(pe, ns.copied, c + 1)

            pe.wait_ge(s_colsv, 2)
            turns(pe, count)
            pe.wait_ge(s_total, 1)
            total = before[:, :, TILES]
            mm(psQ[0][:, 0:HI], later[:, :], total, start=True, stop=True)
            mm(psQ[1][:, 0:HI], ones[:, :], total, start=True, stop=True).then_inc(s_base, 1)
            pe.wait_ge(s_base, 2)
            turns(pe, send_transposes)
            sum_pass()
            pe.wait_ge(s_wts, 16 * len(weight_loads))
            pe.wait_ge(s_x, 32)
            reached(pe, a_sum.folded, 2)
            residual(n_ln[0], project(W0, row_b0, halves=2))
            transposed(n_tr[0], n_ln[0].norm_ready, xN)
            tables(0, by_copied(n_tr[0]))
            attention(0)
            divide_by_sums(0)
            reached(pe, n_nm[0].scaled, len(CHUNKS))
            residual(n_ln[1], project(Wo[0], row_bo[0]))
            transposed(n_tr[1], n_ln[1].norm_ready, nA)

            def feed_up(c):
                b0, nb = CHUNKS[c]
                reached(pe, n_tr[1].copied, c + 1)
                reached(pe, n_ff.up_copied, c)
                for k in range(2):
                    last = mm(psQ[k][:, 0:nb * P], W1[:, k * D:(k + 1) * D], xT[:, b0 * P:(b0 + nb) * P], start=True, stop=True)
                last.then_inc(n_ff.up_ready.sem, 1)
            feed_up(0)
            for c, (b0, nb) in enumerate(CHUNKS):
                if c + 1 < len(CHUNKS):
                    feed_up(c + 1)
                reached(pe, n_ff.up_copied, c + 1)
                if c >= 2:
                    reached(pe, n_ff.scaled, c - 1)
                for j in range(nb):
                    z = zchunk(c)[:, j, :]
                    mm(z, xT[:, (b0 + j) * P:(b0 + j + 1) * P], ident[:, :], start=True, stop=False)
                    for k in range(2):
                        mm(z, ffT[c % 2][:, k, j * P:(j + 1) * P], W2[:, k, :], start=False, stop=False)
                    last = add_row(z, row_c2[0:1, :])
                last.then_inc(n_ff.z_ready.sem, 1)
            transposed(n_tr[2], n_ff.norm_ready, xN)
            tables(1, by_copied(n_tr[2]))
            gat(0)
            pair_total(0)
            tables(2, lambda c: reached(pe, n_pr[0].x_ready, 1))
            gat(1)
            pair_total(1)
            reached(pe, n_pr[1].x_ready, 1)
            residual(n_ln[2], lambda z, b: mm(z, xT[:, b * P:(b + 1) * P], ident[:, :], start=False, stop=True))
            transposed(n_tr[3], n_ln[2].norm_ready, xN)
            tables(3, by_copied(n_tr[3]))
            attention(1)
            divide_by_sums(1)
            reached(pe, n_nm[1].scaled, len(CHUNKS))
            residual(n_ln[3], project(Wo[1], row_bo[1]))


ARGS = ["x", "src", "dst", "edge_weight", "L0_gnn_W", "L0_gnn_b", "L1_gnn_Wq", "L1_gnn_Wk", "L1_gnn_Wv", "L1_gnn_Wo",
        "L1_gnn_bo", "L1_gnn_g1", "L1_gnn_b1", "L1_gnn_g2", "L1_gnn_b2", "L1_gnn_W1", "L1_gnn_c1", "L1_gnn_W2",
        "L1_gnn_c2", "L2_gnn_Wl", "L2_gnn_Wr", "L2_gnn_att", "L2_gnn_bias", "L3_gnn_Wq", "L3_gnn_bq", "L3_gnn_Wk",
        "L3_gnn_bk", "L3_gnn_Wv", "L3_gnn_bv", "L3_gnn_Wo", "L3_gnn_bo"]
TRANSPOSED = ["L3_gnn_Wq", "L3_gnn_Wk", "L3_gnn_Wv", "L3_gnn_Wo"]


def kernel(**inputs):
    import numpy as _np
    import concourse.bacc as _bacc
    from concourse import mybir as _mybir
    from concourse.bass_utils import run_bass_kernel_spmd as _run

    nc = _bacc.Bacc("TRN2", target_bir_lowering=False, num_devices=1)
    arrays, args = {}, {}
    for name in ARGS:
        v = _np.asarray(inputs[name])
        if name in TRANSPOSED:
            v = v.T
        if name == "src":
            v = _np.concatenate([v, _np.full(EPAD - E, HI * P - 1, v.dtype)])
        if name == "edge_weight":
            v = _np.concatenate([v, _np.zeros(EPAD - E, v.dtype)])
        if name == "dst":
            v = _np.concatenate([_np.full(1, -1, v.dtype), v, _np.full(EPAD - E, FAR, v.dtype), _np.full(1, -2, v.dtype)])
        v = _np.ascontiguousarray(v)
        arrays[f"in_{name}"] = v
        args[name] = nc.dram_tensor(f"in_{name}", v.shape, _mybir.dt.from_np(v.dtype), kind="ExternalInput").ap()
    out = nc.dram_tensor("out_0", (N, D), _mybir.dt.float32, kind="ExternalOutput").ap()
    gnn_program(nc, args, out)
    r = _run(nc, [arrays], core_ids=[0])
    return r.results[0]["out_0"]
```

```python
import concourse.bass as bass
from concourse import mybir
from contextlib import ExitStack
from collections import namedtuple

F32 = mybir.dt.float32
I32 = mybir.dt.int32
BF16 = mybir.dt.bfloat16
ALU = mybir.AluOpType
ACT = mybir.ActivationFunctionType
AX = mybir.AxisListType

P = 128
N = 3125
E = 53125
D = 128
TILES = -(-E // P)
G = 4
NG = TILES // G
SLOTS = 4
TURNS = NG // SLOTS
LONG = 2 * SLOTS
EPAD = TILES * P
ROWS = 104
QUARTERS = TILES // ROWS
NB = -(-N // P) + 1
NPAD = NB * P
FULLB = N // P
TAILR = N - FULLB * P
CHUNKS = [(b, min(4, NB - b)) for b in range(0, NB, 4)]
HEADS = 8
DH = D // HEADS
GHEADS = 2
GC = D // GHEADS
BIG = 1e30
LN_EPS = 1e-5
FAR = 1 << 20
HI = -(-N // P)
SENT = D + 4


def gnn_program(nc, a, out):
    ctx = ExitStack()
    with ctx:
        def sb(name, shape, dt=F32):
            return ctx.enter_context(nc.sbuf_tensor(name, shape, dt))

        def ps(name, shape):
            return ctx.enter_context(nc.psum_tensor(name, shape, F32))

        def sem(name):
            return ctx.enter_context(nc.semaphore(name))

        def dram(name, shape):
            return nc.dram_tensor(name, shape, F32, kind="Internal").ap()

        kv_table = [dram(f"kv_table{i}", (NPAD, 2 * D)) for i in range(2)]
        q_table = [dram(f"q_table{i}", (NPAD, D)) for i in range(2)]
        xs_table = [dram(f"xs_table{i}", (NPAD, D)) for i in range(2)]
        xd_table = [dram(f"xd_table{i}", (NPAD, D)) for i in range(2)]
        x_table = dram("x_table", (NPAD, D))
        sorted_msgs = dram("sorted_msgs", (EPAD, SENT))
        edge_rows = [dram(f"edge_rows{i}", (NG, P, G * D)) for i in range(2)]

        rowspace = sb("rowspace", [P, 3 * GHEADS * QUARTERS * P])
        rows_f = rowspace[0:ROWS, 0:5 * QUARTERS * P].rearrange("r (n q p) -> r n q p", n=5, q=QUARTERS)
        src_idx = sb("src_idx", [P, TILES], I32)
        dst_rel = sb("dst_rel", [P, TILES])
        weight = sb("weight", [P, TILES])
        src_f = sb("src_f", [P, TILES])
        softbuf = sb("softbuf", [P, 2 * TILES * GHEADS])
        src_low = softbuf[:, 0:TILES]
        src_high = softbuf[:, TILES:2 * TILES]
        first_src_bc = softbuf[:, 2 * TILES:3 * TILES]
        part_i = softbuf[:, 3 * TILES:4 * TILES].bitcast(I32)
        first_src = sb("first_src", [1, TILES], I32)
        first_src_f = sb("first_src_f", [1, TILES])
        copies = sb("copies", [ROWS, QUARTERS, P])
        first_i = sb("first_i", [1, TILES], I32)
        first_dst = sb("first_dst", [1, TILES], I32)
        first_f = sb("first_f", [1, TILES])
        endbuf = sb("endbuf", [2, 4 * TILES])
        ends_i = endbuf[:, :].bitcast(I32).rearrange("h (n t) -> h n t", n=4)
        ends_f = sb("ends_f", [2, 4, TILES])
        scan_fwd = sb("scan_fwd", [ROWS, QUARTERS, GHEADS, P])
        scan_bwd = sb("scan_bwd", [ROWS, QUARTERS, GHEADS, P])
        open_fwd = sb("open_fwd", [ROWS, QUARTERS, P])
        open_bwd = sb("open_bwd", [ROWS, QUARTERS, P])
        pass_fwd = sb("pass_fwd", [2, TILES])
        pass_bwd = sb("pass_bwd", [2, TILES])
        whole_fwd, whole_bwd = ends_f[:, 0, :], ends_f[:, 3, :]

        ident = sb("ident", [P, P])
        iota = sb("iota", [P, P])
        iota_i = sb("iota_i", [P, P], I32)
        ones = sb("ones", [P, P])
        sel8 = sb("sel8", [P, HEADS])
        eps = sb("eps", [P, 1])
        earlier = sb("earlier", [P, P])
        later = sb("later", [P, P])

        W0 = sb("W0", [P, D])
        Wkvq = [sb(f"Wkvq{i}", [P, 3 * D]) for i in range(2)]
        Wo = [sb(f"Wo{i}", [P, D]) for i in range(2)]
        W1 = sb("W1", [P, 2 * D])
        W2 = sb("W2", [P, 2, D])
        Wsd = [sb(f"Wsd{i}", [P, 2 * D]) for i in range(2)]
        att = [sb(f"att{i}", [P, D]) for i in range(2)]
        row_b0 = sb("row_b0", [1, D])
        row_bo = [sb(f"row_bo{i}", [1, D]) for i in range(2)]
        row_c2 = sb("row_c2", [1, D])
        bc_kvq = sb("bc_kvq", [P, 3 * D])
        col_g1 = sb("col_g1", [P, 1])
        col_b1 = sb("col_b1", [P, 1])
        col_c1 = sb("col_c1", [P, 2])
        col_gat = sb("col_gat", [P, 2])
        bc_g2 = sb("bc_g2", [P, D])
        bc_b2 = sb("bc_b2", [P, D])

        xN = sb("xN", [P, NB, D])
        nodebuf = sb("nodebuf", [P, 4 * NPAD])
        acc = nodebuf[:, 0:2 * NPAD].rearrange("p (w n) -> p w n", w=2)
        parts = nodebuf[:, :].rearrange("p (w n) -> p w n", w=G)
        xT = nodebuf[:, 2 * NPAD:3 * NPAD]
        nA = nodebuf[:, 3 * NPAD:4 * NPAD].rearrange("p (b f) -> p b f", f=D)
        rows_i = nA[0:ROWS, 4:4 + 4 * QUARTERS, :].bitcast(I32).rearrange("r (n q) p -> r n q p", n=4)
        sources = [nodebuf[:, 11264 + k * G * P:11264 + (k + 1) * G * P].bitcast(I32) for k in range(SLOTS)]
        before = nodebuf[:, 0:HI * (TILES + 1)].rearrange("p (h t) -> p h t", h=HI)
        stats = [sb(f"stats{i}", [P, 4, 6]) for i in range(4)]
        mv = [sb(f"mv{i}", [P, 4, 2]) for i in range(4)]
        std = [sb(f"std{i}", [P, 4]) for i in range(4)]
        rstd = [sb(f"rstd{i}", [P, 4]) for i in range(4)]
        shift = [sb(f"shift{i}", [P, 4]) for i in range(4)]
        den = sb("den", [P, NB * HEADS])
        rden = sb("rden", [P, NB * HEADS])
        pair = sb("pair", [P, 8])

        idx = [sb(f"idx{s}", [P, G], I32) for s in range(SLOTS)]
        rowbuf = sb("rowbuf", [P, SLOTS * G * 2 * D])
        rows = [rowbuf[:, s * G * 2 * D:(s + 1) * G * 2 * D] for s in range(SLOTS)]
        winbuf = sb("winbuf", [P, SLOTS, G * D])
        window = [winbuf[:, s, :].rearrange("p (k f) -> p k f", k=G) for s in range(SLOTS)]
        message_rows = [winbuf[:, :, :].rearrange("p s f -> p (s f)")[:, 0:G * SENT]] + [
            rowbuf[:, j * G * SENT:(j + 1) * G * SENT] for j in range(7)]
        table_rows = [rowbuf[:, i * 12 * D:(i + 1) * 12 * D].rearrange("p (b w) -> p b w", b=4) for i in range(2)]
        ffT = [winbuf[:, 2 * i:2 * i + 2, :] for i in range(2)]
        hot = [sb(f"hot{s}", [P, G, P]) for s in range(SLOTS)]
        hotT = [sb(f"hotT{i}", [P, G, P]) for i in range(2)]
        prod = [sb(f"prod{i}", [P, G, D]) for i in range(2)]
        leaky = [sb(f"leaky{i}", [P, G, D]) for i in range(2)]
        raw = [sb(f"raw{i}", [P, G, HEADS]) for i in range(2)]
        clipped = [sb(f"clipped{i}", [P, G, HEADS]) for i in range(2)]
        score = [sb(f"score{i}", [P, G, D]) for i in range(2)]
        msg = [sb(f"msg{i}", [P, G, D]) for i in range(2)]
        low_hot, low_hotT = prod, leaky
        hot_b = [hot[s][:, 0:G // 2, :].rearrange("p k n -> p (k n)").bitcast(BF16).rearrange("p (k n) -> p k n", k=G)
                 for s in range(SLOTS)]
        high_hot = [sb(f"high_hot{i}", [P, G, HI]) for i in range(4)]
        high_b = [sb(f"high_b{i}", [P, G, HI], BF16) for i in range(SLOTS)]
        prior_h = [sb(f"prior_h{i}", [P, G, HI]) for i in range(2)]
        prior = [sb(f"prior{i}", [P, G]) for i in range(2)]
        within = [sb(f"within{i}", [P, G]) for i in range(2)]
        place = [sb(f"place{s}", [P, G], I32) for s in range(SLOTS)]
        base = sb("base", [P, HI])
        high_sum = sb("high_sum", [P, HI + 1])
        matched = score
        msg_rel = [sb(f"msg_rel{i}", [P, G]) for i in range(SLOTS)]

        logits = softbuf[:, 0:GHEADS * TILES].rearrange("p (t h) -> p t h", h=GHEADS)
        alpha = softbuf[:, GHEADS * TILES:].rearrange("p (t h) -> p t h", h=GHEADS)
        best_f, best_b, held = [
            rowspace[0:ROWS, i * 1024:(i + 1) * 1024].rearrange("r (q h p) -> r q h p", q=QUARTERS, h=GHEADS)
            for i in range(3)]
        carry_f = endbuf[:, 0:TILES + 1]
        carry_b = endbuf[:, 2 * TILES:3 * TILES + 1]

        psT = [ps(f"psT{i}", [P, 512]) for i in range(2)]
        psQ = [ps(f"psQ{i}", [P, 512]) for i in range(2)]
        psA = [ps(f"psA{i}", [P, 1024]) for i in range(2)]
        up_psum = [psA[k][:, 512:1024] for k in range(2)]
        psS = [psA[i][:, :].rearrange("p (k w n) -> p k w n", k=G, w=2) for i in range(2)]

        s_meta = sem("meta_landed")
        s_x = sem("x_landed")
        s_wts = sem("weights_landed")
        s_pool = sem("pool_made")
        s_tofloat = sem("tofloat")
        s_cols = sem("cols_in_psum")
        s_colsv = sem("cols_copied")
        s_out = sem("out_stored")

        class Count:

            def __init__(self, sem, base):
                self.sem, self.base = sem, base

        def counted(name, totals):
            handle = sem(name)
            return [Count(handle, sum(totals[:u])) for u in range(len(totals))]

        def shared(prefix, uses):
            spaces = [{} for _ in uses]
            for name in dict.fromkeys(n for use in uses for n in use):
                totals = [use.get(name, 0) for use in uses]
                width = max(len(t) if isinstance(t, list) else 0 for t in totals)
                if width:
                    per_slot = [counted(f"{prefix}_{name}{k}", [t[k] if t and k < len(t) else 0 for t in totals]) for k in range(width)]
                for u, space in enumerate(spaces):
                    if width:
                        space[name] = [slot[u] for slot in per_slot]
                if not width:
                    for space, count in zip(spaces, counted(f"{prefix}_{name}", totals)):
                        space[name] = count
            return [namedtuple("Use", space)(**space) for space in spaces]

        def turns(eng, step):
            for s in range(SLOTS):
                step(0, s)
            with eng.Fori(1, TURNS - 1) as i:
                for s in range(SLOTS):
                    step(i, s)
            for s in range(SLOTS):
                step(TURNS - 1, s)

        def staggered(*stages):
            for step in range(len(CHUNKS) + len(stages) - 1):
                for lag, stage in enumerate(stages):
                    if stage and 0 <= step - lag < len(CHUNKS):
                        stage(step - lag)

        def long_turns(eng, step):
            def turn(n):
                for j in range(LONG):
                    step(2 * n + j // SLOTS, j % SLOTS, n, j)
            turn(0)
            with eng.Fori(1, NG // LONG - 1) as n:
                turn(n)
            turn(NG // LONG - 1)

        def ahead(i, s, n):
            j, t = divmod(s + n, SLOTS)
            if isinstance(i, int) and i + j >= TURNS:
                return None
            return i + j, t

        def behind(i, s):
            if s > 0:
                return i, s - 1
            if isinstance(i, int) and i == 0:
                return None
            return i - 1, SLOTS - 1

        def reached(eng, count, n):
            if isinstance(n, int) and n <= 0:
                return
            eng.wait_ge(count.sem, count.base + n)

        s_chain = sem("dve_chain")
        s_xtable = sem("x_table_stored")
        s_first = sem("first_src_landed")
        s_first_capped = sem("first_src_capped")
        s_first_wide = sem("first_src_in_psum")
        s_first_bc = sem("first_src_on_all_partitions")
        s_total = sem("totals_in_psum")
        s_base = sem("base_ready")

        SP, DVE = mybir.EngineType.SP, mybir.EngineType.DVE

        def load_firsts(engine, g, first=first_dst):
            _, values = nc.values_load_multi_w_load_instructions(
                first[0:1, bass.ds(G * g, G)], engines=[engine], min_val=0, max_val=NPAD - P,
                skip_runtime_bounds_check_because="the program caps them at NPAD - P, and node numbers are not negative")
            return values

        def row(name):
            return a[name].rearrange("(o f) -> o f", o=1)

        def col(name):
            return a[name].rearrange("(f o) -> f o", o=1)

        weight_loads = [
            (W0[:, :], a["L0_gnn_W"]),
            (Wkvq[0][:, 0:D], a["L1_gnn_Wk"]), (Wkvq[0][:, D:2 * D], a["L1_gnn_Wv"]), (Wkvq[0][:, 2 * D:], a["L1_gnn_Wq"]),
            (Wkvq[1][:, 0:D], a["L3_gnn_Wk"]), (Wkvq[1][:, D:2 * D], a["L3_gnn_Wv"]), (Wkvq[1][:, 2 * D:], a["L3_gnn_Wq"]),
            (Wo[0][:, :], a["L1_gnn_Wo"]), (Wo[1][:, :], a["L3_gnn_Wo"]),
            (W1[:, :], a["L1_gnn_W1"]), (W2[:, :, :], a["L1_gnn_W2"].rearrange("(k p) f -> p k f", p=P)),
            (row_b0[:, :], row("L0_gnn_b")), (row_bo[0][:, :], row("L1_gnn_bo")), (row_bo[1][:, :], row("L3_gnn_bo")),
            (row_c2[:, :], row("L1_gnn_c2")),
            (bc_kvq[:, 0:D], row("L3_gnn_bk").to_broadcast([P, D])), (bc_kvq[:, D:2 * D], row("L3_gnn_bv").to_broadcast([P, D])),
            (bc_kvq[:, 2 * D:], row("L3_gnn_bq").to_broadcast([P, D])),
            (col_g1[:, :], col("L1_gnn_g1")), (col_b1[:, :], col("L1_gnn_b1")),
            (col_c1[:, :], a["L1_gnn_c1"].rearrange("(k p) -> p k", p=P)),
            (col_gat[:, :], a["L2_gnn_bias"].rearrange("l f -> f l")),
            (bc_g2[:, :], row("L1_gnn_g2").to_broadcast([P, D])), (bc_b2[:, :], row("L1_gnn_b2").to_broadcast([P, D])),
        ]
        for l in range(2):
            weight_loads += [
                (Wsd[l][:, 0:D], a["L2_gnn_Wl"][l]), (Wsd[l][:, D:], a["L2_gnn_Wr"][l]),
                (att[l][:, :], a["L2_gnn_att"][l:l + 1].rearrange("o h c -> o (h c)").to_broadcast([P, D])),
            ]


        def per_group(names):
            return {n: NG for n in names.split()}

        GATHERED = dict(slot_open=NG, idx_open=NG, idx_landed=[16 * TURNS] * SLOTS, rows_landed=[16 * G * TURNS] * SLOTS)
        SPREAD = dict(window_landed=[16 * G * TURNS] * SLOTS, **per_group("hotT_psum hotT_ready spread_ready"))
        SUMMED = dict(acc_written=TILES, **per_group("hot_ready sums_ready"))
        ATT = {**GATHERED, **SPREAD, **SUMMED, **per_group("squared spread_used raw_ready clip_ready score_ready msg_ready")}
        GAT = {**GATHERED, **SPREAD, **per_group("spread_used hot_ready leaky_ready weighted logit_ready"), "spilled": [16 * TURNS] * SLOTS}
        MIX = {**SUMMED, **per_group("squared last_hot_ready msg_ready"), "folded": 2, "rows_loaded": [16 * TURNS] * SLOTS}
        COUNT = per_group("hot_ready counted before_ready")
        SEND = {**SPREAD, **per_group("hot_ready low_ready low_used low_psum lowT_ready prior_psum slot_open "
                                      "prior_ready within_ready prior_used place_ready scaled"),
                "rows_sent": [16 * G * TURNS] * SLOTS, "sources_landed": [16 * TURNS] * SLOTS}
        SUM = {**SUMMED, **per_group("rel_ready squared last_hot_ready"), "folded": 2, "rows_loaded": [16 * NG // LONG] * LONG}
        a_count, a_send, a_sum, att0, gat0, mix0, gat1, mix1, att1 = shared("edge", [COUNT, SEND, SUM, ATT, GAT, MIX, GAT, MIX, ATT])
        a_att, a_gat, a_mix = [att0, att1], [gat0, gat1], [mix0, mix1]
        NCH = len(CHUNKS)

        def per_chunk(names):
            return {n: NCH for n in names.split()}

        LN = per_chunk("z_ready added stats_ready var_ready std_ready rstd_ready coef_ready norm_ready")
        n_ln = shared("ln", [LN] * 4)
        n_tr = shared("tr", [per_chunk("in_psum copied")] * 4)
        n_ff, = shared("ff", [{**{k: v for k, v in LN.items() if k != "added"}, **per_chunk("up_ready up_copied scaled xb_ready v_ready stats3_ready var3_ready "
                                                 "std3_ready rstd3_ready coef3_ready")}])
        STORED = [32 * len(CHUNKS[c::2]) for c in range(2)]
        n_tb = shared("tb", [dict(product_ready=NB, copied=[NB // 2] * 2, stored=STORED)] * 4)
        n_nm = shared("nm", [dict(den_ready=1, den_copied=1, rden_ready=1, **per_chunk("along spread_ready scaled"))] * 2)
        n_sm = shared("sm", [dict.fromkeys("rowwise scanned ends_up carried carries_down shifted exp_ready sums_scanned "
                                           "sum_ends_up sums_carried sums_down alpha_rows alpha_up alpha_ready".split(), 1)] * 2)
        n_pr = shared("pr", [dict.fromkeys("mean squared total std ready x_ready".split(), 1)] * 2)
        s_zeroed = sem("acc_zeroed")

        ctx.enter_context(nc.allow_non_contiguous_dma(reason="small loads at the start: tile ends, per-feature columns"))
        block = ctx.enter_context(nc.Block())

        TABLES = [
            (Wkvq[0], [(kv_table[0], 0, 2 * D), (q_table[0], 2 * D, 3 * D)]),
            (Wsd[0], [(xs_table[0], 0, D), (xd_table[0], D, 2 * D)]),
            (Wsd[1], [(xs_table[1], 0, D), (xd_table[1], D, 2 * D)]),
            (Wkvq[1], [(kv_table[1], 0, 2 * D), (q_table[1], 2 * D, 3 * D)]),
        ]
        def tables_in_dram(eng, t):
            for c in range(2):
                eng.wait_ge(n_tb[t].stored[c].sem, n_tb[t].stored[c].base + STORED[c])

        @block.sync
        def _(sp):
            for n, at in ((0, 1), (1, 0), (2, 2)):
                sp.dma_start(rows_i[:, n], a["dst"][at:at + EPAD].rearrange("(q r p) -> r q p", q=QUARTERS, r=ROWS)).then_inc(s_meta, 16)
            sp.dma_start(rows_i[:, 3], a["src"].rearrange("(q r p) -> r q p", q=QUARTERS, r=ROWS)).then_inc(s_meta, 16)
            sp.dma_start(rows_f[:, 4], a["edge_weight"].rearrange("(q r p) -> r q p", q=QUARTERS, r=ROWS)).then_inc(s_meta, 16)
            sp.dma_start(first_i[0:1, :], a["dst"][1:1 + P * (TILES - 1) + 1:P].rearrange("(o t) -> o t", o=1)).then_inc(s_meta, 16)
            for h in range(GHEADS):
                for j, at in enumerate((0, 1, P, P + 1)):
                    sp.dma_start(ends_i[h:h + 1, j, :],
                                 a["dst"][at:at + P * (TILES - 1) + 1:P].rearrange("(o t) -> o t", o=1)).then_inc(s_meta, 16)
            sp.dma_start(xN[:, 0:FULLB, :], a["x"][0:FULLB * P, :].rearrange("(b p) f -> p b f", p=P)).then_inc(s_x, 16)
            sp.wait_ge(s_pool, 1)
            sp.dma_start(xN[0:TAILR, FULLB, :], a["x"][FULLB * P:N, :]).then_inc(s_x, 16)
            for dst, src in weight_loads:
                sp.dma_start(dst, src).then_inc(s_wts, 16)

            def fetch_idx(ns, i, s):
                g = SLOTS * i + s
                reached(sp, ns.rows_landed[s], 16 * G * i)
                sp.sem_inc(ns.idx_open.sem, 1)
                sp.dma_start(idx[s][:, :], src_idx[:, bass.ds(G * g, G)]).then_inc(ns.idx_landed[s].sem, 16)

            def fetch_window(ns, table, i, s):
                g = SLOTS * i + s
                firsts = load_firsts(SP, g)
                reached(sp, ns.spread_ready, g - SLOTS + 1)
                for k in range(G):
                    sp.dma_start(window[s][:, k, :], table[bass.ds(firsts[k], P), :]).then_inc(ns.window_landed[s].sem, 16)

            def store_tables(t):
                for c, (b0, nb) in enumerate(CHUNKS):
                    for half in range(2):
                        reached(sp, n_tb[t].copied[half], (b0 + nb) // 2)
                    for table, lo, hi in TABLES[t][1]:
                        sp.dma_start(table[b0 * P:(b0 + nb) * P, :].rearrange("(b p) f -> p b f", p=P),
                                     table_rows[c % 2][:, 0:nb, lo:hi]).then_inc(n_tb[t].stored[c % 2].sem, 16)

            sp.wait_ge(s_x, 32)
            sp.dma_start(x_table.rearrange("(b p) f -> p b f", p=P), xN[:, :, :]).then_inc(s_xtable, 16)
            sp.wait_ge(s_xtable, 16)
            sp.wait_ge(s_colsv, 1)

            def fetch_sources(i, s):
                g = SLOTS * i + s
                reached(sp, a_send.prior_used, g - SLOTS + 1)
                sp.dma_start(sources[s], a["src"][bass.ds(g * (G * P), G * P)].rearrange("(o e) -> o e", o=1)
                             .to_broadcast([P, G * P])).then_inc(a_send.sources_landed[s].sem, 16)
                fetch_window(a_send, x_table, i, s)
            turns(sp, fetch_sources)
            for s in range(SLOTS):
                sp.wait_ge(a_send.rows_sent[s].sem, a_send.rows_sent[s].base + 16 * G * TURNS)
            sp.dma_start(first_src_f[0:1, :], sorted_msgs.rearrange("(t p) w -> t p w", p=P)[:, 0, D]
                         .rearrange("(o t) -> o t", o=1)).then_inc(s_first, 16)

            def fetch_messages(i, s, n, j):
                g = SLOTS * i + s
                reached(sp, a_sum.sums_ready, g - LONG + 1)
                sp.dma_start(message_rows[j].rearrange("p (k w) -> p k w", k=G),
                             sorted_msgs[bass.ds(g * (G * P), G * P), :].rearrange("(k p) w -> p k w", p=P)
                             ).then_inc(a_sum.rows_loaded[j].sem, 16)
            long_turns(sp, fetch_messages)

            def attention(n, t):
                ns = a_att[n]
                store_tables(t)
                for s in range(SLOTS):
                    fetch_idx(ns, 0, s)
                tables_in_dram(sp, t)

                def step(i, s):
                    if not (isinstance(i, int) and i == 0):
                        fetch_idx(ns, i, s)
                    fetch_window(ns, q_table[n], i, s)
                turns(sp, step)

            def gat(n, t):
                ns, mix = a_gat[n], a_mix[n]
                store_tables(t)
                for s in range(SLOTS):
                    fetch_idx(ns, 0, s)
                tables_in_dram(sp, t)

                def step(i, s):
                    if not (isinstance(i, int) and i == 0):
                        fetch_idx(ns, i, s)
                    fetch_window(ns, xd_table[n], i, s)
                    if s >= 2:
                        spill_rows(i, s - 2)
                    elif not (isinstance(i, int) and i == 0):
                        spill_rows(i - 1, s + 2)

                def spill_rows(i, s):
                    g = SLOTS * i + s
                    sp.wait_ge(ns.rows_landed[s].sem, ns.rows_landed[s].base + 16 * G * (i + 1))
                    sp.dma_start(edge_rows[n][bass.ds(g, 1)].rearrange("o p f -> (o p) f"),
                                 rows[s][:, 0:G * D]).then_inc(ns.spilled[s].sem, 16)
                turns(sp, step)
                spill_rows(TURNS - 1, 2)
                spill_rows(TURNS - 1, 3)
                for s in range(SLOTS):
                    sp.wait_ge(ns.spilled[s].sem, ns.spilled[s].base + 16 * TURNS)
                sp.wait_ge(ns.spread_used.sem, ns.spread_used.base + NG)

                def refetch(i, s):
                    g = SLOTS * i + s
                    reached(sp, mix.msg_ready, g - SLOTS + 1)
                    sp.dma_start(rows[s][:, 0:G * D],
                                 edge_rows[n][bass.ds(g, 1)].rearrange("o p f -> (o p) f")).then_inc(mix.rows_loaded[s].sem, 16)
                turns(sp, refetch)

            attention(0, 0)
            gat(0, 1)
            gat(1, 2)
            attention(1, 3)
            for c, (b0, nb) in enumerate(CHUNKS):
                sp.wait_ge(n_ln[3].norm_ready.sem, n_ln[3].norm_ready.base + c + 1)
                full = min(b0 + nb, FULLB) - b0
                if full > 0:
                    sp.dma_start(out[b0 * P:(b0 + full) * P, :].rearrange("(b p) f -> p b f", p=P),
                                 xN[:, b0:b0 + full, :]).then_inc(s_out, 16)
                if b0 <= FULLB < b0 + nb:
                    sp.dma_start(out[FULLB * P:N, :], xN[0:TAILR, FULLB, :]).then_inc(s_out, 16)
            sp.wait_ge(s_out, 16 * 7)

        @block.gpsimd
        def _(pool):
            nc.gpsimd.memset(xN[:, FULLB:NB, :], 0.0).then_inc(s_pool, 1)
            nc.gpsimd.memset(ident[:, :], 0.0)
            nc.gpsimd.memset(ones[:, :], 1.0)
            nc.gpsimd.memset(sel8[:, :], 0.0)
            nc.gpsimd.memset(earlier[:, :], 1.0)
            nc.gpsimd.memset(later[:, :], 1.0)
            nc.gpsimd.memset(rowbuf[:, :], 0.0)
            nc.gpsimd.memset(before[:, :, 0:1], 0.0)
            nc.gpsimd.iota(iota_i[:, :], pattern=[[1, P]], base=0, channel_multiplier=0)
            nc.gpsimd.memset(eps[:, :], LN_EPS).then_inc(s_pool, 1)
            pool.wait_ge(s_pool, 2)
            nc.gpsimd.tensor_copy(iota[:, :], iota_i[:, :])
            nc.gpsimd.affine_select(out=ident[:, :], in_=ident[:, :], compare_op=ALU.not_equal, fill=1.0,
                                    base=0, pattern=[[-1, P]], channel_multiplier=1)
            nc.gpsimd.affine_select(out=earlier[:, :], in_=earlier[:, :], compare_op=ALU.is_gt, fill=0.0,
                                    base=0, pattern=[[-1, P]], channel_multiplier=1)
            nc.gpsimd.affine_select(out=later[:, :], in_=later[:, :], compare_op=ALU.is_gt, fill=0.0,
                                    base=0, pattern=[[1, P]], channel_multiplier=-1)
            nc.gpsimd.affine_select(out=sel8[:, :], in_=sel8[:, :], compare_op=ALU.not_equal, fill=1.0,
                                    base=0, pattern=[[-DH, HEADS]], channel_multiplier=1).then_inc(s_pool, 1)

            def gather(ns, table, width, i, s):
                pool.wait_ge(ns.idx_landed[s].sem, ns.idx_landed[s].base + 16 * (i + 1))
                pool.sem_inc(ns.slot_open.sem, 1)
                for k in range(G):
                    pool.indirect_dma_start(
                        out=rows[s][:, k * width:(k + 1) * width], out_offset=None, in_=table,
                        in_offset=bass.IndirectOffsetOnAxis(ap=idx[s][:, k:k + 1], axis=0)).then_inc(ns.rows_landed[s].sem, 16)

            def send(i, s):
                ns, g = a_send, SLOTS * i + s
                pool.wait_ge(ns.place_ready.sem, ns.place_ready.base + g + 1)
                pool.wait_ge(ns.scaled.sem, ns.scaled.base + g + 1)
                pool.sem_inc(ns.slot_open.sem, 1)
                for k in range(G):
                    pool.indirect_dma_start(
                        out=sorted_msgs, out_offset=bass.IndirectOffsetOnAxis(ap=place[s][:, k:k + 1], axis=0),
                        in_=rows[s][:, k * SENT:(k + 1) * SENT], in_offset=None).then_inc(ns.rows_sent[s].sem, 16)
            turns(pool, send)
            nc.gpsimd.memset(parts[:, 0:2, :], 0.0).then_inc(s_zeroed, 1)
            for s in range(SLOTS):
                pool.wait_ge(a_send.rows_sent[s].sem, a_send.rows_sent[s].base + 16 * G * TURNS)
            pool.wait_ge(s_first_bc, 1)

            def relative(i, s, n, j):
                ns, g = a_sum, SLOTS * i + s
                reached(pool, ns.squared, g - SLOTS + 1)
                reached(pool, ns.last_hot_ready, g - SLOTS + 1)
                pool.wait_ge(ns.rows_loaded[j].sem, ns.rows_loaded[j].base + 16 * (n + 1))
                nc.gpsimd.tensor_tensor(msg_rel[s][:, :], message_rows[j].rearrange("p (k w) -> p k w", k=G)[:, :, D],
                                        first_src_bc[:, bass.ds(G * g, G)], ALU.subtract).then_inc(ns.rel_ready.sem, 1)
            long_turns(pool, relative)

            def fold(ns):
                pool.wait_ge(ns.acc_written.sem, ns.acc_written.base + TILES)
                nc.gpsimd.tensor_tensor(parts[:, 1, :], parts[:, 1, :], parts[:, 3, :], ALU.add).then_inc(ns.folded.sem, 1)
            fold(a_sum)

            def attention(n, t):
                ns = a_att[n]
                tables_in_dram(pool, t)

                def step(i, s):
                    reached(pool, ns.msg_ready, SLOTS * i + s - SLOTS + 1)
                    gather(ns, kv_table[n][:, :], 2 * D, i, s)
                turns(pool, step)

            def gat(n, t):
                ns, mix = a_gat[n], a_mix[n]
                tables_in_dram(pool, t)

                def step(i, s):
                    reached(pool, ns.spread_used, SLOTS * i + s - SLOTS + 1)
                    reached(pool, ns.spilled[s], 16 * i)
                    gather(ns, xs_table[n][:, :], D, i, s)
                turns(pool, step)
                pool.wait_ge(n_sm[n].alpha_ready.sem, n_sm[n].alpha_ready.base + 1)

                def weigh(i, s):
                    g, par = SLOTS * i + s, s % 2
                    reached(pool, mix.sums_ready, g - 1)
                    pool.wait_ge(mix.rows_loaded[s].sem, mix.rows_loaded[s].base + 16 * (i + 1))
                    nc.gpsimd.tensor_tensor(
                        msg[par][:, :, :].rearrange("p k (h c) -> p (k h) c", c=GC),
                        rows[s][:, 0:G * D].rearrange("p (x c) -> p x c", c=GC),
                        alpha[:, bass.ds(G * g, G), :].rearrange("p k h -> p (k h)").unsqueeze(2).to_broadcast([P, G * GHEADS, GC]),
                        ALU.mult).then_inc(mix.msg_ready.sem, 1)
                long_turns(pool, lambda i, s, n, j: weigh(i, s))
                fold(mix)

            def zero_acc(s, n):
                pool.wait_ge(s.sem, s.base + n)
                nc.gpsimd.memset(acc[:, :, :], 0.0).then_inc(s_zeroed, 1)

            zero_acc(n_ln[0].z_ready, len(CHUNKS))
            attention(0, 0)
            pool.wait_ge(s_wts, 16 * len(weight_loads))
            for c, (b0, nb) in enumerate(CHUNKS):
                if c == 0:
                    pool.wait_ge(n_ln[1].added.sem, n_ln[1].added.base + len(CHUNKS))
                nc.gpsimd.tensor_tensor(xN[:, b0:b0 + nb, :], xN[:, b0:b0 + nb, :],
                                        bc_b2[:, :].unsqueeze(1).to_broadcast([P, nb, D]), ALU.add).then_inc(n_ff.xb_ready.sem, 1)
            gat(0, 1)
            gat(1, 2)
            zero_acc(n_pr[1].x_ready, 1)
            attention(1, 3)

        @block.scalar
        def _(act):
            def squares(ns, rel, tiles, i, s):
                reached(act, ns.sums_ready, SLOTS * i + s - SLOTS + 1)
                if ns is a_sum:
                    act.wait_ge(ns.rel_ready.sem, ns.rel_ready.base + SLOTS * i + s + 1)
                for k in range(tiles):
                    last = nc.scalar.activation(hot[s][:, k, :], iota[:, :], ACT.Square, bias=rel(i, s, k), scale=-1.0)
                last.then_inc(ns.squared.sem, 1)

            def hot_from_squares(ns, tiles, i, s):
                act.wait_ge(ns.squared.sem, ns.squared.base + SLOTS * i + s + 1)
                flat = hot[s][:, 0:tiles, :].rearrange("p k n -> p (k n)")
                nc.scalar.activation(flat, flat, ACT.Relu, bias=ones[:, 0:1], scale=-1.0).then_inc(ns.hot_ready.sem, 1)

            def hots(ns, rel):
                def step(i, s):
                    if ahead(i, s, 1):
                        squares(ns, rel, G - 1, *ahead(i, s, 1))
                    hot_from_squares(ns, G - 1, i, s)
                squares(ns, rel, G - 1, 0, 0)
                long_turns(act, lambda i, s, n, j: step(i, s))

            def zero_parts(first):
                nc.scalar.activation(nodebuf[:, first * NPAD:], ones[:, 0:1].to_broadcast([P, (G - first) * NPAD]), ACT.Copy,
                                     scale=0.0).then_inc(s_zeroed, 1)

            def src_rel(i, s, k):
                return msg_rel[s][:, k:k + 1]

            def dst_rel_of(i, s, k):
                return dst_rel[:, bass.ds(G * (SLOTS * i + s) + k, 1)]

            def copy_hotT(ns, i, s):
                g, par = SLOTS * i + s, s % 2
                act.wait_ge(ns.hotT_psum.sem, ns.hotT_psum.base + g + 1)
                reached(act, ns.spread_ready, g - 1)
                nc.scalar.copy(hotT[par][:, :, :].rearrange("p k n -> p (k n)"), psT[par][:, :]).then_inc(ns.hotT_ready.sem, 1)

            def next_hotT(ns, i, s):
                if s < SLOTS - 1:
                    copy_hotT(ns, i, s + 1)
                elif not (isinstance(i, int) and i == TURNS - 1):
                    copy_hotT(ns, i + 1, 0)

            def attention(n):
                ns = a_att[n]

                def step(i, s):
                    g, par = SLOTS * i + s, s % 2
                    next_hotT(ns, i, s)
                    act.wait_ge(ns.clip_ready.sem, ns.clip_ready.base + g + 1)
                    reached(act, ns.sums_ready, g - 1)
                    nc.scalar.activation(score[par][:, :, :].rearrange("p k (h c) -> p (k h) c", c=DH),
                                         clipped[par][:, :, :].rearrange("p k h -> p (k h)").unsqueeze(2)
                                         .to_broadcast([P, G * HEADS, DH]), ACT.Exp,
                                         scale=float(DH) ** -0.5).then_inc(ns.score_ready.sem, 1)
                    if ahead(i, s, 2):
                        squares(ns, dst_rel_of, G, *ahead(i, s, 2))
                        hot_from_squares(ns, G, *ahead(i, s, 2))
                for s in (0, 1):
                    squares(ns, dst_rel_of, G, 0, s)
                    hot_from_squares(ns, G, 0, s)
                copy_hotT(ns, 0, 0)
                turns(act, step)

            def gat(n):
                ns = a_gat[n]

                def step(i, s):
                    next_hotT(ns, i, s)
                copy_hotT(ns, 0, 0)
                turns(act, step)
                mix, sm = a_mix[n], n_sm[n]
                act.wait_ge(ns.logit_ready.sem, ns.logit_ready.base + NG)
                zero_parts(0)
                act.wait_ge(sm.shifted.sem, sm.shifted.base + 1)
                nc.scalar.activation(best_f[:, :, :, :], best_f[:, :, :, :], ACT.Exp).then_inc(sm.exp_ready.sem, 1)
                hots(mix, dst_rel_of)

            def root(dst, var, ready, done, n):
                act.wait_ge(ready.sem, ready.base + n)
                nc.scalar.activation(dst, var, ACT.Sqrt, bias=eps[:, :]).then_inc(done.sem, 1)

            def normalise(ns, dest):
                def stage(c):
                    b0, nb = CHUNKS[c]
                    root(std[c % 4][:, 0:nb], mv[c % 4][:, 0:nb, 1], ns.var_ready, ns.std_ready, c + 1)
                    act.wait_ge(ns.coef_ready.sem, ns.coef_ready.base + c + 1)
                    for j in range(nb):
                        last = nc.scalar.activation(dest[:, b0 + j, :], dest[:, b0 + j, :], ACT.Identity,
                                                    bias=shift[c % 4][:, j:j + 1], scale=rstd[c % 4][:, j:j + 1])
                    last.then_inc(ns.norm_ready.sem, 1)
                return stage

            def spread_rden(n):
                ns = n_nm[n]
                act.wait_ge(ns.rden_ready.sem, ns.rden_ready.base + 1)
                for c, (b0, nb) in enumerate(CHUNKS):
                    nc.scalar.copy(nA[:, b0:b0 + nb, :].rearrange("p b (h c) -> p (b h) c", h=HEADS),
                                   rden[:, b0 * HEADS:(b0 + nb) * HEADS].unsqueeze(2)
                                   .to_broadcast([P, nb * HEADS, DH])).then_inc(ns.along.sem, 1)

            def tables(t):
                ns, width = n_tb[t], 3 * D if TABLES[t][0] in Wkvq else 2 * D

                def stage(c):
                    b0, nb = CHUNKS[c]
                    reached(act, ns.stored[c % 2], 32 * (c // 2))
                    for j in range(0, nb, 2):
                        b = b0 + j
                        act.wait_ge(ns.product_ready.sem, ns.product_ready.base + b + 1)
                        nc.scalar.copy(table_rows[c % 2][:, j, 0:width], psQ[b % 2][:, 0:width]).then_inc(ns.copied[0].sem, 1)
                return stage

            def count(i, s):
                g = SLOTS * i + s
                act.wait_ge(a_count.counted.sem, a_count.counted.base + g + 1)
                nc.scalar.copy(before[:, :, bass.ds(G * g + 1, G)].rearrange("p h k -> p k h"),
                               psQ[s % 2][:, 0:G * HI].rearrange("p (k h) -> p k h", k=G)).then_inc(a_count.before_ready.sem, 1)

            def send(i, s):
                ns, g, par = a_send, SLOTS * i + s, s % 2
                nxt = ahead(i, s, 1)
                if nxt:
                    transposed_hots(*nxt)
                act.wait_ge(ns.spread_ready.sem, ns.spread_ready.base + g + 1)
                reached(act, ns.rows_sent[s], 16 * G * i)
                row = rows[s][:, 0:G * SENT].rearrange("p (k w) -> p k w", k=G)
                for k in range(G):
                    nc.scalar.activation(row[:, k, 0:D], psQ[par][:, k * D:(k + 1) * D], ACT.Copy,
                                         scale=weight[:, bass.ds(G * g + k, 1)])
                nc.scalar.copy(row[:, :, D], src_f[:, bass.ds(G * g, G)]).then_inc(ns.scaled.sem, 1)

            def transposed_hots(i, s):
                ns, g, par = a_send, SLOTS * i + s, s % 2
                act.wait_ge(ns.hotT_psum.sem, ns.hotT_psum.base + g + 1)
                reached(act, ns.spread_ready, g - 1)
                nc.scalar.copy(hotT[par][:, :, :].rearrange("p k n -> p (k n)"), psT[0][:, :]).then_inc(ns.hotT_ready.sem, 1)
                act.wait_ge(ns.low_psum.sem, ns.low_psum.base + g + 1)
                reached(act, ns.prior_psum, g - 1)
                nc.scalar.copy(low_hotT[par][:, :, :].rearrange("p k n -> p (k n)"), psT[1][:, :]).then_inc(ns.lowT_ready.sem, 1)

            act.wait_ge(s_pool, 3)
            turns(act, count)
            act.wait_ge(s_colsv, 2)
            transposed_hots(0, 0)
            turns(act, send)
            act.wait_ge(a_send.place_ready.sem, a_send.place_ready.base + NG)
            zero_parts(2)
            hots(a_sum, src_rel)
            staggered(normalise(n_ln[0], xN))
            staggered(tables(0))
            attention(0)
            spread_rden(0)
            act.wait_ge(s_wts, 16 * len(weight_loads))

            def affine_transposed(c):
                b0, nb = CHUNKS[c]
                act.wait_ge(n_tr[1].in_psum.sem, n_tr[1].in_psum.base + c + 1)
                nc.scalar.activation(xT[:, b0 * P:(b0 + nb) * P], psT[c % 2][:, 0:nb * P], ACT.Identity,
                                     bias=col_b1[:, :], scale=col_g1[:, :]).then_inc(n_tr[1].copied.sem, 1)

            def relu_up(c):
                nb = CHUNKS[c][1]
                act.wait_ge(n_ff.up_ready.sem, n_ff.up_ready.base + c + 1)
                reached(act, n_ff.z_ready, c - 1)
                for k in range(2):
                    last = nc.scalar.activation(ffT[c % 2][:, k, 0:nb * P], up_psum[k][:, 0:nb * P], ACT.Relu,
                                                bias=col_c1[:, k:k + 1])
                last.then_inc(n_ff.up_copied.sem, 1)

            def transformer_norms(c):
                b0, nb = CHUNKS[c]
                root(std[c % 4][:, 0:nb], mv[c % 4][:, 0:nb, 1], n_ff.var_ready, n_ff.std_ready, c + 1)
                root(std[c % 4][:, 0:nb], mv[c % 4][:, 0:nb, 1], n_ff.var3_ready, n_ff.std3_ready, c + 1)
                act.wait_ge(n_ff.coef3_ready.sem, n_ff.coef3_ready.base + c + 1)
                for j in range(nb):
                    last = nc.scalar.activation(xN[:, b0 + j, :], nA[:, b0 + j, :], ACT.Identity,
                                                bias=shift[c % 4][:, j:j + 1], scale=rstd[c % 4][:, j:j + 1])
                last.then_inc(n_ff.norm_ready.sem, 1)
            staggered(normalise(n_ln[1], nA), None, None, affine_transposed)
            staggered(relu_up, transformer_norms)
            staggered(tables(1))

            def pairnorm(n):
                pr = n_pr[n]
                act.wait_ge(pr.mean.sem, pr.mean.base + 1)
                nc.scalar.activation(acc[:, 1, 0:N], acc[:, 0, 0:N], ACT.Square, bias=pair[:, 1:2],
                                     accum_out=pair[:, 2:3]).then_inc(pr.squared.sem, 1)
                act.wait_ge(pr.total.sem, pr.total.base + 1)
                nc.scalar.activation(pair[:, 3:4], psT[1][:, 0:1], ACT.Sqrt, bias=eps[:, :], scale=1.0 / N).then_inc(pr.std.sem, 1)
                act.wait_ge(pr.ready.sem, pr.ready.base + 1)
                nc.scalar.activation(xT[:, 0:N], acc[:, 0, 0:N], ACT.Relu, bias=pair[:, 5:6],
                                     scale=pair[:, 4:5]).then_inc(pr.x_ready.sem, 1)

            gat(0)
            pairnorm(0)
            staggered(tables(2))
            gat(1)
            pairnorm(1)
            staggered(normalise(n_ln[2], xN))
            attention(1)
            spread_rden(1)
            staggered(normalise(n_ln[3], xN))

        @block.vector
        def _(dve):
            chain = [0]

            def link(ins):
                chain[0] += 1
                ins.then_inc(s_chain, 1)
                dve.wait_ge(s_chain, chain[0])

            V = nc.vector
            dve.wait_ge(s_meta, 16 * 14)
            V.tensor_copy(rows_f[:, 0:4], rows_i[:, 0:4])
            V.tensor_scalar(first_dst[:, :], first_i[:, :], float(NPAD - P), None, ALU.min)
            link(V.tensor_copy(ends_f[:, :, :], ends_i[:, :, :]))
            link(V.tensor_copy(first_f[:, :], first_dst[:, :]))
            link(V.tensor_tensor(copies[:, :, :], rows_f[:, 0], rows_f[:, 2], ALU.not_equal))
            V.tensor_scalar(copies[:, :, :], copies[:, :, :], 1.0, None, ALU.add).then_inc(s_tofloat, 1)
            dve.wait_ge(s_cols, 1)
            V.tensor_copy(src_f[:, :], psT[0][:, 0:TILES])
            link(V.tensor_copy(src_idx[:, :], psT[0][:, 0:TILES]))
            for part, op, by in ((src_high, ALU.arith_shift_right, 7), (src_low, ALU.bitwise_and, P - 1)):
                link(V.tensor_scalar(part_i, src_idx[:, :], by, None, op))
                link(V.tensor_copy(part, part_i))
            V.tensor_copy(first_f[:, :], first_dst[:, :]).then_inc(s_colsv, 1)
            V.tensor_copy(weight[:, :], psQ[0][:, 0:TILES])
            link(V.tensor_copy(dst_rel[:, :], psT[1][:, 0:TILES]))
            V.tensor_tensor(dst_rel[:, :], dst_rel[:, :], psA[0][:, 0:TILES], ALU.subtract).then_inc(s_colsv, 1)
            dve.wait_ge(s_colsv, 2)

            def masks():
                for q_scan, q_open, nb, edge, first in ((scan_fwd, open_fwd, 1, 0, 0), (scan_bwd, open_bwd, 2, P - 1, P - 1)):
                    link(V.tensor_tensor(q_open[:, :, :], rows_f[:, 0], rows_f[:, nb], ALU.not_equal))
                    for h in range(GHEADS):
                        link(V.tensor_scalar(q_scan[:, :, h, :], q_open[:, :, :], -BIG, None, ALU.mult))
                    link(V.memset(q_scan[:, :, :, edge:edge + 1], -BIG))
                    link(V.tensor_tensor(q_open[:, :, :], rows_f[:, 0],
                                         rows_f[:, nb, :, edge:edge + 1].to_broadcast([ROWS, QUARTERS, P]), ALU.not_equal))
                    link(V.tensor_scalar(q_open[:, :, :], q_open[:, :, :], -BIG, None, ALU.mult))
                link(V.tensor_tensor(pass_fwd[:, :], ends_f[:, 2, :], ends_f[:, 0, :], ALU.not_equal))
                link(V.tensor_scalar(pass_fwd[:, :], pass_fwd[:, :], -BIG, None, ALU.mult))
                link(V.tensor_tensor(pass_bwd[:, :], ends_f[:, 1, :], ends_f[:, 3, :], ALU.not_equal))
                link(V.tensor_scalar(pass_bwd[:, :], pass_bwd[:, :], -BIG, None, ALU.mult))
                link(V.tensor_scalar(whole_fwd, pass_fwd[:, :], 0.0, None, ALU.is_ge))
                link(V.tensor_scalar(whole_bwd, pass_bwd[:, :], 0.0, None, ALU.is_ge))

            def make_hot(ns, i, s):
                g = SLOTS * i + s
                V.tensor_tensor(hot[s][:, :, :], iota[:, :].unsqueeze(1).to_broadcast([P, G, P]),
                                dst_rel[:, bass.ds(G * g, G)].unsqueeze(2).to_broadcast([P, G, P]),
                                ALU.is_equal).then_inc(ns.hot_ready.sem, 1)

            def add_sums(ns, i, s):
                g, par = SLOTS * i + s, s % 2
                firsts = load_firsts(DVE, g, first_src if ns is a_sum else first_dst)
                dve.wait_ge(ns.sums_ready.sem, ns.sums_ready.base + g + 1)
                reached(dve, ns.acc_written, G * g)
                for k in range(G):
                    d = parts[:, k, bass.ds(firsts[k], P)]
                    V.tensor_tensor(d, d, psS[par][:, k, 0], ALU.add).then_inc(ns.acc_written.sem, 1)

            def add_tile(ns, i, s, k, firsts):
                reached(dve, ns.acc_written, G * (SLOTS * i + s) + k)
                d = acc[:, :, bass.ds(firsts[k], P)]
                V.tensor_tensor(d, d, psS[s % 2][:, k], ALU.add).then_inc(ns.acc_written.sem, 1)

            def last_hot(ns, rel, i, s):
                if ns is a_sum:
                    dve.wait_ge(ns.rel_ready.sem, ns.rel_ready.base + SLOTS * i + s + 1)
                V.tensor_scalar(hot[s][:, G - 1, :], iota[:, :], rel(i, s), None, ALU.is_equal).then_inc(ns.last_hot_ready.sem, 1)

            def sum_tiles(ns, rel):
                def step(i, s):
                    if ahead(i, s, 1):
                        last_hot(ns, rel, *ahead(i, s, 1))
                    add_sums(ns, i, s)
                last_hot(ns, rel, 0, 0)
                long_turns(dve, lambda i, s, n, j: step(i, s))
                fold(ns)

            def fold(ns):
                dve.wait_ge(ns.acc_written.sem, ns.acc_written.base + TILES)
                V.tensor_tensor(parts[:, 0, :], parts[:, 0, :], parts[:, 2, :], ALU.add).then_inc(ns.folded.sem, 1)
                dve.wait_ge(ns.folded.sem, ns.folded.base + 2)

            def hot_high(dst, g):
                return V.tensor_tensor(dst[:, :, :], iota[:, 0:HI].unsqueeze(1).to_broadcast([P, G, HI]),
                                       src_high[:, bass.ds(G * g, G)].unsqueeze(2).to_broadcast([P, G, HI]), ALU.is_equal)

            def hot_low(dst, g):
                return V.tensor_tensor(dst[:, :, :], iota[:, :].unsqueeze(1).to_broadcast([P, G, P]),
                                       src_low[:, bass.ds(G * g, G)].unsqueeze(2).to_broadcast([P, G, P]), ALU.is_equal)

            def count(i, s):
                g = SLOTS * i + s
                reached(dve, a_count.counted, g - SLOTS + 1)
                hot_high(high_b[s], g)
                hot_low(hot_b[s], g).then_inc(a_count.hot_ready.sem, 1)

            def run_up():
                dve.wait_ge(a_count.before_ready.sem, a_count.before_ready.base + NG)
                link(V.memset(high_sum[:, 0:1], 0.0))
                for h in range(HI):
                    c = before[:, h, 1:TILES + 1]
                    last = V.tensor_tensor_scan(c, ones[:, 0:1].to_broadcast([P, TILES]), c, 0.0, ALU.mult, ALU.add)
                last.then_inc(s_total, 1)
                dve.wait_ge(s_base, 1)
                link(V.tensor_tensor_scan(high_sum[:, 1:HI + 1], ones[:, 0:HI], psQ[1][:, 0:HI], 0.0, ALU.mult, ALU.add))
                V.tensor_tensor(base[:, :], psQ[0][:, 0:HI], high_sum[:, 0:HI], ALU.add).then_inc(s_base, 1)

            def send_hots(i, s):
                ns, g, par = a_send, SLOTS * i + s, s % 2
                reached(dve, ns.spread_ready, g - SLOTS + 1)
                make_hot(ns, i, s)
                reached(dve, ns.low_psum, g - 1)
                hot_low(low_hot[par], g)
                hot_high(high_hot[s], g).then_inc(ns.low_ready.sem, 1)

            def send(i, s):
                ns, g, par = a_send, SLOTS * i + s, s % 2
                dve.wait_ge(ns.sources_landed[s].sem, ns.sources_landed[s].base + 16 * (i + 1))
                for k in range(G):
                    V.scalar_tensor_tensor(matched[par][:, k, :], sources[s][:, k * P:(k + 1) * P], src_f[:, bass.ds(G * g + k, 1)],
                                           earlier[:, :], ALU.is_equal, ALU.mult, accum_out=within[par][:, k:k + 1])
                dve.wait_ge(ns.prior_psum.sem, ns.prior_psum.base + g + 1)
                V.tensor_tensor(prior_h[par][:, :, :], psA[par][:, 512:512 + G * HI].rearrange("p (k h) -> p k h", k=G),
                                high_hot[s][:, :, :], ALU.mult).then_inc(ns.prior_used.sem, 1)
                dve.wait_ge(ns.prior_used.sem, ns.prior_used.base + g + 1)
                V.tensor_reduce(prior[par][:, :], prior_h[par][:, :, :], AX.X, ALU.add).then_inc(ns.prior_ready.sem, 1)
                if ahead(i, s, 2):
                    send_hots(*ahead(i, s, 2))
                dve.wait_ge(ns.prior_ready.sem, ns.prior_ready.base + g + 1)
                reached(dve, ns.rows_sent[s], 16 * G * i)
                V.tensor_tensor(place[s][:, :], prior[par][:, :], within[par][:, :], ALU.add).then_inc(ns.place_ready.sem, 1)

            def sum_pass():
                ns = a_sum

                dve.wait_ge(s_first, 16)
                link(V.tensor_scalar(first_src_f[:, :], first_src_f[:, :], float(NPAD - P), None, ALU.min))
                V.tensor_copy(first_src[:, :], first_src_f[:, :]).then_inc(s_first_capped, 1)
                dve.wait_ge(s_first_wide, 1)
                V.tensor_copy(first_src_bc, psT[0][:, 0:TILES]).then_inc(s_first_bc, 1)
                dve.wait_ge(s_first_capped, 1)
                sum_tiles(ns, lambda i, s: msg_rel[s][:, G - 1:G])

            def attention(n):
                ns = a_att[n]

                def step(i, s):
                    g, par = SLOTS * i + s, s % 2
                    kv = rows[s][:, :].rearrange("p (k w) -> p k w", k=G)
                    dve.wait_ge(ns.spread_ready.sem, ns.spread_ready.base + g + 1)
                    dve.wait_ge(ns.rows_landed[s].sem, ns.rows_landed[s].base + 16 * G * (i + 1))
                    V.tensor_tensor(prod[par][:, :, :], kv[:, :, 0:D],
                                    psQ[par][:, :].rearrange("p (k f) -> p k f", k=G), ALU.mult).then_inc(ns.spread_used.sem, 1)
                    before_last = behind(*behind(i, s)) if behind(i, s) else None
                    firsts = before_last and load_firsts(DVE, g - 2)
                    if before_last:
                        reached(dve, ns.sums_ready, g - 1)

                    def add(k):
                        if before_last:
                            add_tile(ns, *before_last, k, firsts)
                    add(0)
                    dve.wait_ge(ns.spread_used.sem, ns.spread_used.base + g + 1)
                    V.tensor_reduce(raw[par][:, :, :].rearrange("p k h -> p (k h)"),
                                    prod[par][:, :, :].rearrange("p k (h c) -> p (k h) c", c=DH),
                                    AX.X, ALU.add).then_inc(ns.raw_ready.sem, 1)
                    add(1)
                    dve.wait_ge(ns.raw_ready.sem, ns.raw_ready.base + g + 1)
                    lim = 5.0 * float(DH) ** 0.5
                    V.tensor_scalar(clipped[par][:, :, :], raw[par][:, :, :], lim, -lim, ALU.min, ALU.max).then_inc(ns.clip_ready.sem, 1)
                    add(2)
                    add(3)
                    dve.wait_ge(ns.score_ready.sem, ns.score_ready.base + g + 1)
                    V.tensor_tensor(msg[par][:, :, :], kv[:, :, D:2 * D], score[par][:, :, :], ALU.mult).then_inc(ns.msg_ready.sem, 1)
                turns(dve, step)
                for s in (SLOTS - 2, SLOTS - 1):
                    firsts = load_firsts(DVE, SLOTS * (TURNS - 1) + s)
                    dve.wait_ge(ns.sums_ready.sem, ns.sums_ready.base + SLOTS * (TURNS - 1) + s + 1)
                    for k in range(G):
                        add_tile(ns, TURNS - 1, s, k, firsts)

            def gat(n, zeroed):
                ns, mix, sm = a_gat[n], a_mix[n], n_sm[n]

                def weigh(i, s):
                    g, par = SLOTS * i + s, s % 2
                    dve.wait_ge(ns.spread_used.sem, ns.spread_used.base + g + 1)
                    V.scalar_tensor_tensor(leaky[par][:, :, :], prod[par][:, :, :], 0.2, prod[par][:, :, :],
                                           ALU.mult, ALU.max).then_inc(ns.leaky_ready.sem, 1)
                    dve.wait_ge(ns.leaky_ready.sem, ns.leaky_ready.base + g + 1)
                    V.tensor_tensor(msg[par][:, :, :], leaky[par][:, :, :],
                                    att[n][:, :].unsqueeze(1).to_broadcast([P, G, D]), ALU.mult).then_inc(ns.weighted.sem, 1)
                    dve.wait_ge(ns.weighted.sem, ns.weighted.base + g + 1)
                    V.tensor_reduce(logits[:, bass.ds(G * g, G), :].rearrange("p k h -> p (k h)"),
                                    msg[par][:, :, :].rearrange("p k (h c) -> p (k h) c", c=GC),
                                    AX.X, ALU.add).then_inc(ns.logit_ready.sem, 1)

                def step(i, s):
                    g, par = SLOTS * i + s, s % 2
                    dve.wait_ge(ns.spread_ready.sem, ns.spread_ready.base + g + 1)
                    dve.wait_ge(ns.rows_landed[s].sem, ns.rows_landed[s].base + 16 * G * (i + 1))
                    V.tensor_tensor(prod[par][:, :, :].rearrange("p k f -> p (k f)"), rows[s][:, 0:G * D],
                                    psQ[par][:, :], ALU.add).then_inc(ns.spread_used.sem, 1)
                    if ahead(i, s, 2):
                        reached(dve, ns.hotT_psum, g - 1)
                        make_hot(ns, *ahead(i, s, 2))
                    if behind(i, s):
                        weigh(*behind(i, s))
                make_hot(ns, 0, 0)
                make_hot(ns, 0, 1)
                turns(dve, step)
                weigh(TURNS - 1, SLOTS - 1)

                flat = "r q h p -> r (q h p)"
                dve.wait_ge(sm.rowwise.sem, sm.rowwise.base + 1)
                rowlog = psA[0][0:ROWS, :]
                V.tensor_tensor_scan(best_f[:, :, :, :].rearrange(flat), scan_fwd[:, :, :, :].rearrange(flat), rowlog,
                                     -BIG, ALU.add, ALU.max)
                V.tensor_tensor_scan(best_b[:, :, :, :].rearrange(flat)[:, ::-1], scan_bwd[:, :, :, :].rearrange(flat)[:, ::-1],
                                     rowlog[:, ::-1], -BIG, ALU.add, ALU.max).then_inc(sm.scanned.sem, 1)
                V.memset(carry_f[:, 0:1], -BIG)
                V.memset(carry_b[:, TILES:TILES + 1], -BIG)
                dve.wait_ge(sm.ends_up.sem, sm.ends_up.base + 1)
                V.tensor_tensor_scan(carry_f[:, 1:TILES + 1], pass_fwd[:, :], psT[0][0:2, 0:TILES], -BIG, ALU.add, ALU.max)
                V.tensor_tensor_scan(carry_b[:, 0:TILES][:, ::-1], pass_bwd[:, ::-1], psT[1][0:2, 0:TILES][:, ::-1],
                                     -BIG, ALU.add, ALU.max).then_inc(sm.carried.sem, 1)
                dve.wait_ge(sm.carries_down.sem, sm.carries_down.base + 1)
                entering = [psc[0:ROWS, 0:QUARTERS * GHEADS].rearrange("r (q h) -> r q h", q=QUARTERS).unsqueeze(3)
                            .to_broadcast([ROWS, QUARTERS, GHEADS, P]) for psc in (psQ[0], psQ[1])]
                per_head = [o[:, :, :].unsqueeze(2).to_broadcast([ROWS, QUARTERS, GHEADS, P]) for o in (open_fwd, open_bwd)]
                whole4 = (slice(None),) * 4
                for best, opened, entry in ((best_f, per_head[0], entering[0]), (best_b, per_head[1], entering[1])):
                    link(V.tensor_tensor(held[whole4], opened, entry, ALU.add))
                    link(V.tensor_tensor(best[whole4], best[whole4], held[whole4], ALU.max))
                link(V.tensor_tensor(best_f[whole4], best_f[whole4], best_b[whole4], ALU.max))
                V.tensor_tensor(best_f[:, :, :, :].rearrange(flat), rowlog, best_f[:, :, :, :].rearrange(flat),
                                ALU.subtract).then_inc(sm.shifted.sem, 1)

                V.tensor_scalar(held[whole4], scan_fwd[whole4], 0.0, None, ALU.is_ge)
                V.tensor_scalar(best_b[whole4], scan_bwd[whole4], 0.0, None, ALU.is_ge)
                V.memset(carry_f[:, 0:1], 0.0)
                V.memset(carry_b[:, TILES:TILES + 1], 0.0)
                dve.wait_ge(sm.exp_ready.sem, sm.exp_ready.base + 1)
                rowexp = psA[1][0:ROWS, :]
                link(V.tensor_tensor(rowexp.rearrange("r (q h p) -> r q h p", q=QUARTERS, h=GHEADS), best_f[whole4],
                                     copies[:, :, :].unsqueeze(2).to_broadcast([ROWS, QUARTERS, GHEADS, P]), ALU.mult))
                V.tensor_tensor_scan(best_f[:, :, :, :].rearrange(flat), held[:, :, :, :].rearrange(flat), rowexp,
                                     0.0, ALU.mult, ALU.add)
                V.tensor_tensor_scan(best_b[:, :, :, :].rearrange(flat)[:, ::-1], best_b[:, :, :, :].rearrange(flat)[:, ::-1],
                                     rowexp[:, ::-1], 0.0, ALU.mult, ALU.add).then_inc(sm.sums_scanned.sem, 1)
                dve.wait_ge(sm.sum_ends_up.sem, sm.sum_ends_up.base + 1)
                V.tensor_tensor_scan(carry_f[:, 1:TILES + 1], whole_fwd, psT[0][0:2, 0:TILES], 0.0, ALU.mult, ALU.add)
                V.tensor_tensor_scan(carry_b[:, 0:TILES][:, ::-1], whole_bwd[:, ::-1], psT[1][0:2, 0:TILES][:, ::-1],
                                     0.0, ALU.mult, ALU.add).then_inc(sm.sums_carried.sem, 1)
                link(V.tensor_tensor(best_f[whole4], best_f[whole4], best_b[whole4], ALU.add))
                link(V.tensor_tensor(best_f[:, :, :, :].rearrange(flat), best_f[:, :, :, :].rearrange(flat), rowexp, ALU.subtract))
                dve.wait_ge(sm.sums_down.sem, sm.sums_down.base + 1)
                for opened, entry in zip(per_head, entering):
                    for q in range(QUARTERS):
                        last = V.scalar_tensor_tensor(held[:, q], opened[:, q], 0.0, entry[:, q], ALU.is_ge, ALU.mult)
                    link(last)
                    link(V.tensor_tensor(best_f[whole4], best_f[whole4], held[whole4], ALU.add))
                link(V.tensor_scalar(best_f[whole4], best_f[whole4], 1e-16, None, ALU.add))
                link(V.reciprocal(best_f[whole4], best_f[whole4]))
                V.tensor_tensor(best_f[:, :, :, :].rearrange(flat), best_f[:, :, :, :].rearrange(flat), rowexp,
                                ALU.mult).then_inc(sm.alpha_rows.sem, 1)
                dve.wait_ge(sm.alpha_up.sem, sm.alpha_up.base + 1)
                for h in range(GHEADS):
                    last = V.tensor_copy(alpha[:, :, h], psT[h][:, 0:TILES])
                last.then_inc(sm.alpha_ready.sem, 1)

                dve.wait_ge(s_zeroed, zeroed)
                sum_tiles(mix, lambda i, s: dst_rel[:, bass.ds(G * (SLOTS * i + s) + G - 1, 1)])

            def block_stats(ready, n, z, st, m, nb, s1, s2):
                dve.wait_ge(ready.sem, ready.base + n)
                for j in range(nb):
                    last = V.bn_stats(st[:, j, :], z[:, j, :])
                last.then_inc(s1.sem, 1)
                dve.wait_ge(s1.sem, s1.base + n)
                for j in range(nb):
                    last = V.bn_aggr(m[:, j, :], st[:, j, :])
                last.then_inc(s2.sem, 1)

            def coefficients(std_ready, s1, s2, n, c, nb):
                dve.wait_ge(std_ready.sem, std_ready.base + n)
                V.reciprocal(rstd[c % 4][:, 0:nb], std[c % 4][:, 0:nb]).then_inc(s1.sem, 1)
                dve.wait_ge(s1.sem, s1.base + n)
                V.scalar_tensor_tensor(shift[c % 4][:, 0:nb], mv[c % 4][:, 0:nb, 0], -1.0, rstd[c % 4][:, 0:nb],
                                       ALU.mult, ALU.mult).then_inc(s2.sem, 1)

            def zchunk(c):
                return psA[c % 2][:, 0:512].rearrange("p (b f) -> p b f", f=D)

            def layernorm(ns, z):
                def statistics(c):
                    b0, nb = CHUNKS[c]
                    reached(dve, ns.norm_ready, c - 3)
                    dve.wait_ge(ns.z_ready.sem, ns.z_ready.base + c + 1)
                    V.tensor_tensor(z[:, b0:b0 + nb, :], zchunk(c)[:, 0:nb, :], xN[:, b0:b0 + nb, :], ALU.add).then_inc(ns.added.sem, 1)
                    block_stats(ns.added, c + 1, z[:, b0:b0 + nb, :], stats[c % 4], mv[c % 4], nb, ns.stats_ready, ns.var_ready)

                def stage(c):
                    if c == 0:
                        statistics(0)
                    if c + 1 < len(CHUNKS):
                        statistics(c + 1)
                    coefficients(ns.std_ready, ns.rstd_ready, ns.coef_ready, c + 1, c, CHUNKS[c][1])
                return stage

            def copy_transposed(ns):
                def stage(c):
                    b0, nb = CHUNKS[c]
                    dve.wait_ge(ns.in_psum.sem, ns.in_psum.base + c + 1)
                    V.tensor_copy(xT[:, b0 * P:(b0 + nb) * P], psT[c % 2][:, 0:nb * P]).then_inc(ns.copied.sem, 1)
                return stage

            def tables(t):
                ns, width = n_tb[t], 3 * D if TABLES[t][0] in Wkvq else 2 * D
                for c, (b0, nb) in enumerate(CHUNKS):
                    reached(dve, ns.stored[c % 2], 32 * (c // 2))
                    for j in range(1, nb, 2):
                        b = b0 + j
                        dve.wait_ge(ns.product_ready.sem, ns.product_ready.base + b + 1)
                        V.tensor_copy(table_rows[c % 2][:, j, 0:width], psQ[b % 2][:, 0:width]).then_inc(ns.copied[1].sem, 1)

            def biased_tables(t):
                ns = n_tb[t]
                for c, (b0, nb) in enumerate(CHUNKS):
                    reached(dve, ns.stored[c % 2], 32 * (c // 2))
                    for j in range(nb):
                        b = b0 + j
                        dve.wait_ge(ns.product_ready.sem, ns.product_ready.base + b + 1)
                        V.tensor_tensor(table_rows[c % 2][:, j, :], psQ[b % 2][:, 0:3 * D], bc_kvq[:, :],
                                        ALU.add).then_inc(ns.copied[b % 2].sem, 1)

            def divide_by_sums(n):
                ns = n_nm[n]
                dve.wait_ge(ns.den_ready.sem, ns.den_ready.base + 1)
                V.tensor_scalar(den[:, :], psT[0][:, 0:NB * HEADS], 1e-30, None, ALU.max).then_inc(ns.den_copied.sem, 1)
                dve.wait_ge(ns.den_copied.sem, ns.den_copied.base + 1)
                V.reciprocal(rden[:, :], den[:, :]).then_inc(ns.rden_ready.sem, 1)

                def stage(c):
                    b0, nb = CHUNKS[c]
                    dve.wait_ge(ns.spread_ready.sem, ns.spread_ready.base + c + 1)
                    d = acc[:, 0, b0 * P:(b0 + nb) * P]
                    V.tensor_tensor(d, d, psQ[c % 2][:, 0:nb * P], ALU.mult).then_inc(ns.scaled.sem, 1)
                return stage

            def pairnorm(n):
                pr = n_pr[n]
                link(V.scalar_tensor_tensor(acc[:, 0, 0:N], acc[:, 0, 0:N], col_gat[:, n:n + 1], acc[:, 1, 0:N],
                                            ALU.add, ALU.add, accum_out=pair[:, 0:1]))
                V.tensor_scalar(pair[:, 1:2], pair[:, 0:1], -1.0 / N, None, ALU.mult).then_inc(pr.mean.sem, 1)
                dve.wait_ge(pr.std.sem, pr.std.base + 1)
                link(V.reciprocal(pair[:, 4:5], pair[:, 3:4]))
                V.tensor_tensor(pair[:, 5:6], pair[:, 1:2], pair[:, 4:5], ALU.mult).then_inc(pr.ready.sem, 1)

            dve.wait_ge(s_pool, 3)
            turns(dve, count)
            run_up()
            send_hots(0, 0)
            send_hots(0, 1)
            turns(dve, send)
            masks()
            dve.wait_ge(s_zeroed, 2)
            sum_pass()
            dve.wait_ge(s_x, 32)
            staggered(layernorm(n_ln[0], xN), None, None, copy_transposed(n_tr[0]))
            tables(0)
            dve.wait_ge(s_zeroed, 3)
            attention(0)
            staggered(divide_by_sums(0), None, layernorm(n_ln[1], nA))
            dve.wait_ge(s_wts, 16 * len(weight_loads))
            dve.wait_ge(n_ln[1].norm_ready.sem, n_ln[1].norm_ready.base + len(CHUNKS))

            def transformer_norms(c):
                b0, nb = CHUNKS[c]
                m, st, z = mv[c % 4], stats[c % 4], zchunk(c)
                if c >= 2:
                    reached(dve, n_ff.norm_ready, c - 1)
                block_stats(n_ff.z_ready, c + 1, z, st, m, nb, n_ff.stats_ready, n_ff.var_ready)
                dve.wait_ge(n_ff.std_ready.sem, n_ff.std_ready.base + c + 1)
                V.reciprocal(rstd[c % 4][:, 0:nb], std[c % 4][:, 0:nb]).then_inc(n_ff.rstd_ready.sem, 1)
                for j in range(nb):
                    last = V.scalar_tensor_tensor(nA[:, b0 + j, :], z[:, j, :], m[:, j, 0:1], bc_g2[:, :],
                                                  ALU.subtract, ALU.mult)
                last.then_inc(n_ff.scaled.sem, 1)
                dve.wait_ge(n_ff.rstd_ready.sem, n_ff.rstd_ready.base + c + 1)
                dve.wait_ge(n_ff.scaled.sem, n_ff.scaled.base + c + 1)
                dve.wait_ge(n_ff.xb_ready.sem, n_ff.xb_ready.base + c + 1)
                for j in range(nb):
                    last = V.scalar_tensor_tensor(nA[:, b0 + j, :], nA[:, b0 + j, :], rstd[c % 4][:, j:j + 1],
                                                  xN[:, b0 + j, :], ALU.mult, ALU.add)
                last.then_inc(n_ff.v_ready.sem, 1)
                block_stats(n_ff.v_ready, c + 1, nA[:, b0:b0 + nb, :], st, m, nb, n_ff.stats3_ready, n_ff.var3_ready)
                coefficients(n_ff.std3_ready, n_ff.rstd3_ready, n_ff.coef3_ready, c + 1, c, nb)
            staggered(transformer_norms, None, copy_transposed(n_tr[2]))
            tables(1)
            gat(0, 4)
            pairnorm(0)
            tables(2)
            gat(1, 5)
            pairnorm(1)
            staggered(layernorm(n_ln[2], xN), None, None, copy_transposed(n_tr[3]))
            biased_tables(3)
            dve.wait_ge(s_zeroed, 6)
            attention(1)
            staggered(divide_by_sums(1), None, layernorm(n_ln[3], xN))

        @block.tensor
        def _(pe):
            mm, tr = nc.tensor.matmul, nc.tensor.transpose
            pe.wait_ge(s_pool, 3)
            pe.wait_ge(s_tofloat, 1)
            for ps_, src in ((psT[0], rows_f[:, 3]), (psT[1], rows_f[:, 0]), (psQ[0], rows_f[:, 4])):
                for q in range(QUARTERS):
                    tr(ps_[:, q * ROWS:(q + 1) * ROWS], src[:, q, :], ident[0:ROWS, 0:ROWS])
            mm(psA[0][:, 0:TILES], ones[0:1, :], first_f[0:1, :], start=True, stop=True).then_inc(s_cols, 1)

            def transpose_hot(ns, i, s):
                g, par = SLOTS * i + s, s % 2
                pe.wait_ge(ns.hot_ready.sem, ns.hot_ready.base + g + 1)
                reached(pe, ns.hotT_ready, g - 1)
                for k in range(G):
                    last = tr(psT[par][:, k * P:(k + 1) * P], hot[s][:, k, :], ident[:, :])
                last.then_inc(ns.hotT_psum.sem, 1)

            def spread(ns, i, s):
                g, par = SLOTS * i + s, s % 2
                pe.wait_ge(ns.window_landed[s].sem, ns.window_landed[s].base + 16 * G * (i + 1))
                reached(pe, ns.spread_used, g - 1)
                pe.wait_ge(ns.hotT_ready.sem, ns.hotT_ready.base + g + 1)
                for k in range(G):
                    last = mm(psQ[par][:, k * D:(k + 1) * D], hotT[par][:, k, :], window[s][:, k, :], start=True, stop=True)
                last.then_inc(ns.spread_ready.sem, 1)

            def next_spread(ns, i, s):
                if s < SLOTS - 1:
                    nxt = (i, s + 1)
                elif isinstance(i, int) and i == TURNS - 1:
                    return
                else:
                    nxt = (i + 1, 0)
                transpose_hot(ns, *nxt)
                spread(ns, *nxt)

            def scatter(ns, i, s, messages, weights):
                g, par = SLOTS * i + s, s % 2
                reached(pe, ns.acc_written, G * (g - 1))
                for k in range(G):
                    last = mm(psS[par][:, k, 0, :], messages(s, k), hot[s][:, k, :], start=True, stop=True)
                    if weights:
                        last = mm(psS[par][:, k, 1, :], weights(par, k), hot[s][:, k, :], start=True, stop=True)
                last.then_inc(ns.sums_ready.sem, 1)

            def count(i, s):
                g = SLOTS * i + s
                pe.wait_ge(a_count.hot_ready.sem, a_count.hot_ready.base + g + 1)
                reached(pe, a_count.before_ready, g - 1)
                for k in range(G):
                    last = mm(psQ[s % 2][:, k * HI:(k + 1) * HI], hot_b[s][:, k, :], high_b[s][:, k, :], start=True, stop=True)
                last.then_inc(a_count.counted.sem, 1)

            def send_transposes(i, s):
                ns, g, par = a_send, SLOTS * i + s, s % 2
                pe.wait_ge(ns.hot_ready.sem, ns.hot_ready.base + g + 1)
                reached(pe, ns.hotT_ready, g)
                for k in range(G):
                    last = tr(psT[0][:, k * P:(k + 1) * P], hot[s][:, k, :], ident[:, :])
                last.then_inc(ns.hotT_psum.sem, 1)
                pe.wait_ge(ns.low_ready.sem, ns.low_ready.base + g + 1)
                reached(pe, ns.lowT_ready, g)
                for k in range(G):
                    last = tr(psT[1][:, k * P:(k + 1) * P], low_hot[par][:, k, :], ident[:, :])
                last.then_inc(ns.low_psum.sem, 1)
                pe.wait_ge(ns.window_landed[s].sem, ns.window_landed[s].base + 16 * G * (i + 1))
                reached(pe, ns.scaled, g - 1)
                pe.wait_ge(ns.hotT_ready.sem, ns.hotT_ready.base + g + 1)
                for k in range(G):
                    last = mm(psQ[par][:, k * D:(k + 1) * D], hotT[par][:, k, :], window[s][:, k, :], start=True, stop=True)
                last.then_inc(ns.spread_ready.sem, 1)
                pe.wait_ge(ns.lowT_ready.sem, ns.lowT_ready.base + g + 1)
                reached(pe, ns.prior_used, g - 1)
                for k in range(G):
                    at = psA[par][:, 512 + k * HI:512 + (k + 1) * HI]
                    mm(at, low_hotT[par][:, k, :], base[:, :], start=True, stop=False)
                    last = mm(at, low_hotT[par][:, k, :], before[:, :, bass.ds(G * g + k, 1)].rearrange("p h o -> p (h o)"),
                              start=False, stop=True)
                last.then_inc(ns.prior_psum.sem, 1)

            def sum_pass():
                ns = a_sum
                pe.wait_ge(s_first_capped, 1)
                mm(psT[0][:, 0:TILES], ones[0:1, :], first_src_f[0:1, :], start=True, stop=True).then_inc(s_first_wide, 1)

                def step(i, s, n, j):
                    pe.wait_ge(ns.hot_ready.sem, ns.hot_ready.base + SLOTS * i + s + 1)
                    pe.wait_ge(ns.last_hot_ready.sem, ns.last_hot_ready.base + SLOTS * i + s + 1)
                    pe.wait_ge(ns.rows_loaded[j].sem, ns.rows_loaded[j].base + 16 * (n + 1))
                    scatter(ns, i, s, lambda s, k: message_rows[j][:, k * SENT:k * SENT + D], None)
                long_turns(pe, step)

            def attention(n):
                ns = a_att[n]

                def step(i, s):
                    next_spread(ns, i, s)
                    pe.wait_ge(ns.msg_ready.sem, ns.msg_ready.base + SLOTS * i + s + 1)
                    scatter(ns, i, s, lambda s, k: msg[s % 2][:, k, :],
                            lambda par, k: score[par][:, k, :])
                transpose_hot(ns, 0, 0)
                spread(ns, 0, 0)
                turns(pe, step)

            def ends_up(done):
                for q in range(QUARTERS):
                    tr(psT[0][0:GHEADS, q * ROWS:(q + 1) * ROWS], best_f[:, q, :, P - 1], ident[0:ROWS, 0:ROWS])
                    last = tr(psT[1][0:GHEADS, q * ROWS:(q + 1) * ROWS], best_b[:, q, :, 0], ident[0:ROWS, 0:ROWS])
                last.then_inc(done.sem, 1)

            def carries_down(done):
                for q in range(QUARTERS):
                    at = q * ROWS
                    tr(psQ[0][0:ROWS, q * GHEADS:(q + 1) * GHEADS], carry_f[:, at:at + ROWS], ident[0:2, 0:2])
                    last = tr(psQ[1][0:ROWS, q * GHEADS:(q + 1) * GHEADS], carry_b[:, at + 1:at + 1 + ROWS], ident[0:2, 0:2])
                last.then_inc(done.sem, 1)

            def gat(n):
                ns, mix, sm = a_gat[n], a_mix[n], n_sm[n]
                transpose_hot(ns, 0, 0)
                spread(ns, 0, 0)
                turns(pe, lambda i, s: next_spread(ns, i, s))

                pe.wait_ge(ns.logit_ready.sem, ns.logit_ready.base + NG)
                for q in range(QUARTERS):
                    for h in range(GHEADS):
                        at = (q * GHEADS + h) * P
                        last = tr(psA[0][0:ROWS, at:at + P], logits[:, q * ROWS:(q + 1) * ROWS, h], ident[:, :])
                last.then_inc(sm.rowwise.sem, 1)
                pe.wait_ge(sm.scanned.sem, sm.scanned.base + 1)
                ends_up(sm.ends_up)
                pe.wait_ge(sm.carried.sem, sm.carried.base + 1)
                carries_down(sm.carries_down)
                pe.wait_ge(sm.sums_scanned.sem, sm.sums_scanned.base + 1)
                ends_up(sm.sum_ends_up)
                pe.wait_ge(sm.sums_carried.sem, sm.sums_carried.base + 1)
                carries_down(sm.sums_down)
                pe.wait_ge(sm.alpha_rows.sem, sm.alpha_rows.base + 1)
                for q in range(QUARTERS):
                    for h in range(GHEADS):
                        last = tr(psT[h][:, q * ROWS:(q + 1) * ROWS], best_f[:, q, h, :], ident[0:ROWS, 0:ROWS])
                last.then_inc(sm.alpha_up.sem, 1)
                pe.wait_ge(sm.alpha_ready.sem, sm.alpha_ready.base + 1)

                def mix_step(i, s):
                    g = SLOTS * i + s
                    pe.wait_ge(mix.hot_ready.sem, mix.hot_ready.base + g + 1)
                    pe.wait_ge(mix.last_hot_ready.sem, mix.last_hot_ready.base + g + 1)
                    pe.wait_ge(mix.msg_ready.sem, mix.msg_ready.base + g + 1)
                    scatter(mix, i, s, lambda s, k: msg[s % 2][:, k, :], None)
                long_turns(pe, lambda i, s, n, j: mix_step(i, s))

            def add_row(dst, row):
                return mm(dst, ones[0:1, :], row, start=False, stop=True)

            def zchunk(c):
                return psA[c % 2][:, 0:512].rearrange("p (b f) -> p b f", f=D)

            def residual(ns, product, ready=None):
                def stage(c):
                    b0, nb = CHUNKS[c]
                    if ready:
                        pe.wait_ge(ready.sem, ready.base + c + 1)
                    if c >= 2:
                        reached(pe, ns.added, c - 1)
                    for j in range(nb):
                        last = product(zchunk(c)[:, j, :], b0 + j)
                    last.then_inc(ns.z_ready.sem, 1)
                return stage

            def transposed(ns, ready, src):
                def stage(c):
                    b0, nb = CHUNKS[c]
                    pe.wait_ge(ready.sem, ready.base + c + 1)
                    if c >= 2:
                        reached(pe, ns.copied, c - 1)
                    for j in range(nb):
                        last = tr(psT[c % 2][:, j * P:(j + 1) * P], src[:, b0 + j, :], ident[:, :])
                    last.then_inc(ns.in_psum.sem, 1)
                return stage

            def tables(t, ready):
                ns, (w, _) = n_tb[t], TABLES[t]
                width = 3 * D if w in Wkvq else 2 * D

                def stage(c):
                    b0, nb = CHUNKS[c]
                    ready(c)
                    for b in range(b0, b0 + nb):
                        reached(pe, ns.copied[b % 2], b // 2)
                        last = mm(psQ[b % 2][:, 0:width], xT[:, b * P:(b + 1) * P], w[:, 0:width], start=True, stop=True)
                        last.then_inc(ns.product_ready.sem, 1)
                return stage

            def divide_by_sums(n):
                ns = n_nm[n]
                pe.wait_ge(a_att[n].acc_written.sem, a_att[n].acc_written.base + TILES)
                for b in range(NB):
                    last = mm(psT[0][:, b * HEADS:(b + 1) * HEADS], acc[:, 1, b * P:(b + 1) * P], sel8[:, :], start=True, stop=True)
                last.then_inc(ns.den_ready.sem, 1)

                def stage(c):
                    b0, nb = CHUNKS[c]
                    pe.wait_ge(ns.along.sem, ns.along.base + c + 1)
                    if c >= 2:
                        reached(pe, ns.scaled, c - 1)
                    for j in range(nb):
                        last = mm(psQ[c % 2][:, j * P:(j + 1) * P], nA[:, b0 + j, :], ident[:, :], start=True, stop=True)
                    last.then_inc(ns.spread_ready.sem, 1)
                return stage

            def project(w, bias, halves=1):
                def product(z, b):
                    for h in range(halves):
                        mm(z, acc[:, h, b * P:(b + 1) * P], w[:, :], start=h == 0, stop=False)
                    return add_row(z, bias[0:1, :])
                return product

            def pair_total(n):
                pe.wait_ge(n_pr[n].squared.sem, n_pr[n].squared.base + 1)
                mm(psT[1][:, 0:1], ones[:, :], pair[:, 2:3], start=True, stop=True).then_inc(n_pr[n].total.sem, 1)

            def by_copied(ns):
                return lambda c: reached(pe, ns.copied, c + 1)

            pe.wait_ge(s_colsv, 2)
            turns(pe, count)
            pe.wait_ge(s_total, 1)
            total = before[:, :, TILES]
            mm(psQ[0][:, 0:HI], later[:, :], total, start=True, stop=True)
            mm(psQ[1][:, 0:HI], ones[:, :], total, start=True, stop=True).then_inc(s_base, 1)
            pe.wait_ge(s_base, 2)
            turns(pe, send_transposes)
            sum_pass()
            pe.wait_ge(s_wts, 16 * len(weight_loads))
            pe.wait_ge(s_x, 32)
            pe.wait_ge(a_sum.folded.sem, a_sum.folded.base + 2)
            staggered(residual(n_ln[0], project(W0, row_b0, halves=2)), None, None, transposed(n_tr[0], n_ln[0].norm_ready, xN))
            staggered(tables(0, by_copied(n_tr[0])))
            attention(0)
            staggered(divide_by_sums(0), residual(n_ln[1], project(Wo[0], row_bo[0]), n_nm[0].scaled), None, None, transposed(n_tr[1], n_ln[1].norm_ready, nA))

            def feed_up(c):
                b0, nb = CHUNKS[c]
                pe.wait_ge(n_ln[1].norm_ready.sem, n_ln[1].norm_ready.base + len(CHUNKS))
                pe.wait_ge(n_tr[1].copied.sem, n_tr[1].copied.base + c + 1)
                reached(pe, n_ff.up_copied, c)
                for k in range(2):
                    last = mm(up_psum[k][:, 0:nb * P], W1[:, k * D:(k + 1) * D], xT[:, b0 * P:(b0 + nb) * P], start=True, stop=True)
                last.then_inc(n_ff.up_ready.sem, 1)

            def feed_down(c):
                b0, nb = CHUNKS[c]
                pe.wait_ge(n_ff.up_copied.sem, n_ff.up_copied.base + c + 1)
                reached(pe, n_ff.scaled, c - 1)
                for j in range(nb):
                    z = zchunk(c)[:, j, :]
                    mm(z, xT[:, (b0 + j) * P:(b0 + j + 1) * P], ident[:, :], start=True, stop=False)
                    for k in range(2):
                        mm(z, ffT[c % 2][:, k, j * P:(j + 1) * P], W2[:, k, :], start=False, stop=False)
                    last = add_row(z, row_c2[0:1, :])
                last.then_inc(n_ff.z_ready.sem, 1)
            staggered(feed_up, feed_down, None, transposed(n_tr[2], n_ff.norm_ready, xN))
            staggered(tables(1, by_copied(n_tr[2])))
            gat(0)
            pair_total(0)
            staggered(tables(2, lambda c: reached(pe, n_pr[0].x_ready, 1)))
            gat(1)
            pair_total(1)
            pe.wait_ge(n_pr[1].x_ready.sem, n_pr[1].x_ready.base + 1)
            own_x = lambda z, b: mm(z, xT[:, b * P:(b + 1) * P], ident[:, :], start=True, stop=True)
            staggered(residual(n_ln[2], own_x), None, None, transposed(n_tr[3], n_ln[2].norm_ready, xN))
            staggered(tables(3, by_copied(n_tr[3])))
            attention(1)
            staggered(divide_by_sums(1), residual(n_ln[3], project(Wo[1], row_bo[1]), n_nm[1].scaled))


ARGS = ["x", "src", "dst", "edge_weight", "L0_gnn_W", "L0_gnn_b", "L1_gnn_Wq", "L1_gnn_Wk", "L1_gnn_Wv", "L1_gnn_Wo",
        "L1_gnn_bo", "L1_gnn_g1", "L1_gnn_b1", "L1_gnn_g2", "L1_gnn_b2", "L1_gnn_W1", "L1_gnn_c1", "L1_gnn_W2",
        "L1_gnn_c2", "L2_gnn_Wl", "L2_gnn_Wr", "L2_gnn_att", "L2_gnn_bias", "L3_gnn_Wq", "L3_gnn_bq", "L3_gnn_Wk",
        "L3_gnn_bk", "L3_gnn_Wv", "L3_gnn_bv", "L3_gnn_Wo", "L3_gnn_bo"]
TRANSPOSED = ["L3_gnn_Wq", "L3_gnn_Wk", "L3_gnn_Wv", "L3_gnn_Wo"]


def kernel(**inputs):
    import numpy as _np
    import concourse.bacc as _bacc
    from concourse import mybir as _mybir
    from concourse.bass_utils import run_bass_kernel_spmd as _run

    nc = _bacc.Bacc("TRN2", target_bir_lowering=False, num_devices=1)
    arrays, args = {}, {}
    for name in ARGS:
        v = _np.asarray(inputs[name])
        if name in TRANSPOSED:
            v = v.T
        if name == "src":
            v = _np.concatenate([v, _np.full(EPAD - E, HI * P - 1, v.dtype)])
        if name == "edge_weight":
            v = _np.concatenate([v, _np.zeros(EPAD - E, v.dtype)])
        if name == "dst":
            v = _np.concatenate([_np.full(1, -1, v.dtype), v, _np.full(EPAD - E, FAR, v.dtype), _np.full(1, -2, v.dtype)])
        v = _np.ascontiguousarray(v)
        arrays[f"in_{name}"] = v
        args[name] = nc.dram_tensor(f"in_{name}", v.shape, _mybir.dt.from_np(v.dtype), kind="ExternalInput").ap()
    out = nc.dram_tensor("out_0", (N, D), _mybir.dt.float32, kind="ExternalOutput").ap()
    gnn_program(nc, args, out)
    r = _run(nc, [arrays], core_ids=[0])
    return r.results[0]["out_0"]
```
